# Optimizing a Trainium2 kernel written in Bass

```python
import numpy as np
import jax
import jax.numpy as jnp

def _softmax(x, axis=-1):
    return jax.nn.softmax(x, axis=axis)

def _gelu(x):
    return jax.nn.gelu(x, approximate=True)

def _silu(x):
    return jax.nn.silu(x)

def _sigmoid(x):
    return jax.nn.sigmoid(x)

def _layernorm(x, axis=-1, eps=1e-05):
    m = jnp.mean(x, axis=axis, keepdims=True)
    v = jnp.var(x, axis=axis, keepdims=True)
    return (x - m) / jnp.sqrt(v + eps)

def _scatter_add(tgt, idx, src, axis=0):
    return tgt.at[idx].add(src)

def _segment_sum(src, seg, n):
    return jax.ops.segment_sum(src, seg, n)
kernel_name = 'mk_vit_tower_d1_tok_img768_r4_cad461'

def setup_inputs(seed: int=0):
    np.random.seed(seed)
    _w = jnp.asarray

    def _rec_inputs():
        import jax
        import jax.numpy as jnp
        _rk = jax.random.key(seed)
        x = -0.00016672 + 0.999947 * jax.random.normal(jax.random.fold_in(_rk, 1), (64, 3, 96, 96), jnp.float32)
        return x
    x = _rec_inputs()

    def _L0_tok_setup():
        import jax, jax.numpy as jnp
        import numpy as np
        B, C, H, W = (64, 3, 96, 96)
        P = 16
        NH, NW = (H // P, W // P)
        N = NH * NW
        PATCH_DIM = C * P * P
        DIM = 192

        def _layernorm(x, g, b, eps=1e-05):
            mu = jnp.mean(x, axis=-1, keepdims=True)
            var = jnp.var(x, axis=-1, keepdims=True)
            return (x - mu) * jax.lax.rsqrt(var + eps) * g + b
        key = jax.random.key(seed)
        ks = jax.random.split(key, 8)
        img = jax.random.normal(ks[0], (B, C, H, W), dtype=jnp.float32)
        ln1_g = jnp.ones((PATCH_DIM,), jnp.float32)
        ln1_b = jnp.zeros((PATCH_DIM,), jnp.float32)
        W_lin = jax.random.normal(ks[1], (PATCH_DIM, DIM), jnp.float32) / np.sqrt(PATCH_DIM)
        b_lin = jnp.zeros((DIM,), jnp.float32)
        ln2_g = jnp.ones((DIM,), jnp.float32)
        ln2_b = jnp.zeros((DIM,), jnp.float32)
        pos_embedding = jax.random.normal(ks[2], (1, N + 1, DIM), jnp.float32)
        cls_token = jax.random.normal(ks[3], (1, 1, DIM), jnp.float32)
        return {'img': img, 'ln1_g': ln1_g, 'ln1_b': ln1_b, 'W_lin': W_lin, 'b_lin': b_lin, 'ln2_g': ln2_g, 'ln2_b': ln2_b, 'pos_embedding': pos_embedding, 'cls_token': cls_token}
    _L0_tok_all = _L0_tok_setup()
    _L0_tok_in = {k: v for k, v in _L0_tok_all.items() if k in ('ln1_g', 'ln1_b', 'W_lin', 'b_lin', 'ln2_g', 'ln2_b', 'pos_embedding', 'cls_token')}
    del _L0_tok_all

    def _L0_attn_setup():
        import jax, jax.numpy as jnp
        import numpy as np
        B, T, D = (2, 512, 192)
        H, K, V = (8, 64, 96)
        F = 32

        def positional_features(positions, feature_size, seq_length):
            nb = feature_size // 2
            pow_rate = np.exp(np.log(seq_length + 1) / nb).astype(np.float32)
            center_widths = pow_rate ** jnp.arange(1, nb + 1, dtype=jnp.float32) - 1.0
            emb = (center_widths[None, :] > jnp.abs(positions)[:, None]).astype(jnp.float32)
            return jnp.concatenate([emb, jnp.sign(positions)[:, None] * emb], axis=-1)

        def relative_shift(x):
            b, h, t1, t2 = x.shape
            x = jnp.pad(x, ((0, 0), (0, 0), (0, 0), (1, 0)))
            x = x.reshape(b, h, t2 + 1, t1)[:, :, 1:, :].reshape(b, h, t1, t2)
            return x[..., :(t2 + 1) // 2]
        key = jax.random.key(seed)
        ks = jax.random.split(key, 9)
        w = lambda k, shape: jax.random.normal(k, shape, jnp.float32) * 0.02
        return {'x': jax.random.normal(ks[0], (B, T, D), jnp.float32), 'Wq': w(ks[1], (D, H * K)), 'Wk': w(ks[2], (D, H * K)), 'Wv': w(ks[3], (D, H * V)), 'Wrk': w(ks[4], (F, H * K)), 'r_w_bias': w(ks[5], (H, K)), 'r_r_bias': w(ks[6], (H, K)), 'Wo': w(ks[7], (H * V, D)), 'bo': jnp.zeros((D,), jnp.float32)}
    _L0_attn_all = _L0_attn_setup()
    _L0_attn_in = {k: v for k, v in _L0_attn_all.items() if k in ('Wq', 'Wk', 'Wv', 'Wrk', 'r_w_bias', 'r_r_bias', 'Wo', 'bo')}
    del _L0_attn_all

    def _L0_ffn_setup():
        import jax, jax.numpy as jnp
        import numpy as np
        DIM = 192
        NUM_EXPERTS = 8
        TOP_K = 2
        MLP_RATIO = 4
        CAPACITY_RATIO = 1.25
        key = jax.random.key(seed)
        ks = jax.random.split(key, 6)
        B, N, C = (16, 256, DIM)
        H = MLP_RATIO * C
        s_in = 1.0 / np.sqrt(C)
        s_h = 1.0 / np.sqrt(H)
        return {'x': jax.random.normal(ks[0], (B, N, C), dtype=jnp.float32), 'Wg': jax.random.normal(ks[1], (C, NUM_EXPERTS), dtype=jnp.float32) * s_in, 'W1': jax.random.normal(ks[2], (NUM_EXPERTS, C, H), dtype=jnp.float32) * s_in, 'b1': jnp.zeros((NUM_EXPERTS, H), dtype=jnp.float32), 'W2': jax.random.normal(ks[3], (NUM_EXPERTS, H, C), dtype=jnp.float32) * s_h, 'b2': jnp.zeros((NUM_EXPERTS, C), dtype=jnp.float32)}
    _L0_ffn_all = _L0_ffn_setup()
    _L0_ffn_in = {k: v for k, v in _L0_ffn_all.items() if k in ('Wg', 'W1', 'b1', 'W2', 'b2')}
    del _L0_ffn_all
    return {'x': x, 'L0_tok_ln1_g': _L0_tok_in['ln1_g'], 'L0_tok_ln1_b': _L0_tok_in['ln1_b'], 'L0_tok_W_lin': _L0_tok_in['W_lin'], 'L0_tok_b_lin': _L0_tok_in['b_lin'], 'L0_tok_ln2_g': _L0_tok_in['ln2_g'], 'L0_tok_ln2_b': _L0_tok_in['ln2_b'], 'L0_tok_pos_embedding': _L0_tok_in['pos_embedding'], 'L0_tok_cls_token': _L0_tok_in['cls_token'], 'L0_attn_Wq': _L0_attn_in['Wq'], 'L0_attn_Wk': _L0_attn_in['Wk'], 'L0_attn_Wv': _L0_attn_in['Wv'], 'L0_attn_Wrk': _L0_attn_in['Wrk'], 'L0_attn_r_w_bias': _L0_attn_in['r_w_bias'], 'L0_attn_r_r_bias': _L0_attn_in['r_r_bias'], 'L0_attn_Wo': _L0_attn_in['Wo'], 'L0_attn_bo': _L0_attn_in['bo'], 'L0_ffn_Wg': _L0_ffn_in['Wg'], 'L0_ffn_W1': _L0_ffn_in['W1'], 'L0_ffn_b1': _L0_ffn_in['b1'], 'L0_ffn_W2': _L0_ffn_in['W2'], 'L0_ffn_b2': _L0_ffn_in['b2']}

def reference(x, L0_tok_ln1_g, L0_tok_ln1_b, L0_tok_W_lin, L0_tok_b_lin, L0_tok_ln2_g, L0_tok_ln2_b, L0_tok_pos_embedding, L0_tok_cls_token, L0_attn_Wq, L0_attn_Wk, L0_attn_Wv, L0_attn_Wrk, L0_attn_r_w_bias, L0_attn_r_r_bias, L0_attn_Wo, L0_attn_bo, L0_ffn_Wg, L0_ffn_W1, L0_ffn_b1, L0_ffn_W2, L0_ffn_b2):
    import jax
    import jax.numpy as jnp

    def _L0_tok_ref(img, ln1_g, ln1_b, W_lin, b_lin, ln2_g, ln2_b, pos_embedding, cls_token):
        import jax, jax.numpy as jnp
        import numpy as np
        B, C, H, W = (64, 3, 96, 96)
        P = 16
        NH, NW = (H // P, W // P)
        N = NH * NW
        PATCH_DIM = C * P * P
        DIM = 192

        def _layernorm(x, g, b, eps=1e-05):
            mu = jnp.mean(x, axis=-1, keepdims=True)
            var = jnp.var(x, axis=-1, keepdims=True)
            return (x - mu) * jax.lax.rsqrt(var + eps) * g + b
        b = img.shape[0]
        x = img.reshape(b, C, NH, P, NW, P)
        x = jnp.transpose(x, (0, 2, 4, 3, 5, 1))
        x = x.reshape(b, N, PATCH_DIM)
        x = _layernorm(x, ln1_g, ln1_b)
        x = jnp.einsum('bnp,pd->bnd', x, W_lin) + b_lin
        x = _layernorm(x, ln2_g, ln2_b)
        cls = jnp.broadcast_to(cls_token, (b, 1, DIM))
        x = jnp.concatenate([cls, x], axis=1)
        x = x + pos_embedding[:, :N + 1]
        return x

    def _L0_attn_ref(x, Wq, Wk, Wv, Wrk, r_w_bias, r_r_bias, Wo, bo):
        import jax, jax.numpy as jnp
        import numpy as np
        B, T, D = (2, 512, 192)
        H, K, V = (8, 64, 96)
        F = 32

        def positional_features(positions, feature_size, seq_length):
            nb = feature_size // 2
            pow_rate = np.exp(np.log(seq_length + 1) / nb).astype(np.float32)
            center_widths = pow_rate ** jnp.arange(1, nb + 1, dtype=jnp.float32) - 1.0
            emb = (center_widths[None, :] > jnp.abs(positions)[:, None]).astype(jnp.float32)
            return jnp.concatenate([emb, jnp.sign(positions)[:, None] * emb], axis=-1)

        def relative_shift(x):
            b, h, t1, t2 = x.shape
            x = jnp.pad(x, ((0, 0), (0, 0), (0, 0), (1, 0)))
            x = x.reshape(b, h, t2 + 1, t1)[:, :, 1:, :].reshape(b, h, t1, t2)
            return x[..., :(t2 + 1) // 2]
        b, t, _ = x.shape
        q = (x @ Wq).reshape(b, t, H, K).transpose(0, 2, 1, 3) * K ** (-0.5)
        k = (x @ Wk).reshape(b, t, H, K).transpose(0, 2, 1, 3)
        v = (x @ Wv).reshape(b, t, H, V).transpose(0, 2, 1, 3)
        content = jnp.einsum('bhtk,bhsk->bhts', q + r_w_bias[None, :, None, :], k)
        positions = jnp.arange(-t + 1, t, dtype=jnp.float32)
        pos_emb = positional_features(positions, F, t)
        r_k = (pos_emb @ Wrk).reshape(2 * t - 1, H, K)
        rel = jnp.einsum('bhtk,rhk->bhtr', q + r_r_bias[None, :, None, :], r_k)
        rel = relative_shift(rel)
        attn = jax.nn.softmax(content + rel, axis=-1)
        out = jnp.einsum('bhts,bhsv->bhtv', attn, v)
        out = out.transpose(0, 2, 1, 3).reshape(b, t, H * V)
        return out @ Wo + bo

    def _L0_ffn_ref(x, Wg, W1, b1, W2, b2):
        import jax, jax.numpy as jnp
        import numpy as np
        DIM = 192
        NUM_EXPERTS = 8
        TOP_K = 2
        MLP_RATIO = 4
        CAPACITY_RATIO = 1.25
        B, N, C = x.shape
        E = W1.shape[0]
        K = TOP_K
        T = B * N
        cap = int(CAPACITY_RATIO * T * K / E)
        xf = x.reshape(T, C)
        logits = xf @ Wg
        topv, topi = jax.lax.top_k(logits, K)
        w = jax.nn.softmax(topv, axis=-1)
        priority = w[:, 0]
        order = jnp.argsort(-priority)
        e_ids = topi[order].reshape(T * K)
        w_ord = w[order].reshape(T * K)
        tok_rep = jnp.repeat(order, K)
        oh = jax.nn.one_hot(e_ids, E, dtype=jnp.int32)
        pos = (jnp.cumsum(oh, axis=0) * oh).sum(-1) - 1
        keep = pos < cap
        slot = jnp.where(keep, e_ids * cap + pos, E * cap)
        buf = jnp.zeros((E * cap + 1, C), xf.dtype).at[slot].set(xf[tok_rep])
        buf_e = buf[:E * cap].reshape(E, cap, C)
        h = jax.nn.gelu(jnp.einsum('ecd,edh->ech', buf_e, W1) + b1[:, None, :], approximate=False)
        out = jnp.einsum('ech,ehd->ecd', h, W2) + b2[:, None, :]
        out_flat = jnp.concatenate([out.reshape(E * cap, C), jnp.zeros((1, C), xf.dtype)], axis=0)
        y_assign = out_flat[slot] * (w_ord * keep.astype(xf.dtype))[:, None]
        y = jnp.zeros((T, C), xf.dtype).at[tok_rep].add(y_assign)
        return y.reshape(B, N, C)
    h = _L0_tok_ref(x, L0_tok_ln1_g, L0_tok_ln1_b, L0_tok_W_lin, L0_tok_b_lin, L0_tok_ln2_g, L0_tok_ln2_b, L0_tok_pos_embedding, L0_tok_cls_token)
    h = h + _L0_attn_ref(_layernorm(h, axis=-1), L0_attn_Wq, L0_attn_Wk, L0_attn_Wv, L0_attn_Wrk, L0_attn_r_w_bias, L0_attn_r_r_bias, L0_attn_Wo, L0_attn_bo)
    h = h + _L0_ffn_ref(_layernorm(h, axis=-1), L0_ffn_Wg, L0_ffn_W1, L0_ffn_b1, L0_ffn_W2, L0_ffn_b2)
    return h

_drawn_inputs = setup_inputs


def setup_inputs(seed=0):
    import zlib

    import numpy as np

    out = dict(_drawn_inputs(seed))
    spreads = {'L0_tok_ln1_g': (1.0, 0.2),
     'L0_tok_ln1_b': (0.0, 0.1),
     'L0_tok_b_lin': (0.0, 0.1),
     'L0_tok_ln2_g': (1.0, 0.2),
     'L0_tok_ln2_b': (0.0, 0.1),
     'L0_attn_bo': (0.0, 0.1),
     'L0_ffn_b1': (0.0, 0.1),
     'L0_ffn_b2': (0.0, 0.1)}
    factors = {'L0_attn_Wq': 6.086,
     'L0_attn_Wk': 4.636,
     'L0_attn_Wrk': 8.0,
     'L0_attn_r_w_bias': 7.579,
     'L0_attn_r_r_bias': 8.0}
    for name, (base, spread) in spreads.items():
        noise = np.random.default_rng([zlib.crc32(name.encode()), seed]).standard_normal(out[name].shape)
        drawn = base * np.exp(spread * noise) if base else spread * noise
        out[name] = jnp.asarray(drawn.astype(out[name].dtype))
    for name, factor in factors.items():
        out[name] = (out[name] * factor).astype(out[name].dtype)
    return out
```

```python
from contextlib import ExitStack

import numpy as np

import concourse.bass as bass
from concourse import mybir

F32 = mybir.dt.float32
BF16 = mybir.dt.bfloat16
I32 = mybir.dt.int32
ALU = mybir.AluOpType
ACT = mybir.ActivationFunctionType
AX = mybir.AxisListType

B, C, IMG, PATCH = 64, 3, 96, 16
NH = IMG // PATCH
D = 192
T = NH * NH + 1
H, K, V, F = 8, 64, 96, 32
R = 2 * T - 1
E, HID = 8, 4 * D
CAP = int(1.25 * B * T * 2 / E)
EPS = 1e-5

IPG = 3
G = IPG * T
NG = -(-B // IPG)
STEPS = NG // 2
ROWS = NG * G
LAST = B * T - (NG - 1) * G
G2 = 2 * G
KD = D // 2
HB = H // 2
WIDE = 640
SKEW = WIDE - 1
REL_IMG = T * SKEW
SPLIT = 96
PD = C * PATCH * PATCH
PC = PD // 128
XF = NH * PD
ZR = 8
TAIL = 4
XW = D + TAIL
NT = -(-CAP // 128)
HALF = CAP // 2
HC = HID // 128
N_CONST, N_AW = 23, 10
N_FILL = 2 + -(-(2 * ROWS // ZR) // 128) + (2 * ROWS % ZR > 0)
BIG = 1.0e6
assert NG % 2 == 0 and 36 * WIDE + H * R <= REL_IMG


def head_at(j):
    return j % HB * 2 + j // HB


def is_step(s, n):
    return isinstance(s, int) and s == n


def tile_rows(i):
    return min(128, CAP - 128 * i)


def build(nc, x, ln1_g, ln1_b, W_lin, b_lin, ln2_g, ln2_b, pos_embedding, cls_token,
          Wq, Wk, Wv, Wrk, r_w_bias, r_r_bias, Wo, bo, Wg, W1, b1, W2, b2,
          c_ident, c_block, c_ind, c_pos, c_iota, c_upper, c_real, c_tok, c_blank, out):
    h_dram = nc.dram_tensor("h_tokens", [ROWS, D], F32).ap()
    rel_dram = nc.dram_tensor("rel_scores", [NG * IPG * REL_IMG + WIDE], F32).ap()
    xbuf = nc.dram_tensor("routed_rows", [E * CAP, XW], F32).ap()
    ybuf = nc.dram_tensor("expert_out", [2 * ROWS, D], F32).ap()

    with ExitStack() as ctx:
        def sb(name, shape, dt=F32):
            return ctx.enter_context(nc.sbuf_tensor(name, shape, dt))

        def sem(name):
            return ctx.enter_context(nc.semaphore(name))

        PS = ctx.enter_context(nc.psum_tensor("PS", [128, 8, 512], F32))

        ident = sb("ident", [128, 128])
        block = sb("block", [G, G])
        ind = sb("ind", [G, IPG])
        pos_f = sb("pos_f", [F, R])
        iota8 = sb("iota8", [G, 2, E])
        upper = sb("upper", [G, G])
        real = sb("real", [G, NG])
        tok = sb("tok", [G, NG])
        eidx = sb("eidx", [128, E])
        blank = sb("blank", [128, XW])
        ones = sb("ones", [128, 128])
        zeros = sb("zeros", [128, ZR * D])
        meanw = sb("meanw", [128, 128])
        g1 = sb("g1", [128, PC])
        bb1 = sb("bb1", [128, PC])
        blin = sb("blin", [1, D])
        cB = sb("cB", [128, D])
        g2B = sb("g2B", [128, D])
        b2B = sb("b2B", [128, D])
        clsB = sb("clsB", [64, 2, D])
        clsP = sb("clsP", [64, D])
        wq = sb("wq", [KD, 2, H * K])
        wk = sb("wk", [KD, 2, H * K])
        wv = sb("wv", [KD, 2, H * V])
        wrk = sb("wrk", [F, H * K])
        rk = sb("rk", [128, HB, R])
        rwb = sb("rwb", [128, HB])
        rrb = sb("rrb", [128, HB])
        wo = sb("wo", [128, HC, D])
        bo_r = sb("bo_r", [1, D])
        wg = sb("wg", [KD, 2, E])

        def carve(memory):
            at = [0]

            def piece(parts, n, dt=F32):
                words = n if dt is F32 else n // 2
                a, at[0] = at[0], at[0] + words
                assert at[0] <= memory.shape[1]
                v = memory[0:parts, a:a + words]
                return v if dt is F32 else v.bitcast(dt)
            return piece

        wide = sb("wide", [128, (NH // 2) * XF])
        xv = wide[:, :].rearrange("p (j w f) -> p j w f", j=NH // 2, w=NH)
        piece = carve(wide)
        xT = piece(KD, 2 * G2).rearrange("p (k n) -> p k n", k=2)
        qw = piece(128, HB * G2).rearrange("p (m n) -> p m n", m=HB)
        qr = piece(128, HB * G2).rearrange("p (m n) -> p m n", m=HB)
        kT = piece(128, HB * G2).rearrange("p (m n) -> p m n", m=HB)
        v_sb = piece(G, 2 * H * V).rearrange("p (g n) -> p g n", g=2)
        rel = piece(G, 2 * H * R).rearrange("p (g n) -> p g n", g=2)
        relw = piece(G, 2 * H * T).rearrange("p (g n) -> p g n", g=2)
        sc = piece(G, 2 * H * T).rearrange("p (g n) -> p g n", g=2)
        pb = piece(G, 2 * H * G).rearrange("p (g n) -> p g n", g=2)
        pT = piece(G, 2 * H * G).rearrange("p (g n) -> p g n", g=2)
        o_sb = piece(G, 2 * H * V).rearrange("p (g n) -> p g n", g=2)
        oT = piece(128, 2 * HC * G).rearrange("p (g n) -> p g n", g=2)
        piece = carve(wide)
        hT = [piece(128, HC * CAP).rearrange("p (c n) -> p c n", c=HC) for _ in range(2)]
        prow = piece(G, ROWS)
        before = piece(G, 2 * ROWS, BF16).rearrange("p (a n) -> p a n", a=2)
        piece = carve(wide)
        ycat = piece(G, 8 * D).rearrange("p (a b c d) -> p a b c d", a=2, b=2, c=2)
        res = piece(G, 4 * D).rearrange("p (a c d) -> p a c d", a=2, c=2)

        narrow = sb("narrow", [128, 60 * D])
        piece = carve(narrow)
        W_raw = piece(128, PC * D).rearrange("p (c d) -> p c d", c=PC)
        W_cen = piece(128, PC * D).rearrange("p (c d) -> p c d", c=PC)
        posB = piece(128, NH * NH // 2 * D).rearrange("p (j n) -> p j n", j=NH // 2)
        xTt = piece(128, 2 * 6 * 128).rearrange("p (a c n) -> p a c n", a=2, c=6)
        zt = piece(128, NH * D).rearrange("p (w d) -> p w d", w=NH)
        ht = piece(128, 2 * NH * D).rearrange("p (a w d) -> p a w d", a=2, w=NH)
        piece = carve(narrow)
        xe = piece(128, 2 * NT * XW).rearrange("p (a n w) -> p a n w", a=2, n=NT)
        xeT = piece(KD, 2 * CAP).rearrange("p (k n) -> p k n", k=2)
        w1s = piece(KD, 4 * HID).rearrange("p (a k n) -> p a k n", a=2, k=2)
        w2s = piece(128, 2 * HC * D).rearrange("p (a c d) -> p a c d", a=2, c=HC)
        ye = piece(128, 2 * NT * D).rearrange("p (a n d) -> p a n d", a=2, n=NT)

        bn1 = sb("bn1", [128, NH, 2, 6])
        mv1 = sb("mv1", [128, NH, 2])
        ve1 = sb("ve1", [128, NH])
        rs1 = sb("rs1", [128, NH])
        nhalf = sb("nhalf", [128, NH])
        h_all = sb("h_all", [G, NG + 2, D])
        xr_all = sb("xr_all", [G, NG, XW])
        xn = sb("xn", [G, 2, D])
        xn2 = sb("xn2", [G, 2, D])
        xnT = sb("xnT", [KD, 2, G2])
        st = sb("st", [G, 6])
        mv = sb("mv", [G, 2, 2])
        ve = sb("ve", [G, 2])
        rs = sb("rs", [G, 2])
        st2 = sb("st2", [G, 6])
        mv2 = sb("mv2", [G, 2, 2])
        ve2 = sb("ve2", [G, 2])
        rs2 = sb("rs2", [G, 2])
        mx = sb("mx", [G, 2, H])
        rsum = sb("rsum", [G, 2, H])
        rinv = sb("rinv", [G, 2, H])
        logit = sb("logit", [G, NG, E])

        m1 = sb("m1", [G, NG])
        m2 = sb("m2", [G, NG])
        i1 = sb("i1", [G, NG])
        i2 = sb("i2", [G, NG])
        oh = sb("oh", [G, 2, NG, E])
        ohb = sb("ohb", [G, NG, E], BF16)
        tmp8 = sb("tmp8", [G, NG, E])
        l2 = sb("l2", [G, NG, E])
        ex = sb("ex", [G, NG])
        w01 = sb("w01", [G, 2, NG])
        prio = sb("prio", [G, NG])
        diag = sb("diag", [G, G])
        rank = sb("rank", [G, NG, E])
        posk = sb("posk", [G, 2, NG])
        keep = sb("keep", [G, 2, NG])
        slot = sb("slot", [G, 2, NG])
        sloti = sb("sloti", [G, 2, NG], I32)

        b1s = sb("b1s", [128, 2, HC])
        b2s = sb("b2s", [1, 2, D])
        first = sb("first", [128, 2, NT])
        wsel = sb("wsel", [128, 2, NT])
        wtmp = sb("wtmp", [128, 2, NT])
        dst = sb("dst", [128, 2, NT])
        dsti = sb("dsti", [128, 2, NT], I32)

        s_const = sem("const_loaded")
        s_x = [sem(f"x_loaded{j}") for j in range(NH // 2)]
        s_aw = sem("attn_weights_loaded")
        s_set = sem("memsets_done")
        s_setv = sem("dve_consts_done")
        s_gw = sem("gw_done")
        s_mean = sem("colmean_psum")
        s_rkp = sem("rk_psum")
        s_wc = sem("w_centred")
        s_rk = sem("rk_ready")
        s_xrc = [sem(f"routed_rows_copied{g}") for g in range(2)]
        s_cls = sem("cls_ready")
        s_tT = sem("tok_transposed")
        s_tTa = sem("tok_evac_act")
        s_tTd = sem("tok_evac_dve")
        s_tz = sem("tok_product")
        s_tze = sem("tok_product_used")
        s_v1 = sem("tok_var1")
        s_r1 = sem("tok_rstd1")
        s_v2 = sem("tok_var2")
        s_r2 = sem("tok_rstd2")
        s_tn = sem("tok_normed")
        s_ht = sem("tok_rows_ready")
        s_ho = [sem(f"tok_rows_stored{j}") for j in range(NH // 2)]
        s_fill = sem("dram_prefilled")
        s_h = sem("h_loaded")
        s_va = sem("ln1_var")
        s_ra = sem("ln1_rstd")
        s_xn = sem("ln1_rows")
        s_xTp = sem("xT_psum")
        s_xT = sem("xT_ready")
        s_qp = sem("q_psum")
        s_kp = sem("k_psum")
        s_q = sem("q_ready")
        s_k = sem("k_ready")
        s_rp = [sem(f"rel_psum{g}") for g in range(2)]
        s_re = [sem(f"rel_evacuated{g}") for g in range(2)]
        s_ro = [sem(f"rel_stored{g}") for g in range(2)]
        s_ri = [sem(f"rel_skewed{g}") for g in range(2)]
        s_vp = [sem(f"v_psum{g}") for g in range(2)]
        s_v = [sem(f"v_ready{g}") for g in range(2)]
        s_sp = [sem(f"scores_psum{g}") for g in range(2)]
        s_sc = [sem(f"scores_compact{g}") for g in range(2)]
        s_sh = [sem(f"scores_shifted{g}") for g in range(2)]
        s_p = [sem(f"probs_ready{g}") for g in range(2)]
        s_ptp = [sem(f"pT_psum{g}") for g in range(2)]
        s_pt = [sem(f"pT_ready{g}") for g in range(2)]
        s_op = [sem(f"o_psum{g}") for g in range(2)]
        s_o = [sem(f"o_ready{g}") for g in range(2)]
        s_otp = [sem(f"oT_psum{g}") for g in range(2)]
        s_ot = [sem(f"oT_ready{g}") for g in range(2)]
        s_wop = [sem(f"proj_psum{g}") for g in range(2)]
        s_h1 = [sem(f"h1_ready{g}") for g in range(2)]
        s_vb = [sem(f"ln2_var{g}") for g in range(2)]
        s_rb = [sem(f"ln2_rstd{g}") for g in range(2)]
        s_xr = [sem(f"ln2_rows{g}") for g in range(2)]
        s_xrp = sem("xnT_psum")
        s_xrT = sem("xnT_ready")
        s_lp = sem("logits_psum")
        s_l = sem("logits_ready")
        s_d = sem("gap_ready")
        s_e = sem("gap_exp")
        s_prio = sem("prio_ready")
        s_pbp = sem("prio_rows_psum")
        s_pb = sem("prio_rows_ready")
        s_bef = sem("before_ready")
        s_cnt = sem("before_counted")
        s_slot = sem("slots_ready")
        s_sct = sem("rows_scattered")
        s_ex = [sem(f"expert_rows_loaded{p}") for p in range(2)]
        s_ew = [sem(f"expert_weights_loaded{p}") for p in range(2)]
        s_xep = sem("xeT_psum")
        s_xea = sem("xeT_evac_act")
        s_xed = sem("xeT_evac_dve")
        s_hp = sem("hidden_psum")
        s_hg = sem("hidden_ready")
        s_yp = sem("y_psum")
        s_ye = sem("y_scaled")
        s_di = sem("dest_ready")
        s_ys = [sem(f"y_scattered{p}") for p in range(2)]
        s_yl = [sem(f"y_loaded{p}") for p in range(2)]
        s_sum = sem("sum_ready")
        s_out = [sem(f"out_stored{p}") for p in range(2)]

        def bc(ap, shape):
            return ap.to_broadcast(shape)

        def heads(bank, n):
            return PS[0:G, bank:bank + 2, :].rearrange("p a (h t) -> p (a h) t", h=HB)[:, :, 0:n]

        blk = ctx.enter_context(nc.Block())

        @blk.sync
        def _(sp):
            def load_x(j):
                for u in range(2):
                    sp.dma_start(wide[64 * u:64 * u + 64, j * XF:(j + 1) * XF], x[2 * j + u]).then_inc(s_x[j], 16)

            load_x(0)
            sp.dma_start(W_raw[:, :, :], W_lin.rearrange("(c p) d -> p c d", p=128)).then_inc(s_const, 16)
            sp.dma_start(g1[:, :], ln1_g).then_inc(s_const, 16)
            sp.dma_start(bb1[:, :], ln1_b).then_inc(s_const, 16)
            row = lambda ap: ap.rearrange("(a d) -> a d", a=1)
            sp.dma_start(blin[:, :], row(b_lin)).then_inc(s_const, 16)
            sp.dma_start(ident[:, :], c_ident).then_inc(s_const, 16)
            sp.dma_start(block[:, :], c_block).then_inc(s_const, 16)
            sp.dma_start(ind[:, :], c_ind).then_inc(s_const, 16)
            sp.dma_start(pos_f[:, :], c_pos).then_inc(s_const, 16)
            sp.dma_start(iota8[:, :, :], c_iota[0:G]).then_inc(s_const, 16)
            sp.dma_start(eidx[:, :], c_iota[:, 0, :]).then_inc(s_const, 16)
            sp.dma_start(upper[:, :], c_upper).then_inc(s_const, 16)
            sp.dma_start(real[:, :], c_real).then_inc(s_const, 16)
            sp.dma_start(blank[:, :], c_blank).then_inc(s_const, 16)
            sp.dma_start(g2B[:, :], bc(row(ln2_g), [128, D])).then_inc(s_const, 16)
            sp.dma_start(b2B[:, :], bc(row(ln2_b), [128, D])).then_inc(s_const, 16)
            for n in range(NH):
                src = pos_embedding[0, 1 + n * NH:1 + (n + 1) * NH, :].rearrange("(a t) d -> a (t d)", a=1)
                sp.dma_start(posB[64 * (n % 2):64 * (n % 2) + 64, n // 2, :],
                             bc(src, [64, NH * D])).then_inc(s_const, 16)
            sp.dma_start(clsB[:, 0, :], bc(cls_token[0], [64, D])).then_inc(s_const, 16)
            sp.dma_start(clsB[:, 1, :], bc(pos_embedding[0, 0:1, :], [64, D])).then_inc(s_const, 16)
            load_x(1)
            load_x(2)
            sp.dma_start(wq[:, :, :], Wq.rearrange("(k p) n -> p k n", k=2)).then_inc(s_aw, 16)
            sp.dma_start(wk[:, :, :], Wk.rearrange("(k p) n -> p k n", k=2)).then_inc(s_aw, 16)
            sp.dma_start(wv[:, :, :], Wv.rearrange("(k p) n -> p k n", k=2)).then_inc(s_aw, 16)
            sp.dma_start(wrk[:, :], Wrk).then_inc(s_aw, 16)
            sp.dma_start(rwb[:, :], r_w_bias).then_inc(s_aw, 16)
            sp.dma_start(rrb[:, :], r_r_bias).then_inc(s_aw, 16)
            sp.dma_start(wo[:, :, :], Wo.rearrange("(c p) d -> p c d", p=128)).then_inc(s_aw, 16)
            sp.dma_start(bo_r[:, :], row(bo)).then_inc(s_aw, 16)
            sp.dma_start(wg[:, :, :], Wg.rearrange("(k p) n -> p k n", k=2)).then_inc(s_aw, 16)
            sp.dma_start(tok[:, :], c_tok).then_inc(s_aw, 16)

            sp.wait_ge(s_set, 1)
            sp.wait_ge(s_const, 16 * N_CONST)
            n0 = E * CAP // 128 * 128
            sp.dma_start(xbuf[0:n0].rearrange("(p n) w -> p n w", p=128),
                         bc(blank[:, :].rearrange("p (a w) -> p a w", a=1), [128, n0 // 128, XW])).then_inc(s_fill, 16)
            sp.dma_start(xbuf[n0:E * CAP], blank[0:E * CAP - n0, :]).then_inc(s_fill, 16)
            nz = 2 * ROWS // ZR
            for a in range(0, nz, 128):
                n = min(128, nz - a)
                sp.dma_start(ybuf[a * ZR:(a + n) * ZR].rearrange("(n r) d -> n (r d)", r=ZR),
                             zeros[0:n, :]).then_inc(s_fill, 16)
            if 2 * ROWS % ZR:
                sp.dma_start(ybuf[nz * ZR:2 * ROWS], zeros[0:2 * ROWS % ZR, 0:D]).then_inc(s_fill, 16)

            hv = h_dram[0:B * T, :].rearrange("(b t) d -> b t d", t=T)
            for j in range(NH // 2):
                sp.wait_ge(s_ht, j + 1)
                for u in range(2):
                    n = 2 * j + u
                    sp.dma_start(hv[:, 1 + n * NH:1 + (n + 1) * NH, :].rearrange("b t d -> b (t d)"),
                                 ht[64 * u:64 * u + 64, j % 2].rearrange("p t d -> p (t d)")).then_inc(s_ho[j], 16)
                if j == 0:
                    sp.wait_ge(s_cls, 1)
                    sp.dma_start(hv[:, 0, :], clsP[:, :]).then_inc(s_ho[0], 16)
                    sp.dma_start(h_dram[B * T:ROWS, :], zeros[0:ROWS - B * T, 0:D]).then_inc(s_ho[0], 16)
            for j in range(NH // 2):
                sp.wait_ge(s_ho[j], 64 if j == 0 else 32)

            hg = h_dram.rearrange("(g p) d -> p g d", p=G)
            for a, b_ in ((0, 2), (2, NG)):
                sp.dma_start(h_all[0:SPLIT, a:b_], hg[0:SPLIT, a:b_]).then_inc(s_h, 16)
                sp.dma_start(h_all[SPLIT:G, a:b_], hg[SPLIT:G, a:b_]).then_inc(s_h, 16)
                sp.wait_ge(s_h, 32 if a == 0 else 64)

            def rows_of(start, n, pitch):
                return rel_dram[bass.ds(start, n * pitch)].rearrange("(p w) -> p w", w=pitch)[:, 0:H * R]

            def rel_roundtrip(s):
                for g in range(2):
                    base = (2 * s + g) * (IPG * REL_IMG)
                    sp.wait_ge(s_re[g], s + 1)
                    for i in range(IPG):
                        for t0, t1 in ((0, 32), (32, T)):
                            sp.dma_start(rows_of(base + i * REL_IMG + t0 * WIDE, t1 - t0, WIDE),
                                         rel[i * T + t0:i * T + t1, g, :]).then_inc(s_ro[g], 16)
                for g in range(2):
                    base = (2 * s + g) * (IPG * REL_IMG) + T - 1
                    sp.wait_ge(s_ro[g], 16 * 6 * (s + 1))
                    if not isinstance(s, int) or s:
                        sp.wait_ge(s_sc[g], s)
                    for p0, p1 in ((0, SPLIT), (SPLIT, G)):
                        sp.dma_start(relw[p0:p1, g, :].rearrange("p (h t) -> p h t", h=H),
                                     rows_of(base + p0 * SKEW, p1 - p0, SKEW).rearrange(
                                         "p (h r) -> p h r", h=H)[:, :, 0:T]).then_inc(s_ri[g], 16)

            rel_roundtrip(0)
            with sp.Fori(1, STEPS) as s:
                rel_roundtrip(s)

            def load_weights(e, p):
                sp.dma_start(w1s[:, p], W1[bass.ds(e, 1)].rearrange("a (k p) n -> p (a k) n", k=2)).then_inc(s_ew[p], 16)
                sp.dma_start(w2s[:, p], W2[bass.ds(e, 1)].rearrange("a (c p) d -> p (a c) d", p=128)).then_inc(s_ew[p], 16)
                sp.dma_start(b1s[:, p], b1[bass.ds(e, 1)].rearrange("a p c -> p (a c)")).then_inc(s_ew[p], 16)
                sp.dma_start(b2s[:, p], b2[bass.ds(e, 1)]).then_inc(s_ew[p], 16)

            def load_rows(e, p):
                full = CAP // 128
                sp.dma_start(xe[:, p, 0:full],
                             xbuf[bass.ds(e * CAP, full * 128)].rearrange("(n q) w -> q n w", q=128)
                             ).then_inc(s_ex[p], 16)
                sp.dma_start(xe[0:CAP - full * 128, p, full],
                             xbuf[bass.ds(e * CAP + full * 128, CAP - full * 128)]).then_inc(s_ex[p], 16)

            for p in range(2):
                load_weights(p, p)
            sp.wait_ge(s_sct, 16 * 2 * NG)
            for p in range(2):
                load_rows(p, p)
            with sp.Fori(1, E // 2) as i:
                for p in range(2):
                    e = i * 2 + p
                    sp.wait_ge(s_ye, NT * (e - 1))
                    load_weights(e, p)
                    load_rows(e, p)

            yv = ybuf.rearrange("(k g p) d -> p k g d", k=2, p=G)
            for p in range(2):
                sp.wait_ge(s_ys[p], 16 * NT * (E // 2))

            def load_y(s, p):
                for k in range(2):
                    for p0, p1 in ((0, SPLIT), (SPLIT, G)):
                        sp.dma_start(ycat[p0:p1, p, k], yv[p0:p1, k, bass.ds(2 * s, 2), :]).then_inc(s_yl[p], 16)

            def store(s, p, groups):
                for g, n in groups:
                    for p0, p1 in ((0, min(n, SPLIT)), (SPLIT, n)):
                        if p1 > p0:
                            sp.dma_start(out[bass.ds((2 * s + g) * G + p0, p1 - p0)],
                                         res[p0:p1, p, g]).then_inc(s_out[p], 16)

            load_y(0, 0)
            load_y(1, 1)
            both = ((0, G), (1, G))
            with sp.Fori(0, STEPS // 2 - 1) as i:
                for p in range(2):
                    sp.wait_ge(s_sum, i * 2 + p + 1)
                    store(i * 2 + p, p, both)
                    load_y(i * 2 + p + 2, p)
            for s in range(STEPS - 3, STEPS):
                sp.wait_ge(s_sum, s + 1)
                store(s, s % 2, both if s < STEPS - 1 else ((0, G), (1, LAST)))
                if s + 2 < STEPS:
                    load_y(s + 2, s % 2)
            sp.wait_ge(s_out[0], 64 * (STEPS // 2) + 48)
            sp.wait_ge(s_out[1], 64 * (STEPS // 2))
            sp.wait_ge(s_fill, 16 * N_FILL)

        @blk.tensor
        def _(pe):
            pe.wait_ge(s_const, 16 * N_CONST)
            pe.wait_ge(s_set, 2)
            pe.wait_ge(s_gw, 1)
            for c in range(PC):
                pe.matmul(PS[:, 6, 0:D], meanw[:, :], W_cen[:, c, :], start=(c == 0), stop=(c == PC - 1))
            for c in range(PC):
                pe.matmul(PS[:, 7, 0:D], bc(bb1[:, c:c + 1], [128, 128]), W_raw[:, c, :], start=(c == 0), stop=False)
            pe.matmul(PS[:, 7, 0:D], ones[0:1, :], blin[:, :], start=False, stop=True).then_inc(s_mean, 1)

            units = [(j, w) for j in range(NH // 2) for w in range(NH)]

            def tok_transpose(u):
                j, w = units[u]
                if w == 0:
                    pe.wait_ge(s_x[j], 32)
                if u >= 2:
                    pe.wait_ge(s_tTa, u - 1)
                    pe.wait_ge(s_tTd, u - 1)
                for c in range(PC):
                    last = pe.transpose(PS[:, 2 * (u % 2) + c // 3, 128 * (c % 3):128 * (c % 3) + 128],
                                        xv[:, j, w, 128 * c:128 * c + 128], ident[:, :])
                last.then_inc(s_tT, 1)

            def tok_product(u):
                pe.wait_ge(s_tTa, u + 1)
                pe.wait_ge(s_tTd, u + 1)
                if u >= 2:
                    pe.wait_ge(s_tze, u - 1)
                for c in range(PC):
                    last = pe.matmul(PS[:, 4 + u % 2, 0:D], xTt[:, u % 2, c, :], W_cen[:, c, :],
                                     start=(c == 0), stop=(c == PC - 1))
                last.then_inc(s_tz, 1)

            tok_transpose(0)
            pe.wait_ge(s_wc, 1)
            for u in range(len(units)):
                if u + 1 < len(units):
                    tok_transpose(u + 1)
                tok_product(u)

            pe.wait_ge(s_aw, 16 * N_AW)
            for m in range(HB):
                last = pe.matmul(PS[:, 6, m * R:(m + 1) * R], wrk[:, m * 128:(m + 1) * 128], pos_f[:, :],
                                 start=(m == 0), stop=(m == HB - 1), skip_group_check=True)
            last.then_inc(s_rkp, 1)

            def front(s, first):
                pe.wait_ge(s_xn, s + 1)
                if not first:
                    pe.wait_ge(s_v[0], s)
                for g in range(2):
                    for k in range(2):
                        last = pe.transpose(PS[0:KD, 0, k * G2 + g * G:k * G2 + (g + 1) * G],
                                            xn[:, g, k * KD:(k + 1) * KD], ident[0:G, 0:G])
                last.then_inc(s_xTp, 1)
                pe.wait_ge(s_xT, s + 1)
                for m2 in range(2):
                    if m2 == 1 and not first and not is_step(s, 1):
                        pe.wait_ge(s_l, s - 1)
                    for w, bank, done in ((wq, 1 - m2, s_qp), (wk, 2 + m2, s_kp)):
                        for m in (2 * m2, 2 * m2 + 1):
                            for k in range(2):
                                last = pe.matmul(PS[:, bank, (m % 2) * G2:(m % 2 + 1) * G2],
                                                 w[:, k, m * 128:(m + 1) * 128], xT[:, k, :],
                                                 start=(k == 0 and m % 2 == 0), stop=(k == 1),
                                                 skip_group_check=True)
                        last.then_inc(done, 1)
                pe.wait_ge(s_q, s * 2 + 2)
                if first:
                    pe.wait_ge(s_rk, 1)
                else:
                    pe.wait_ge(s_sc[1], s)
                for g in range(2):
                    for h in range(H):
                        q0 = 64 * (h % 2)
                        last = pe.matmul(PS[0:G, (6, 0)[g] + h % 2, (h // 2) * R:(h // 2 + 1) * R],
                                         qr[q0:q0 + 64, h // 2, g * G:(g + 1) * G], rk[q0:q0 + 64, h // 2, :],
                                         start=(h // 2 == 0), stop=True, skip_group_check=True)
                    last.then_inc(s_rp[g], 1)

            def back(s):
                for g in range(2):
                    pe.wait_ge(s_p[g], s + 1)
                    if g == 0:
                        pe.wait_ge(s_k, fronts(s) * 2)
                        if is_step(s, STEPS - 1):
                            pe.wait_ge(s_l, s)
                    for j in range(H):
                        last = pe.transpose(heads(2 + 2 * g, G)[:, j, :],
                                            pb[:, g, j * G:(j + 1) * G], ident[0:G, 0:G])
                    last.then_inc(s_ptp[g], 1)
                for g in range(2):
                    pe.wait_ge(s_pt[g], s + 1)
                    pe.wait_ge(s_v[g], s + 1)
                    if g == 0:
                        pe.wait_ge(s_re[0], fronts(s))
                    for j in range(H):
                        h = head_at(j)
                        last = pe.matmul(heads((6, 2)[g], V)[:, j, :],
                                         pT[:, g, j * G:(j + 1) * G], v_sb[:, g, h * V:(h + 1) * V],
                                         start=(j % HB == 0), stop=True, skip_group_check=True)
                    last.then_inc(s_op[g], 1)
                for g in range(2):
                    pe.wait_ge(s_o[g], s + 1)
                    for c in range(HC):
                        last = pe.transpose(PS[:, (4, 6)[g] + c // 3, (c % 3) * G:(c % 3 + 1) * G],
                                            o_sb[:, g, c * 128:(c + 1) * 128], ident[0:G, 0:G])
                    last.then_inc(s_otp[g], 1)
                pe.wait_ge(s_re[1], fronts(s))
                for g in range(2):
                    pe.wait_ge(s_ot[g], s + 1)
                    for c in range(HC):
                        pe.matmul(PS[0:G, g, 0:D], oT[:, g, c * G:(c + 1) * G], wo[:, c, :],
                                  start=(c == 0), stop=False)
                    pe.matmul(PS[0:G, g, 0:D], ones[0:1, 0:G], bo_r[:, :], start=False, stop=True
                              ).then_inc(s_wop[g], 1)

            def scores(s, first):
                for g in range(2):
                    if not first:
                        if g == 0:
                            pe.wait_ge(s_h1[0], s)
                            pe.wait_ge(s_h1[1], s)
                        else:
                            pe.wait_ge(s_o[1], s)
                    else:
                        if g == 0:
                            pe.wait_ge(s_re[1], 1)
                        else:
                            pe.wait_ge(s_k, 2)
                    for n in range(2):
                        for k in range(2):
                            last = pe.matmul(PS[0:G, 2 * g + n, 0:HB * V], xT[:, k, g * G:(g + 1) * G],
                                             wv[:, k, n * HB * V:(n + 1) * HB * V], start=(k == 0), stop=(k == 1))
                    last.then_inc(s_vp[g], 1)
                pe.wait_ge(s_k, s * 2 + 2)
                for g in range(2):
                    if not first:
                        pe.wait_ge(s_ot[g], s)
                    elif g == 1:
                        pe.wait_ge(s_re[0], 1)
                    for h in range(H):
                        q0 = 64 * (h % 2)
                        last = pe.matmul(heads(4 + 2 * g, G)[:, h % 2 * HB + h // 2, :],
                                         qw[q0:q0 + 64, h // 2, g * G:(g + 1) * G],
                                         kT[q0:q0 + 64, h // 2, g * G:(g + 1) * G],
                                         start=(h // 2 == 0), stop=True, skip_group_check=True)
                    last.then_inc(s_sp[g], 1)

            def gate(s, n):
                pe.wait_ge(s_v[1], n)
                for g in range(2):
                    pe.wait_ge(s_xr[g], s + 1)
                    for k in range(2):
                        last = pe.transpose(PS[0:KD, 2, k * G2 + g * G:k * G2 + (g + 1) * G],
                                            xn2[:, g, k * KD:(k + 1) * KD], ident[0:G, 0:G])
                last.then_inc(s_xrp, 1)
                pe.wait_ge(s_xrT, s + 1)
                for g in range(2):
                    for k in range(2):
                        last = pe.matmul(PS[0:G, 3, g * E:(g + 1) * E], xnT[:, k, g * G:(g + 1) * G], wg[:, k, :],
                                         start=(g == 0 and k == 0), stop=(k == 1), skip_group_check=True)
                last.then_inc(s_lp, 1)

            def fronts(s):
                return STEPS if isinstance(s, int) and s == STEPS - 1 else s + 2

            front(0, True)
            scores(0, True)

            def step(s):
                front(s, False)
                back(s - 1)
                scores(s, False)
                gate(s - 1, s + 1)

            step(1)
            with pe.Fori(2, STEPS) as s:
                step(s)
            back(STEPS - 1)
            gate(STEPS - 1, STEPS)

            pe.wait_ge(s_prio, 1)
            for g in range(NG):
                last = pe.transpose(PS[0:G, g // 4, (g % 4) * G:(g % 4 + 1) * G],
                                    bc(prio[:, g:g + 1], [G, G]), ident[0:G, 0:G])
                if g % 4 == 3 or g == NG - 1:
                    last.then_inc(s_pbp, 1)

            def count(i, slot_, first):
                for j in range(NG):
                    last = pe.matmul(PS[0:G, 7, j * E:(j + 1) * E], before[:, slot_, j * G:(j + 1) * G],
                                     ohb[:, i, :], start=(first and j == 0), stop=True, skip_group_check=True)
                last.then_inc(s_cnt, 1)

            for i in range(2):
                pe.wait_ge(s_bef, i + 1)
                count(i, i, i == 0)
            with pe.Fori(1, NG // 2) as ii:
                for p in range(2):
                    pe.wait_ge(s_bef, ii * 2 + p + 1)
                    count(ii * 2 + p, p, False)

            def expert(i2, p, first):
                e = i2 * 2 + p
                pe.wait_ge(s_ex[p], i2 * 32 + 32)
                for k in range(2):
                    for i in range(NT):
                        n = tile_rows(i)
                        last = pe.transpose(PS[0:KD, 2 * k + i // 4, 128 * (i % 4):128 * (i % 4) + n],
                                            xe[0:n, p, i, k * KD:(k + 1) * KD], ident[0:n, 0:n])
                last.then_inc(s_xep, 1)
                pe.wait_ge(s_ew[p], i2 * 64 + 64)
                pe.wait_ge(s_xea, e + 1)
                pe.wait_ge(s_xed, e + 1)
                per = 2 * HC
                for c in range(HC):
                    for n in range(2):
                        u = 2 * c + n
                        bank = 4 + u % 4
                        if u >= 4:
                            pe.wait_ge(s_hg, e * per + u - 3)
                        elif u < 2 and not first:
                            pe.wait_ge(s_ye, e * NT - 1 + u)
                        for k in range(2):
                            last = pe.matmul(PS[:, bank, 0:HALF], w1s[:, p, k, c * 128:(c + 1) * 128],
                                             xeT[:, k, n * HALF:(n + 1) * HALF], start=(k == 0), stop=(k == 1))
                        last.then_inc(s_hp, 1)
                for i in range(NT):
                    bank = 4 + i % 4
                    n = tile_rows(i)
                    if i >= 4:
                        pe.wait_ge(s_ye, e * NT + i - 3)
                    else:
                        pe.wait_ge(s_hg, e * per + per)
                    for c in range(HC):
                        pe.matmul(PS[0:n, bank, 0:D], hT[p][:, c, 128 * i:128 * i + n], w2s[:, p, c, :],
                                  start=(c == 0), stop=False)
                    pe.matmul(PS[0:n, bank, 0:D], ones[0:1, 0:n], b2s[:, p, :], start=False, stop=True
                              ).then_inc(s_yp, 1)

            for p in range(2):
                expert(0, p, p == 0)
            with pe.Fori(1, E // 2) as i:
                for p in range(2):
                    expert(i, p, False)

        @blk.scalar
        def _(act):
            for u in range((NH // 2) * NH):
                act.wait_ge(s_tT, u + 1)
                if u >= 2:
                    act.wait_ge(s_tz, u - 1)
                nc.scalar.copy(xTt[:, u % 2, 0:3, :].rearrange("p c n -> p (c n)"),
                               PS[:, 2 * (u % 2), 0:384]).then_inc(s_tTa, 1)

            def front(s, first):
                act.wait_ge(s_xTp, s + 1)
                nc.scalar.copy(xT[:, :, :].rearrange("p k n -> p (k n)"), PS[0:KD, 0, 0:2 * G2]).then_inc(s_xT, 1)
                for m2 in range(2):
                    act.wait_ge(s_qp, s * 2 + m2 + 1)
                    for q, b_ in ((qr, rrb), (qw, rwb)):
                        for m in (2 * m2, 2 * m2 + 1):
                            last = nc.scalar.activation(q[:, m, :], PS[:, 1 - m2, (m % 2) * G2:(m % 2 + 1) * G2],
                                                        ACT.Identity, bias=b_[:, m:m + 1], scale=K ** -0.5)
                    last.then_inc(s_q, 1)
                for g in range(2):
                    act.wait_ge(s_rp[g], s + 1)
                    if not first:
                        act.wait_ge(s_ro[g], 96 * s)
                    nc.scalar.copy(rel[:, g, :].rearrange("p (a n) -> p a n", a=2),
                                   PS[0:G, (6, 0)[g]:(8, 2)[g], 0:HB * R]).then_inc(s_re[g], 1)

            def back(s):
                for g in range(2):
                    act.wait_ge(s_otp[g], s + 1)
                    nc.scalar.copy(oT[:, g, :].rearrange("p (a n) -> p a n", a=2),
                                   PS[:, (4, 6)[g]:(6, 8)[g], 0:3 * G]).then_inc(s_ot[g], 1)

            def values(s):
                for g in range(2):
                    act.wait_ge(s_vp[g], s + 1)
                    nc.scalar.copy(v_sb[:, g, :].rearrange("p (a n) -> p a n", a=2),
                                   PS[0:G, 2 * g:2 * g + 2, 0:HB * V]).then_inc(s_v[g], 1)

            def probs(s):
                for g in range(2):
                    act.wait_ge(s_sh[g], s + 1)
                    nc.scalar.activation(
                        pb[:, g, :].rearrange("p (h i t) -> p h i t", h=H, i=IPG),
                        bc(sc[:, g, :].rearrange("p (h a t) -> p h a t", h=H, a=1), [G, H, IPG, T]),
                        ACT.Exp).then_inc(s_p[g], 1)

            def gate(s):
                act.wait_ge(s_xrp, s + 1)
                nc.scalar.copy(xnT[:, :, :].rearrange("p k n -> p (k n)"), PS[0:KD, 2, 0:2 * G2]).then_inc(s_xrT, 1)

            act.wait_ge(s_aw, 16 * N_AW)
            front(0, True)
            values(0)
            probs(0)

            def step(s):
                front(s, False)
                back(s - 1)
                values(s)
                gate(s - 1)
                probs(s)

            step(1)
            with act.Fori(2, STEPS) as s:
                step(s)
            back(STEPS - 1)
            gate(STEPS - 1)
            act.wait_ge(s_d, 1)
            nc.scalar.activation(ex[:, :], ex[:, :], ACT.Exp).then_inc(s_e, 1)

            def expert(e, p):
                act.wait_ge(s_xep, e + 1)
                for k in range(2):
                    last = nc.scalar.copy(xeT[:, k, 512:CAP], PS[0:KD, 2 * k + 1, 0:CAP - 512])
                last.then_inc(s_xea, 1)
                for c in range(HC):
                    for n in range(2):
                        act.wait_ge(s_hp, e * (2 * HC) + 2 * c + n + 1)
                        nc.scalar.activation(hT[p][:, c, n * HALF:(n + 1) * HALF], PS[:, 4 + (2 * c + n) % 4, 0:HALF],
                                             ACT.Gelu, bias=b1s[:, p, c:c + 1]).then_inc(s_hg, 1)

            with act.Fori(0, E // 2) as i:
                for p in range(2):
                    act.wait_ge(s_ew[p], i * 64 + 64)
                    expert(i * 2 + p, p)

        @blk.vector
        def _(dve):
            v = nc.vector

            def ch(ins):
                dve.drain()

            v.memset(ones[:, :], 1.0)
            v.memset(zeros[:, :], 0.0).then_inc(s_set, 1)
            v.memset(meanw[:, :], 1.0 / PD).then_inc(s_set, 1)
            v.memset(h_all[:, NG:NG + 2, :], 0.0)
            v.memset(nhalf[:, :], -0.5).then_inc(s_setv, 1)

            dve.wait_ge(s_const, 16 * N_CONST)
            for c in range(PC):
                last = v.tensor_scalar(W_cen[:, c, :], W_raw[:, c, :], g1[:, c:c + 1], None, ALU.mult)
            last.then_inc(s_gw, 1)
            dve.wait_ge(s_gw, 1)
            ch(v.tensor_tensor(posB[:, :, :].rearrange("p j (w d) -> p (j w) d", w=NH),
                               posB[:, :, :].rearrange("p j (w d) -> p (j w) d", w=NH),
                               bc(b2B[:, :].rearrange("p (a d) -> p a d", a=1), [128, NH * NH // 2, D]), ALU.add))
            dve.wait_ge(s_mean, 1)
            for c in range(PC):
                last = v.tensor_tensor(W_cen[:, c, :], W_cen[:, c, :], PS[:, 6, 0:D], ALU.subtract)
            last.then_inc(s_wc, 1)
            ch(v.tensor_copy(cB[:, :], PS[:, 7, 0:D]))
            v.tensor_tensor(clsP[:, :], clsB[:, 0, :], clsB[:, 1, :], ALU.add).then_inc(s_cls, 1)

            def ln1_stats(j):
                dve.wait_ge(s_x[j], 32)
                for w in range(NH):
                    for q in range(2):
                        last = v.bn_stats(bn1[:, w, q, :], xv[:, j, w, q * (PD // 2):(q + 1) * (PD // 2)])
                ch(last)
                for w in range(NH):
                    last = v.bn_aggr(mv1[:, w, :], bn1[:, w, :, :])
                ch(last)
                v.tensor_scalar(ve1[:, :], mv1[:, :, 1], EPS, None, ALU.add).then_inc(s_v1, 1)

            def evac(u):
                dve.wait_ge(s_tT, u + 1)
                if u >= 2:
                    dve.wait_ge(s_tz, u - 1)
                v.tensor_copy(xTt[:, u % 2, 3:6, :].rearrange("p c n -> p (c n)"),
                              PS[:, 2 * (u % 2) + 1, 0:384]).then_inc(s_tTd, 1)

            evac(0)
            for j in range(NH // 2):
                ln1_stats(j)
                for w in range(NH):
                    u = j * NH + w
                    if u + 1 < (NH // 2) * NH:
                        evac(u + 1)
                    if w == 0:
                        dve.wait_ge(s_r1, j + 1)
                    dve.wait_ge(s_tz, u + 1)
                    ins = v.scalar_tensor_tensor(zt[:, w, :], PS[:, 4 + u % 2, 0:D], rs1[:, w:w + 1], cB[:, :],
                                                 ALU.mult, ALU.add)
                    ins.then_inc(s_tze, 1)
                dve.wait_ge(s_tze, (j + 1) * NH)
                for w in range(NH):
                    last = v.bn_stats(bn1[:, w, 0, :], zt[:, w, :])
                ch(last)
                for w in range(NH):
                    last = v.bn_aggr(mv1[:, w, :], bn1[:, w, 0, :])
                ch(last)
                v.tensor_scalar(ve1[:, :], mv1[:, :, 1], EPS, None, ALU.add).then_inc(s_v2, 1)
                dve.wait_ge(s_r2, j + 1)
                for w in range(NH):
                    last = v.tensor_scalar(zt[:, w, :], zt[:, w, :], mv1[:, w, 0:1], rs1[:, w:w + 1],
                                           ALU.subtract, ALU.mult)
                ch(last)
                ch(v.tensor_tensor(zt[:, :, :], zt[:, :, :],
                                   bc(g2B[:, :].rearrange("p (a d) -> p a d", a=1), [128, NH, D]), ALU.mult))
                if j >= 2:
                    dve.wait_ge(s_ho[j - 2], 64)
                ins = v.tensor_tensor(ht[:, j % 2], zt[:, :, :],
                                      posB[:, j, :].rearrange("p (w d) -> p w d", w=NH), ALU.add)
                ins.then_inc(s_ht, 1)
                dve.wait_ge(s_ht, j + 1)
            dve.wait_ge(s_rkp, 1)
            v.tensor_copy(rk[:, :, :].rearrange("p m r -> p (m r)"), PS[:, 6, 0:HB * R]).then_inc(s_rk, 1)

            def ln1(s):
                for g in range(2):
                    ch(v.bn_stats(st[:, :], h_all[:, 2 * s + g, :]))
                    ch(v.bn_aggr(mv[:, g, :], st[:, :]))
                v.tensor_scalar(ve[:, :], mv[:, :, 1], EPS, None, ALU.add).then_inc(s_va, 1)
                dve.wait_ge(s_ra, s + 1)
                for g in range(2):
                    last = v.tensor_scalar(xn[:, g, :], h_all[:, 2 * s + g, :], mv[:, g, 0:1], rs[:, g:g + 1],
                                           ALU.subtract, ALU.mult)
                last.then_inc(s_xn, 1)

            def keys(s):
                for m2 in range(2):
                    dve.wait_ge(s_kp, s * 2 + m2 + 1)
                    v.tensor_copy(kT[:, 2 * m2:2 * m2 + 2, :].rearrange("p m n -> p (m n)"),
                                  PS[:, 2 + m2, 0:2 * G2]).then_inc(s_k, 1)

            def softmax(s):
                for g in range(2):
                    dve.wait_ge(s_sp[g], s + 1)
                    dve.wait_ge(s_ri[g], s * 32 + 32)
                    a3 = sc[:, g, :].rearrange("p (h t) -> p h t", h=H)
                    r3 = relw[:, g, :].rearrange("p (h t) -> p h t", h=H)
                    for i in range(IPG):
                        ins = v.scalar_tensor_tensor(a3, heads(4 + 2 * g, G)[:, :, i * T:(i + 1) * T],
                                                     ind[:, i:i + 1], a3 if i else r3, ALU.mult, ALU.add)
                        if i < IPG - 1:
                            ch(ins)
                    ins.then_inc(s_sc[g], 1)
                    dve.wait_ge(s_sc[g], s + 1)
                    ch(v.tensor_reduce(mx[:, g, :], a3, AX.X, ALU.max))
                    v.tensor_tensor(a3, a3, bc(mx[:, g, :].rearrange("p (h a) -> p h a", a=1), [G, H, T]),
                                    ALU.subtract).then_inc(s_sh[g], 1)

            def back(s):
                for g in range(2):
                    dve.wait_ge(s_p[g], s + 1)
                    ch(v.tensor_reduce(rsum[:, g, :], pb[:, g, :].rearrange("p (h i t) -> p h i t", h=H, i=IPG)[:, :, 0, :],
                                       AX.X, ALU.add))
                    ch(v.reciprocal(rinv[:, g, :], rsum[:, g, :]))
                for g in range(2):
                    dve.wait_ge(s_ptp[g], s + 1)
                    v.tensor_tensor(pT[:, g, :].rearrange("p (h t) -> p h t", h=H), heads(2 + 2 * g, G),
                                    bc(block[:, :].rearrange("p (a t) -> p a t", a=1), [G, H, G]),
                                    ALU.mult).then_inc(s_pt[g], 1)
                for g in range(2):
                    dve.wait_ge(s_op[g], s + 1)
                    v.tensor_tensor(o_sb[:, g, :].rearrange("p (h t) -> p h t", h=H), heads((6, 2)[g], V),
                                    bc(rinv[:, g, :].rearrange("p (h a) -> p h a", a=1), [G, H, V]),
                                    ALU.mult).then_inc(s_o[g], 1)
                for g in range(2):
                    dve.wait_ge(s_wop[g], s + 1)
                    v.tensor_tensor(h_all[:, 2 * s + g, :], h_all[:, 2 * s + g, :], PS[0:G, g, 0:D],
                                    ALU.add).then_inc(s_h1[g], 1)
                    dve.drain()
                    ch(v.bn_stats(st2[:, :], h_all[:, 2 * s + g, :]))
                    ch(v.bn_aggr(mv2[:, g, :], st2[:, :]))
                    v.tensor_scalar(ve2[:, g:g + 1], mv2[:, g, 1:2], EPS, None, ALU.add).then_inc(s_vb[g], 1)
                for g in range(2):
                    dve.wait_ge(s_rb[g], s + 1)
                    if g == 0:
                        if not is_step(s, 0):
                            for c in s_xrc:
                                dve.wait_ge(c, s)
                    v.tensor_scalar(xn2[:, g, :], h_all[:, 2 * s + g, :], mv2[:, g, 0:1], rs2[:, g:g + 1],
                                    ALU.subtract, ALU.mult).then_inc(s_xr[g], 1)

            def logits(s):
                dve.wait_ge(s_lp, s + 1)
                v.tensor_copy(logit[:, bass.ds(2 * s, 2), :],
                              PS[0:G, 3, 0:2 * E].rearrange("p (g e) -> p g e", g=2)).then_inc(s_l, 1)

            dve.wait_ge(s_h, 32)
            ln1(0)
            keys(0)
            dve.wait_ge(s_h, 64)
            ln1(1)
            softmax(0)

            def step(s):
                keys(s)
                back(s - 1)
                ln1(s + 1)
                softmax(s)
                logits(s - 1)

            step(1)
            with dve.Fori(2, STEPS) as s:
                step(s)
            back(STEPS - 1)
            logits(STEPS - 1)

            dve.wait_ge(s_l, STEPS)
            dve.wait_ge(s_aw, 16 * N_AW)
            io = bc(iota8[:, 0:1, :], [G, NG, E])
            io8 = bc(iota8[:, 1:2, :], [G, NG, E])
            col = lambda a: bc(a.rearrange("p (g a) -> p g a", a=1), [G, NG, E])
            src = logit[:, :, :]
            for k, (m, ii) in enumerate(((m1, i1), (m2, i2))):
                ch(v.tensor_reduce(m[:, :], src, AX.X, ALU.max))
                ch(v.tensor_tensor(tmp8[:, :, :], src, col(m[:, :]), ALU.is_equal))
                ch(v.scalar_tensor_tensor(tmp8[:, :, :], tmp8[:, :, :], -8.0, io8, ALU.mult, ALU.add))
                ch(v.tensor_reduce(ii[:, :], tmp8[:, :, :], AX.X, ALU.min))
                ch(v.tensor_tensor(oh[:, k], io, col(ii[:, :]), ALU.is_equal))
                if k == 0:
                    ch(v.scalar_tensor_tensor(l2[:, :, :], oh[:, 0], -1.0e30, src, ALU.mult, ALU.add))
                    src = l2[:, :, :]
            v.tensor_tensor(ex[:, :], m2[:, :], m1[:, :], ALU.subtract).then_inc(s_d, 1)
            for k in range(2):
                ch(v.tensor_tensor(oh[:, k], oh[:, k], col(real[:, :]), ALU.mult))
            ch(v.tensor_tensor(ohb[:, :, :], oh[:, 0], oh[:, 1], ALU.add))
            dve.wait_ge(s_e, 1)
            ch(v.tensor_scalar(w01[:, 0, :], ex[:, :], 1.0, None, ALU.add))
            ch(v.reciprocal(w01[:, 0, :], w01[:, 0, :]))
            ch(v.tensor_tensor(w01[:, 1, :], w01[:, 0, :], ex[:, :], ALU.mult))
            v.tensor_tensor(prio[:, :], w01[:, 0, :], real[:, :], ALU.mult).then_inc(s_prio, 1)
            v.tensor_copy(xr_all[:, :, D], w01[:, 0, :])
            v.tensor_copy(xr_all[:, :, D + 1], w01[:, 1, :])
            v.tensor_copy(xr_all[:, :, D + 2], i1[:, :])
            v.tensor_copy(xr_all[:, :, D + 3], tok[:, :])
            dve.wait_ge(s_prio, 1)
            for b_ in range(-(-NG // 4)):
                dve.wait_ge(s_pbp, b_ + 1)
                n = min(4, NG - 4 * b_) * G
                last = v.tensor_copy(prow[:, b_ * 4 * G:b_ * 4 * G + n], PS[0:G, b_, 0:n])
            last.then_inc(s_pb, 1)
            dve.wait_ge(s_pb, 1)
            v.memset(xe[:, :, :, :], 0.0)

            for i in range(NG):
                if i >= 2:
                    dve.wait_ge(s_cnt, i - 1)
                pi = prio[:, i:i + 1]
                a, b_ = i * G, (i + 1) * G
                if a:
                    v.tensor_scalar(before[:, i % 2, 0:a], prow[:, 0:a], pi, None, ALU.is_lt)
                if b_ < ROWS:
                    v.tensor_scalar(before[:, i % 2, b_:ROWS], prow[:, b_:ROWS], pi, None, ALU.is_le)
                ch(v.scalar_tensor_tensor(diag[:, :], prow[:, a:b_], pi, upper[:, :], ALU.is_equal, ALU.mult))
                v.scalar_tensor_tensor(before[:, i % 2, a:b_], prow[:, a:b_], pi, diag[:, :], ALU.is_lt,
                                       ALU.add).then_inc(s_bef, 1)
                dve.wait_ge(s_bef, i + 1)
            dve.wait_ge(s_cnt, NG)
            ch(v.tensor_copy(rank[:, :, :], PS[0:G, 7, 0:NG * E].rearrange("p (g e) -> p g e", e=E)))
            for k, ii in enumerate((i1, i2)):
                ch(v.tensor_tensor(tmp8[:, :, :], oh[:, k], rank[:, :, :], ALU.mult))
                ch(v.tensor_reduce(posk[:, k, :], tmp8[:, :, :], AX.X, ALU.add))
                ch(v.scalar_tensor_tensor(keep[:, k, :], posk[:, k, :], float(CAP), real[:, :], ALU.is_lt, ALU.mult))
                ch(v.scalar_tensor_tensor(slot[:, k, :], ii[:, :], float(CAP), posk[:, k, :], ALU.mult, ALU.add))
                ch(v.tensor_scalar(slot[:, k, :], slot[:, k, :], BIG, None, ALU.add))
                ch(v.scalar_tensor_tensor(slot[:, k, :], keep[:, k, :], -BIG, slot[:, k, :], ALU.mult, ALU.add))
            v.tensor_copy(sloti[:, :, :], slot[:, :, :]).then_inc(s_slot, 1)

            def expert(e, p, i):
                dve.wait_ge(s_xep, e + 1)
                for k in range(2):
                    last = v.tensor_copy(xeT[:, k, 0:512], PS[0:KD, 2 * k, 0:512])
                last.then_inc(s_xed, 1)
                t = lambda n: xe[:, p, :, D + n]
                ch(v.tensor_scalar(first[:, p, :], t(2), eidx[:, bass.ds(e, 1)], None, ALU.is_equal))
                ch(v.tensor_tensor(wtmp[:, p, :], first[:, p, :], t(0), ALU.mult))
                ch(v.tensor_scalar(first[:, p, :], first[:, p, :], -1.0, 1.0, ALU.mult, ALU.add))
                ch(v.tensor_tensor(wsel[:, p, :], first[:, p, :], t(1), ALU.mult))
                ch(v.tensor_tensor(wsel[:, p, :], wsel[:, p, :], wtmp[:, p, :], ALU.add))
                ch(v.scalar_tensor_tensor(dst[:, p, :], first[:, p, :], float(ROWS), t(3), ALU.mult, ALU.add))
                dve.wait_ge(s_ys[p], i * (16 * NT)) if not isinstance(i, int) or i else None
                v.tensor_copy(dsti[:, p, :], dst[:, p, :]).then_inc(s_di, 1)
                for n in range(NT):
                    dve.wait_ge(s_yp, e * NT + n + 1)
                    r = tile_rows(n)
                    v.tensor_scalar(ye[0:r, p, n, :], PS[0:r, 4 + n % 4, 0:D], wsel[0:r, p, n:n + 1], None,
                                    ALU.mult).then_inc(s_ye, 1)

            dve.wait_ge(s_slot, 1)
            for p in range(2):
                expert(p, p, 0)
            with dve.Fori(1, E // 2) as i:
                for p in range(2):
                    expert(i * 2 + p, p, i)

            def total(s, p, i):
                dve.wait_ge(s_yl[p], i * 64 + 64)
                ch(v.tensor_tensor(ycat[:, p, 0], ycat[:, p, 0], ycat[:, p, 1], ALU.add))
                if not isinstance(i, int) or i:
                    dve.wait_ge(s_out[p], i * 64)
                v.tensor_tensor(res[:, p], ycat[:, p, 0], h_all[:, bass.ds(2 * s, 2), :], ALU.add).then_inc(s_sum, 1)

            for p in range(2):
                total(p, p, 0)
            with dve.Fori(1, (STEPS - 1) // 2) as i:
                for p in range(2):
                    total(i * 2 + p, p, i)
            total(STEPS - 1, 0, (STEPS - 1) // 2)

        @blk.gpsimd
        def _(pool):
            p_ = nc.gpsimd

            def rsqrt(o, i):
                return p_.tensor_tensor(o, i, nhalf[0:i.shape[0], 0:i.shape[1]], ALU.pow)

            pool.wait_ge(s_setv, 1)
            for j in range(NH // 2):
                pool.wait_ge(s_v1, j + 1)
                rsqrt(rs1[:, :], ve1[:, :]).then_inc(s_r1, 1)
                pool.wait_ge(s_v2, j + 1)
                rsqrt(rs1[:, :], ve1[:, :]).then_inc(s_r2, 1)

            def ln1(s):
                pool.wait_ge(s_va, s + 1)
                rsqrt(rs[:, :], ve[:, :]).then_inc(s_ra, 1)

            def ln2(s):
                for g in range(2):
                    pool.wait_ge(s_vb[g], s + 1)
                    rsqrt(rs2[:, g:g + 1], ve2[:, g:g + 1]).then_inc(s_rb[g], 1)
                for g in range(2):
                    pool.wait_ge(s_xr[g], s + 1)
                    p_.tensor_copy(xr_all[:, 2 * s + g, 0:D], xn2[:, g, :]).then_inc(s_xrc[g], 1)

            ln1(0)
            ln1(1)
            with pool.Fori(1, STEPS) as s:
                ln2(s - 1)
                ln1(s + 1)
            ln2(STEPS - 1)

            for c in s_xrc:
                pool.wait_ge(c, STEPS)
            pool.wait_ge(s_slot, 1)
            pool.wait_ge(s_fill, 16 * N_FILL)
            for k in range(2):
                for g in range(NG):
                    p_.indirect_dma_start(xbuf, bass.IndirectOffsetOnAxis(ap=sloti[:, k, g:g + 1], axis=0),
                                          xr_all[:, g, :], None, bounds_check=E * CAP - 1,
                                          oob_is_err=False).then_inc(s_sct, 16)

            def expert(e, p):
                pool.wait_ge(s_di, e + 1)
                for n in range(NT):
                    r = tile_rows(n)
                    pool.wait_ge(s_ye, e * NT + n + 1)
                    p_.indirect_dma_start(ybuf, bass.IndirectOffsetOnAxis(ap=dsti[0:r, p, n:n + 1], axis=0),
                                          ye[0:r, p, n, :], None, bounds_check=2 * ROWS - 1,
                                          oob_is_err=False).then_inc(s_ys[p], 16)

            for e in range(E):
                expert(e, e % 2)


_INS = ["x", "L0_tok_ln1_g", "L0_tok_ln1_b", "L0_tok_W_lin", "L0_tok_b_lin", "L0_tok_ln2_g", "L0_tok_ln2_b",
        "L0_tok_pos_embedding", "L0_tok_cls_token", "L0_attn_Wq", "L0_attn_Wk", "L0_attn_Wv", "L0_attn_Wrk",
        "L0_attn_r_w_bias", "L0_attn_r_r_bias", "L0_attn_Wo", "L0_attn_bo", "L0_ffn_Wg", "L0_ffn_W1", "L0_ffn_b1",
        "L0_ffn_W2", "L0_ffn_b2"]


def constants():
    f = np.float32
    r = np.arange(G)
    block = (r[:, None] // T == r[None, :] // T).astype(f)
    ind = (r[:, None] // T == np.arange(IPG)[None, :]).astype(f)
    positions = np.arange(-T + 1, T).astype(f)
    nb = F // 2
    widths = np.exp(np.log(T + 1) / nb).astype(f) ** np.arange(1, nb + 1).astype(f) - f(1)
    emb = (widths[None, :] > np.abs(positions)[:, None]).astype(f)
    pos = np.concatenate([emb, np.sign(positions)[:, None] * emb], axis=-1)
    iota = np.stack([np.arange(E), np.arange(E) + E]).astype(f)
    tok = (np.arange(NG)[None, :] * G + r[:, None]).astype(f)
    blank = np.zeros((128, XW), f)
    blank[:, XW - 1] = BIG
    return {
        "c_ident": np.eye(128, dtype=f), "c_block": block, "c_ind": ind, "c_pos": np.ascontiguousarray(pos.T),
        "c_iota": np.ascontiguousarray(np.broadcast_to(iota, (128, 2, E))),
        "c_upper": (r[None, :] > r[:, None]).astype(f), "c_real": (tok < B * T).astype(f), "c_tok": tok,
        "c_blank": blank,
    }


def kernel(**inputs):
    import concourse.bacc as bacc
    from concourse.bass_utils import run_bass_kernel_spmd

    nc = bacc.Bacc("TRN2", target_bir_lowering=False, num_devices=1)
    arrays, args = {}, []
    feed = [(n, np.ascontiguousarray(inputs[n])) for n in _INS] + list(constants().items())
    for name, a in feed:
        if name in ("L0_attn_r_w_bias", "L0_attn_r_r_bias"):
            a = np.ascontiguousarray(a.reshape(HB, 128).T)
        elif name == "L0_attn_Wo":
            a = np.ascontiguousarray(a.reshape(H, V, D)[[head_at(j) for j in range(H)]].reshape(H * V, D))
        elif name in ("L0_tok_ln1_g", "L0_tok_ln1_b"):
            a = np.ascontiguousarray(a.reshape(PC, 128).T)
        elif name == "x":
            a = a.reshape(B, C, NH, PATCH, NH, PATCH).transpose(2, 0, 4, 3, 5, 1)
            a = np.ascontiguousarray(a.reshape(NH, B, NH * PD))
        elif name == "L0_ffn_b1":
            a = np.ascontiguousarray(a.reshape(E, HC, 128).transpose(0, 2, 1))
        arrays[name] = a
        args.append(nc.dram_tensor(name, a.shape, mybir.dt.from_np(a.dtype), kind="ExternalInput").ap())
    args.append(nc.dram_tensor("out", (B * T, D), F32, kind="ExternalOutput").ap())
    build(nc, *args)
    r = run_bass_kernel_spmd(nc, [arrays], core_ids=[0])
    return r.results[0]["out"].reshape(B, T, D)
```

```python
from contextlib import ExitStack

import numpy as np

import concourse.bass as bass
from concourse import mybir

F32 = mybir.dt.float32
BF16 = mybir.dt.bfloat16
F32R = mybir.dt.float32r
I32 = mybir.dt.int32
ALU = mybir.AluOpType
ACT = mybir.ActivationFunctionType
AX = mybir.AxisListType

B, C, IMG, PATCH = 64, 3, 96, 16
NH = IMG // PATCH
D = 192
T = NH * NH + 1
H, K, V, F = 8, 64, 96, 32
R = 2 * T - 1
E, HID = 8, 4 * D
CAP = int(1.25 * B * T * 2 / E)
EPS = 1e-5

IPG = 3
G = IPG * T
NG = -(-B // IPG)
STEPS = NG // 2
ROWS = NG * G
LAST = B * T - (NG - 1) * G
G2 = 2 * G
KD = D // 2
HB = H // 2
WIDE = 640
SKEW = WIDE - 1
REL_IMG = T * SKEW
SPLIT = 96
PD = C * PATCH * PATCH
PC = PD // 128
XF = NH * PD
ZR = 4
TAIL = 4
XW = D + TAIL
NT = -(-CAP // 128)
HALF = CAP // 2
HC = HID // 128
NQKV = 2 * H * K + H * V
HIGH_BY_DVE = (1, 3)
NARROW_FREE = 3 * HID + HC * D
N_EARLY, N_CONST, N_QKV, N_AW = 5, 18, 12, 7
UNITS = NH * NH // 2
N_FILL = 2 + -(-(2 * ROWS // ZR) // 128) + (2 * ROWS % ZR > 0)
RT = 8
RANKED = [0, 1, 2, 7, 3, 8, 4, 9, 5, 10, 6]
SLOTS_AFTER = {2: 0, 4: 1, 6: 2, 8: 3, 9: 4, 10: 5, 11: 6, 12: 7, 13: 8}
HALF_ULP = 2.0 ** -25
BIG = 1.0e6
assert NG % 2 == 0 and 36 * WIDE + H * R <= REL_IMG


BLOCKS = ((0, 0), (0, 1), (0, 2), (1, 0), (1, 1))


def head_at(j):
    return j % HB * 2 + j // HB


def is_step(s, n):
    return isinstance(s, int) and s == n


def tile_rows(i):
    return min(128, CAP - 128 * i)


def build(nc, x, ln1_g, ln1_b, W_lin, b_lin, ln2_g, ln2_b, pos_embedding, cls_token,
          Wq, Wk, Wv, Wrk, r_w_bias, r_r_bias, Wo, bo, Wg, W1, b1, W2, b2,
          c_ident, c_block, c_ind, c_pos, c_iota, c_upper, c_real, c_tok, c_blank, out):
    h_dram = nc.dram_tensor("h_tokens", [ROWS, D], F32).ap()
    rel_dram = nc.dram_tensor("rel_scores", [NG * IPG * REL_IMG + WIDE], F32).ap()
    xbuf = nc.dram_tensor("routed_rows", [E * CAP, XW], F32).ap()
    ybuf = nc.dram_tensor("expert_out", [2 * ROWS, D], F32).ap()

    with ExitStack() as ctx:
        def sb(name, shape, dt=F32):
            return ctx.enter_context(nc.sbuf_tensor(name, shape, dt))

        phase = ctx.enter_context(ExitStack())

        def early(name, shape, dt=F32):
            return phase.enter_context(nc.sbuf_tensor(name, shape, dt))

        def sem(name):
            return ctx.enter_context(nc.semaphore(name))

        PS = ctx.enter_context(nc.psum_tensor("PS", [128, 8, 512], F32))

        ident = sb("ident", [128, 128])
        eidx = sb("eidx", [128, E])
        h_all = sb("h_all", [G, NG + 2, D])
        b1s = sb("b1s", [128, 2, HC])
        b2s = sb("b2s", [128, 2, D])
        first = sb("first", [128, 2, NT])
        wsel = sb("wsel", [128, 2, NT])
        wtmp = sb("wtmp", [128, 2, NT])
        dst = sb("dst", [128, 2, NT])
        dsti = sb("dsti", [128, 2, NT], I32)

        narrow = early("narrow", [128, 60 * D])
        wide = early("wide", [128, (NH // 2) * XF])

        block = early("block", [G, G])
        ind = early("ind", [G, IPG])
        pos_f = early("pos_f", [F, R])
        iota8 = early("iota8", [G, 2, E])
        upper = early("upper", [G, G])
        real = early("real", [G, NG])
        tok = early("tok", [G, NG])
        blank = early("blank", [128, XW])
        ones = early("ones", [128, 128])
        zeros = early("zeros", [128, ZR * D])
        meanw = early("meanw", [128, 128])
        g1 = early("g1", [128, PC])
        bb1 = early("bb1", [128, PC])
        blin = early("blin", [1, D])
        cB = early("cB", [128, D])
        g2B = early("g2B", [128, D])
        b2B = early("b2B", [128, D])
        wh = early("wh", [128, 3, NQKV], F32R)
        wl = early("wl", [128, 2, NQKV], F32R)
        xT = early("xT", [128, 3, G2], F32R)
        wrk = early("wrk", [F, H * K])
        rk = early("rk", [128, HB, R])
        rwb = early("rwb", [128, HB])
        rrb = early("rrb", [128, HB])
        wo = early("wo", [128, HC, D])
        boB = early("boB", [G, D])
        wg = early("wg", [KD, 2, E])

        def carve(memory):
            at = [0]

            def piece(parts, n, dt=F32):
                words = n if dt is F32 else n // 2
                a, at[0] = at[0], at[0] + words
                assert at[0] <= memory.shape[1]
                v = memory[0:parts, a:a + words]
                return v if dt is F32 else v.bitcast(dt)
            return piece

        xv = wide[:, :].rearrange("p (j w f) -> p j w f", j=NH // 2, w=NH)
        piece = carve(wide)
        wraw = piece(128, 3 * NQKV).rearrange("p (b n) -> p b n", b=3)
        piece = carve(wide)
        qw = piece(128, HB * G2).rearrange("p (m n) -> p m n", m=HB)
        qr = piece(128, HB * G2).rearrange("p (m n) -> p m n", m=HB)
        kT = piece(128, HB * G2).rearrange("p (m n) -> p m n", m=HB)
        v_sb = piece(G, 2 * H * V).rearrange("p (g n) -> p g n", g=2)
        rel = piece(G, 2 * H * R).rearrange("p (g n) -> p g n", g=2)
        relw = piece(G, 2 * H * T).rearrange("p (g n) -> p g n", g=2)
        sc = piece(G, 2 * H * T).rearrange("p (g n) -> p g n", g=2)
        pb = piece(G, 2 * H * G).rearrange("p (g n) -> p g n", g=2)
        pT = piece(G, 2 * H * G).rearrange("p (g n) -> p g n", g=2)
        o_sb = piece(G, 2 * H * V).rearrange("p (g n) -> p g n", g=2)
        oT = piece(128, 2 * HC * G).rearrange("p (g n) -> p g n", g=2)
        piece = carve(wide)
        prow = piece(G, ROWS)
        sgn = piece(G, RT * ROWS, BF16).rearrange("p (j i n) -> p j i n", j=RT, i=NG)

        piece = carve(narrow)
        W_raw = piece(128, PC * D).rearrange("p (c d) -> p c d", c=PC)
        W_cen = piece(128, PC * D).rearrange("p (c d) -> p c d", c=PC)
        posB = piece(128, NH * NH // 2 * D).rearrange("p (j n) -> p j n", j=NH // 2)
        xTt = piece(128, 2 * 6 * 128).rearrange("p (a c n) -> p a c n", a=2, c=6)
        zt = piece(128, UNITS * D).rearrange("p (j w d) -> p j w d", j=NH // 2, w=NH)
        clsB = piece(64, 2 * D).rearrange("p (a d) -> p a d", a=2)
        clsP = piece(64, D)
        piece = carve(narrow)
        piece(G, NARROW_FREE)
        nudged = piece(G, ROWS).rearrange("p (j n) -> p j n", j=NG)
        own = piece(G, ROWS, BF16).rearrange("p (j n) -> p j n", j=NG)
        before = [piece(G, ROWS, BF16).rearrange("p (i n) -> p i n", i=NG) for _ in range(2)]

        bn1 = early("bn1", [128, NH // 2, NH, 2, 6])
        mv1 = early("mv1", [128, NH // 2, NH, 2])
        ve1 = early("ve1", [128, NH // 2, NH])
        rs1 = early("rs1", [128, NH // 2, NH])
        bnt = early("bnt", [128, NH // 2, NH, 6])
        mvt = early("mvt", [128, NH // 2, NH, 2])
        vet = early("vet", [128, NH // 2, NH])
        rst = early("rst", [128, NH // 2, NH])
        nhalf = early("nhalf", [128, NH])
        xr_all = early("xr_all", [G, NG, XW])
        xn = early("xn", [G, 2, D])
        xn2 = early("xn2", [G, 2, D])
        xnT = early("xnT", [KD, 2, G2])
        st = early("st", [G, 6])
        mv = early("mv", [G, 2, 2])
        ve = early("ve", [G, 2])
        rs = early("rs", [G, 2])
        st2 = early("st2", [G, 6])
        mv2 = early("mv2", [G, 2, 2])
        ve2 = early("ve2", [G, 2])
        rs2 = early("rs2", [G, 2])
        mx = early("mx", [G, 2, H])
        rsum = early("rsum", [G, 2, H])
        rinv = early("rinv", [G, 2, H])
        logit = early("logit", [G, NG, E])

        m1 = early("m1", [G, NG])
        m2 = early("m2", [G, NG])
        i1 = early("i1", [G, NG])
        i2 = early("i2", [G, NG])
        oh = early("oh", [G, 2, NG, E])
        ohb = early("ohb", [G, NG, E], BF16)
        tmp8 = early("tmp8", [G, NG, E])
        l2 = early("l2", [G, NG, E])
        ex = early("ex", [G, NG])
        w01 = early("w01", [G, 2, NG])
        prio = early("prio", [G, NG])
        prio_up = early("prio_up", [G, NG])
        prio_dn = early("prio_dn", [G, NG])
        lower_by = early("lower_by", [G, G])
        ohh = early("ohh", [G, NG, E], BF16)
        ohn = early("ohn", [G, NG, E], BF16)
        ohs = early("ohs", [G, E])
        ohsb = early("ohsb", [G, E], BF16)
        onesb = early("onesb", [G, G], BF16)
        base = early("base", [G, 2, NG])
        tmp4 = early("tmp4", [G, 2, 2, E])
        posk = early("posk", [G, 2, NG])
        keep = early("keep", [G, 2, NG])
        slot = early("slot", [G, 2, NG])
        sloti = early("sloti", [G, 2, NG], I32)


        phase.close()
        w1r = sb("w1r", [128, 3, HID])
        w2r = sb("w2r", [128, HC, D])
        xe = sb("xe", [128, 2, NT, XW])
        w1h = sb("w1h", [128, 3, HID], F32R)
        w1l = sb("w1l", [128, 2, HID], F32R)
        w2h = sb("w2h", [128, HC, D], F32R)
        w2l = sb("w2l", [128, HC, D], F32R)
        xeT = sb("xeT", [128, 3, CAP], F32R)
        hTh = sb("hTh", [128, HC, CAP], F32R)
        hTl = sb("hTl", [128, HC, CAP], F32R)
        hf = sb("hf", [128, 2, CAP])
        ye = sb("ye", [128, 2, NT, D])
        wb2 = sb("wb2", [128, 2, NT, D])
        ycat = sb("ycat", [G, 2, 2, 2, D])
        res = sb("res", [G, 2, 2, D])

        s_const = sem("const_loaded")
        s_early = sem("tok_weights_loaded")
        s_x = [[sem(f"x_loaded{j}_{f}") for f in range(2)] for j in range(NH // 2)]
        s_aw = sem("attn_weights_loaded")
        s_set = sem("memsets_done")
        s_setv = sem("dve_consts_done")
        s_gw = sem("gw_done")
        s_mean = sem("colmean_psum")
        s_rkp = sem("rk_psum")
        s_wc = sem("w_centred")
        s_rk = sem("rk_ready")
        s_xrc = [sem(f"routed_rows_copied{g}") for g in range(2)]
        s_cls = sem("cls_ready")
        s_tT = sem("tok_transposed")
        s_tTa = sem("tok_evac_act")
        s_tz = sem("tok_product")
        s_tze = sem("tok_product_used")
        s_v1 = sem("tok_var1")
        s_r1 = sem("tok_rstd1")
        s_v2 = sem("tok_var2")
        s_r2 = sem("tok_rstd2")
        s_tn = sem("tok_normed")
        s_pos = sem("positions_ready")
        s_hb = sem("h_with_bias")
        s_wsel = sem("routing_weights_ready")
        s_wb = sem("weighted_bias_ready")
        s_ht = sem("tok_rows_ready")
        s_ho = [sem(f"tok_rows_stored{j}") for j in range(NH // 2)]
        s_fill = sem("dram_prefilled")
        s_h = sem("h_loaded")
        s_va = sem("ln1_var")
        s_ra = sem("ln1_rstd")
        s_xn = sem("ln1_rows")
        s_xTp = sem("xT_psum")
        s_xTh = sem("xT_high")
        s_xT = sem("xT_ready")
        s_qkv = sem("qkv_weights_loaded")
        s_wh = sem("qkv_weights_high")
        s_wl = sem("qkv_weights_low")
        s_qp = sem("q_psum")
        s_kp = sem("k_psum")
        s_q = sem("q_ready")
        s_k = sem("k_ready")
        s_rp = [sem(f"rel_psum{g}") for g in range(2)]
        s_re = [sem(f"rel_evacuated{g}") for g in range(2)]
        s_ro = [sem(f"rel_stored{g}") for g in range(2)]
        s_ri = [sem(f"rel_skewed{g}") for g in range(2)]
        s_vp = [sem(f"v_psum{g}") for g in range(2)]
        s_v = [sem(f"v_ready{g}") for g in range(2)]
        s_sp = [sem(f"scores_psum{g}") for g in range(2)]
        s_sc = [sem(f"scores_compact{g}") for g in range(2)]
        s_sh = [sem(f"scores_shifted{g}") for g in range(2)]
        s_p = [sem(f"probs_ready{g}") for g in range(2)]
        s_ptp = [sem(f"pT_psum{g}") for g in range(2)]
        s_pt = [sem(f"pT_ready{g}") for g in range(2)]
        s_op = [sem(f"o_psum{g}") for g in range(2)]
        s_o = [sem(f"o_ready{g}") for g in range(2)]
        s_otp = [sem(f"oT_psum{g}") for g in range(2)]
        s_ot = [sem(f"oT_ready{g}") for g in range(2)]
        s_wop = [sem(f"proj_psum{g}") for g in range(2)]
        s_h1 = [sem(f"h1_ready{g}") for g in range(2)]
        s_vb = [sem(f"ln2_var{g}") for g in range(2)]
        s_rb = [sem(f"ln2_rstd{g}") for g in range(2)]
        s_xr = [sem(f"ln2_rows{g}") for g in range(2)]
        s_xrp = sem("xnT_psum")
        s_xrT = sem("xnT_ready")
        s_lp = sem("logits_psum")
        s_l = sem("logits_ready")
        s_d = sem("gap_ready")
        s_e = sem("gap_exp")
        s_prio = sem("prio_ready")
        s_pbp = sem("prio_rows_psum")
        s_pb = sem("prio_rows_ready")
        s_bef = sem("before_ready")
        s_cnt = sem("before_counted")
        s_nudge = sem("nudged_prios_ready")
        s_sgn = sem("signs_ready")
        s_own = sem("own_tiles_ready")
        s_pba = sem("prio_rows_ready_act")
        s_xe0 = sem("expert_rows_cleared")
        s_slot = sem("slots_ready")
        s_sct = sem("rows_scattered")
        s_ex = [sem(f"expert_rows_loaded{p}") for p in range(2)]
        s_eb = [sem(f"expert_biases_loaded{p}") for p in range(2)]
        s_w1r = sem("w1_loaded")
        s_w2r = sem("w2_loaded")
        s_w1h = sem("w1_high")
        s_w1l = sem("w1_low")
        s_w2h = sem("w2_high")
        s_w2l = sem("w2_low")
        s_xep = sem("xeT_psum")
        s_xeh = sem("xeT_high")
        s_xel = sem("xeT_low")
        s_hp = sem("hidden_psum")
        s_hg = sem("hidden_ready")
        s_hl = sem("hidden_low_ready")
        s_yp = sem("y_psum")
        s_ye = sem("y_scaled")
        s_di = sem("dest_ready")
        s_zw = sem("w1_low_zeros")
        s_ys = [sem(f"y_scattered{p}") for p in range(2)]
        s_yl = [sem(f"y_loaded{p}") for p in range(2)]
        s_sum = sem("sum_ready")
        s_out = [sem(f"out_stored{p}") for p in range(2)]

        def bc(ap, shape):
            return ap.to_broadcast(shape)

        def heads(bank, n):
            return PS[0:G, bank:bank + 2, :].rearrange("p a (h t) -> p (a h) t", h=HB)[:, :, 0:n]

        def hidden_bank(c):
            return 2 + 2 * (c % 3)

        def both_banks(bank):
            return PS[:, bank:bank + 2, :].rearrange("p a n -> p (a n)")[:, 0:CAP]

        blk = ctx.enter_context(nc.Block())

        @blk.sync
        def _(sp):
            def load_x(j):
                for f in range(2):
                    for u in range(2):
                        sp.dma_start(wide[64 * u:64 * u + 64, j * XF + f * (XF // 2):j * XF + (f + 1) * (XF // 2)],
                                     x[2 * j + u][:, f * (XF // 2):(f + 1) * (XF // 2)]).then_inc(s_x[j][f], 16)

            sp.dma_start(W_raw[:, :, :], W_lin.rearrange("(c p) d -> p c d", p=128)).then_inc(s_early, 16)
            sp.dma_start(g1[:, :], ln1_g).then_inc(s_early, 16)
            sp.dma_start(bb1[:, :], ln1_b).then_inc(s_early, 16)
            row = lambda ap: ap.rearrange("(a d) -> a d", a=1)
            sp.dma_start(blin[:, :], row(b_lin)).then_inc(s_early, 16)
            sp.dma_start(ident[:, :], c_ident).then_inc(s_early, 16)
            load_x(0)
            load_x(1)
            sp.dma_start(block[:, :], c_block).then_inc(s_const, 16)
            sp.dma_start(ind[:, :], c_ind).then_inc(s_const, 16)
            sp.dma_start(pos_f[:, :], c_pos).then_inc(s_const, 16)
            sp.dma_start(iota8[:, :, :], c_iota[0:G]).then_inc(s_const, 16)
            sp.dma_start(eidx[:, :], c_iota[:, 0, :]).then_inc(s_const, 16)
            sp.dma_start(upper[:, :], c_upper).then_inc(s_const, 16)
            sp.dma_start(real[:, :], c_real).then_inc(s_const, 16)
            sp.dma_start(blank[:, :], c_blank).then_inc(s_const, 16)
            sp.dma_start(g2B[:, :], bc(row(ln2_g), [128, D])).then_inc(s_const, 16)
            sp.dma_start(b2B[:, :], bc(row(ln2_b), [128, D])).then_inc(s_const, 16)
            for n in range(NH):
                src = pos_embedding[0, 1 + n * NH:1 + (n + 1) * NH, :].rearrange("(a t) d -> a (t d)", a=1)
                sp.dma_start(posB[64 * (n % 2):64 * (n % 2) + 64, n // 2, :],
                             bc(src, [64, NH * D])).then_inc(s_const, 16)
            sp.dma_start(clsB[:, 0, :], bc(cls_token[0], [64, D])).then_inc(s_const, 16)
            sp.dma_start(clsB[:, 1, :], bc(pos_embedding[0, 0:1, :], [64, D])).then_inc(s_const, 16)
            load_x(2)
            sp.dma_start(wrk[:, :], Wrk).then_inc(s_aw, 16)
            sp.dma_start(rwb[:, :], r_w_bias).then_inc(s_aw, 16)
            sp.dma_start(rrb[:, :], r_r_bias).then_inc(s_aw, 16)
            sp.dma_start(wo[:, :, :], Wo.rearrange("(c p) d -> p c d", p=128)).then_inc(s_aw, 16)
            sp.dma_start(boB[:, :], bc(row(bo), [G, D])).then_inc(s_aw, 16)
            sp.dma_start(wg[:, :, :], Wg.rearrange("(k p) n -> p k n", k=2)).then_inc(s_aw, 16)
            sp.dma_start(tok[:, :], c_tok).then_inc(s_aw, 16)

            sp.wait_ge(s_set, 1)
            sp.wait_ge(s_const, 16 * N_CONST)
            n0 = E * CAP // 128 * 128
            sp.dma_start(xbuf[0:n0].rearrange("(p n) w -> p n w", p=128),
                         bc(blank[:, :].rearrange("p (a w) -> p a w", a=1), [128, n0 // 128, XW])).then_inc(s_fill, 16)
            sp.dma_start(xbuf[n0:E * CAP], blank[0:E * CAP - n0, :]).then_inc(s_fill, 16)
            nz = 2 * ROWS // ZR
            for a in range(0, nz, 128):
                n = min(128, nz - a)
                sp.dma_start(ybuf[a * ZR:(a + n) * ZR].rearrange("(n r) d -> n (r d)", r=ZR),
                             zeros[0:n, :]).then_inc(s_fill, 16)
            if 2 * ROWS % ZR:
                sp.dma_start(ybuf[nz * ZR:2 * ROWS], zeros[0:2 * ROWS % ZR, 0:D]).then_inc(s_fill, 16)

            hv = h_dram[0:B * T, :].rearrange("(b t) d -> b t d", t=T)
            for j in range(NH // 2):
                sp.wait_ge(s_ht, j + 1)
                for u in range(2):
                    n = 2 * j + u
                    sp.dma_start(hv[:, 1 + n * NH:1 + (n + 1) * NH, :].rearrange("b t d -> b (t d)"),
                                 zt[64 * u:64 * u + 64, j].rearrange("p t d -> p (t d)")).then_inc(s_ho[j], 16)
                if j == 0:
                    sp.wait_ge(s_cls, 1)
                    sp.dma_start(hv[:, 0, :], clsP[:, :]).then_inc(s_ho[0], 16)
                    sp.dma_start(h_dram[B * T:ROWS, :], zeros[0:ROWS - B * T, 0:D]).then_inc(s_ho[0], 16)
                    sp.wait_ge(s_tT, 3 * NH // 2)
                    sp.wait_ge(s_v1, 2)
                    at = 0
                    for W in (Wq, Wk, Wv):
                        n = W.shape[1]
                        for p0, b_, r0, rows_ in ((0, 0, 0, 128), (0, 1, 0, 64), (64, 1, 128, 64), (0, 2, 64, 128)):
                            sp.dma_start(wraw[p0:p0 + rows_, b_, at:at + n], W[r0:r0 + rows_]).then_inc(s_qkv, 16)
                        at += n
            for j in range(NH // 2):
                sp.wait_ge(s_ho[j], 64 if j == 0 else 32)

            hg = h_dram.rearrange("(g p) d -> p g d", p=G)
            for a, b_ in ((0, 2), (2, NG)):
                sp.dma_start(h_all[0:SPLIT, a:b_], hg[0:SPLIT, a:b_]).then_inc(s_h, 16)
                sp.dma_start(h_all[SPLIT:G, a:b_], hg[SPLIT:G, a:b_]).then_inc(s_h, 16)
                sp.wait_ge(s_h, 32 if a == 0 else 64)

            def rows_of(start, n, pitch):
                return rel_dram[bass.ds(start, n * pitch)].rearrange("(p w) -> p w", w=pitch)[:, 0:H * R]

            def rel_roundtrip(s):
                for g in range(2):
                    base = (2 * s + g) * (IPG * REL_IMG)
                    sp.wait_ge(s_re[g], s + 1)
                    for i in range(IPG):
                        for t0, t1 in ((0, 32), (32, T)):
                            sp.dma_start(rows_of(base + i * REL_IMG + t0 * WIDE, t1 - t0, WIDE),
                                         rel[i * T + t0:i * T + t1, g, :]).then_inc(s_ro[g], 16)
                for g in range(2):
                    base = (2 * s + g) * (IPG * REL_IMG) + T - 1
                    sp.wait_ge(s_ro[g], 16 * 6 * (s + 1))
                    if not isinstance(s, int) or s:
                        sp.wait_ge(s_sc[g], s)
                    for p0, p1 in ((0, SPLIT), (SPLIT, G)):
                        sp.dma_start(relw[p0:p1, g, :].rearrange("p (h t) -> p h t", h=H),
                                     rows_of(base + p0 * SKEW, p1 - p0, SKEW).rearrange(
                                         "p (h r) -> p h r", h=H)[:, :, 0:T]).then_inc(s_ri[g], 16)

            rel_roundtrip(0)
            with sp.Fori(1, STEPS) as s:
                rel_roundtrip(s)

            def load_w1(e):
                w = W1[bass.ds(e, 1)]
                half = w.rearrange("a (c p) n -> p (a c) n", p=64)
                sp.dma_start(w1r[:, 0, :], w.rearrange("a d n -> d (a n)")[0:128]).then_inc(s_w1r, 16)
                sp.dma_start(w1r[0:64, 1, :], half[:, 0, :]).then_inc(s_w1r, 16)
                sp.dma_start(w1r[64:128, 1, :], half[:, 2, :]).then_inc(s_w1r, 16)
                sp.dma_start(w1r[:, 2, :], w.rearrange("a d n -> d (a n)")[64:192]).then_inc(s_w1r, 16)

            def load_w2(e):
                sp.dma_start(w2r[:, :, :], W2[bass.ds(e, 1)].rearrange("a (c p) d -> p (a c) d", p=128)
                             ).then_inc(s_w2r, 16)

            def load_biases(e, p):
                sp.dma_start(b1s[:, p], b1[bass.ds(e, 1)].rearrange("a p c -> p (a c)")).then_inc(s_eb[p], 16)
                sp.dma_start(b2s[:, p], bc(b2[bass.ds(e, 1)], [128, D])).then_inc(s_eb[p], 16)

            def load_rows(e, p):
                full = CAP // 128
                sp.dma_start(xe[:, p, 0:full],
                             xbuf[bass.ds(e * CAP, full * 128)].rearrange("(n q) w -> q n w", q=128)
                             ).then_inc(s_ex[p], 16)
                sp.dma_start(xe[0:CAP - full * 128, p, full],
                             xbuf[bass.ds(e * CAP + full * 128, CAP - full * 128)]).then_inc(s_ex[p], 16)

            load_w1(0)
            load_w2(0)
            for p in range(2):
                load_biases(p, p)
            sp.wait_ge(s_sct, 16 * 2 * NG)
            sp.wait_ge(s_xe0, 1)
            for p in range(2):
                load_rows(p, p)

            def load_next(e, p, more):
                sp.wait_ge(s_w1h, e)
                sp.wait_ge(s_w1l, e)
                load_w1(e)
                sp.wait_ge(s_w2h, e)
                sp.wait_ge(s_w2l, e)
                load_w2(e)
                if more:
                    sp.wait_ge(s_di, e)
                    sp.wait_ge(s_xep, e)
                    load_rows(e + 1, 1 - p)
                    sp.wait_ge(s_hg, e * HC)
                    sp.wait_ge(s_wb, e)
                    load_biases(e + 1, 1 - p)

            load_next(1, 1, True)
            with sp.Fori(1, E // 2 - 1) as i:
                load_next(i * 2, 0, True)
                load_next(i * 2 + 1, 1, True)
            load_next(E - 2, 0, True)
            load_next(E - 1, 1, False)

            yv = ybuf.rearrange("(k g p) d -> p k g d", k=2, p=G)
            for p in range(2):
                sp.wait_ge(s_ys[p], 16 * NT * (E // 2))

            def load_y(s, p):
                for k in range(2):
                    for p0, p1 in ((0, SPLIT), (SPLIT, G)):
                        sp.dma_start(ycat[p0:p1, p, k], yv[p0:p1, k, bass.ds(2 * s, 2), :]).then_inc(s_yl[p], 16)

            def store(s, p, groups):
                for g, n in groups:
                    for p0, p1 in ((0, min(n, SPLIT)), (SPLIT, n)):
                        if p1 > p0:
                            sp.dma_start(out[bass.ds((2 * s + g) * G + p0, p1 - p0)],
                                         res[p0:p1, p, g]).then_inc(s_out[p], 16)

            load_y(0, 0)
            load_y(1, 1)
            both = ((0, G), (1, G))
            with sp.Fori(0, STEPS // 2 - 1) as i:
                for p in range(2):
                    sp.wait_ge(s_sum, i * 2 + p + 1)
                    store(i * 2 + p, p, both)
                    load_y(i * 2 + p + 2, p)
            for s in range(STEPS - 3, STEPS):
                sp.wait_ge(s_sum, s + 1)
                store(s, s % 2, both if s < STEPS - 1 else ((0, G), (1, LAST)))
                if s + 2 < STEPS:
                    load_y(s + 2, s % 2)
            sp.wait_ge(s_out[0], 64 * (STEPS // 2) + 48)
            sp.wait_ge(s_out[1], 64 * (STEPS // 2))
            sp.wait_ge(s_fill, 16 * N_FILL)

        @blk.tensor
        def _(pe):
            pe.wait_ge(s_early, 16 * N_EARLY)
            pe.wait_ge(s_set, 2)
            pe.wait_ge(s_gw, 1)
            for c in range(PC):
                pe.matmul(PS[:, 6, 0:D], meanw[:, :], W_cen[:, c, :], start=(c == 0), stop=(c == PC - 1))
            for c in range(PC):
                pe.matmul(PS[:, 7, 0:D], bc(bb1[:, c:c + 1], [128, 128]), W_raw[:, c, :], start=(c == 0), stop=False)
            pe.matmul(PS[:, 7, 0:D], ones[0:1, :], blin[:, :], start=False, stop=True).then_inc(s_mean, 1)

            units = [(j, w) for j in range(NH // 2) for w in range(NH)]

            def tok_transpose(u):
                j, w = units[u]
                if w % (NH // 2) == 0:
                    pe.wait_ge(s_x[j][w // (NH // 2)], 32)
                if u >= 2:
                    pe.wait_ge(s_tTa, u - 1)
                for c in range(PC):
                    last = pe.transpose(PS[:, 2 * (u % 2) + c // 3, 128 * (c % 3):128 * (c % 3) + 128],
                                        xv[:, j, w, 128 * c:128 * c + 128], ident[:, :])
                last.then_inc(s_tT, 1)

            def tok_product(u):
                pe.wait_ge(s_tTa, u + 1)
                if u >= 4:
                    pe.wait_ge(s_tze, u - 3)
                for c in range(PC):
                    last = pe.matmul(PS[:, 4 + u % 4, 0:D], xTt[:, u % 2, c, :], W_cen[:, c, :],
                                     start=(c == 0), stop=(c == PC - 1))
                last.then_inc(s_tz, 1)

            tok_transpose(0)
            pe.wait_ge(s_wc, 1)
            for u in range(len(units)):
                if u + 1 < len(units):
                    tok_transpose(u + 1)
                tok_product(u)

            pe.wait_ge(s_tze, UNITS)
            pe.wait_ge(s_const, 16 * N_CONST)
            pe.wait_ge(s_aw, 16 * N_AW)
            for m in range(HB):
                last = pe.matmul(PS[:, 6, m * R:(m + 1) * R], wrk[:, m * 128:(m + 1) * 128], pos_f[:, :],
                                 start=(m == 0), stop=(m == HB - 1), skip_group_check=True)
            last.then_inc(s_rkp, 1)

            def rows_transposed(s):
                pe.wait_ge(s_xn, s + 1)
                if not is_step(s, 0):
                    pe.wait_ge(s_v[1], s)
                for g in range(2):
                    for k in range(2):
                        last = pe.transpose(PS[:, 2, k * G2 + g * G:k * G2 + (g + 1) * G],
                                            xn[:, g, k * 64:k * 64 + 128], ident[0:G, 0:G])
                last.then_inc(s_xTp, 1)

            def project(m2, w0, bank, done):
                for m in (2 * m2, 2 * m2 + 1):
                    for nth, (w, b_) in enumerate(BLOCKS):
                        lhsT = (wh, wl)[w][:, b_, w0 + m * 128:w0 + (m + 1) * 128]
                        last = pe.matmul(PS[:, bank, (m % 2) * G2:(m % 2 + 1) * G2], lhsT, xT[:, b_, :],
                                         start=(nth == 0 and m % 2 == 0), stop=(nth == len(BLOCKS) - 1),
                                         skip_group_check=True)
                last.then_inc(done, 1)

            def relative(g):
                for h in range(H):
                    q0 = 64 * (h % 2)
                    last = pe.matmul(PS[0:G, (6, 0)[g] + h % 2, (h // 2) * R:(h // 2 + 1) * R],
                                     qr[q0:q0 + 64, h // 2, g * G:(g + 1) * G], rk[q0:q0 + 64, h // 2, :],
                                     start=(h // 2 == 0), stop=True, skip_group_check=True)
                last.then_inc(s_rp[g], 1)

            def probs_transposed(g):
                for j in range(H):
                    last = pe.transpose(heads(4 - 2 * g, G)[:, j, :], pb[:, g, j * G:(j + 1) * G], ident[0:G, 0:G])
                last.then_inc(s_ptp[g], 1)

            def probs_values(g):
                for j in range(H):
                    h = head_at(j)
                    last = pe.matmul(heads(4 - 2 * g, V)[:, j, :],
                                     pT[:, g, j * G:(j + 1) * G], v_sb[:, g, h * V:(h + 1) * V],
                                     start=(j % HB == 0), stop=True, skip_group_check=True)
                last.then_inc(s_op[g], 1)

            def outputs_transposed(g):
                for c in range(HC):
                    last = pe.transpose(PS[:, (6, 4)[g] + c // 3, (c % 3) * G:(c % 3 + 1) * G],
                                        o_sb[:, g, c * 128:(c + 1) * 128], ident[0:G, 0:G])
                last.then_inc(s_otp[g], 1)

            def output_product(g):
                for c in range(HC):
                    last = pe.matmul(PS[0:G, g, 0:D], oT[:, g, c * G:(c + 1) * G], wo[:, c, :],
                                     start=(c == 0), stop=(c == HC - 1))
                last.then_inc(s_wop[g], 1)

            def values(g):
                for n in range(2):
                    at = 2 * H * K + n * HB * V
                    for nth, (w, b_) in enumerate(BLOCKS):
                        last = pe.matmul(PS[0:G, 2 * g + n, 0:HB * V], xT[:, b_, g * G:(g + 1) * G],
                                         (wh, wl)[w][:, b_, at:at + HB * V],
                                         start=(nth == 0), stop=(nth == len(BLOCKS) - 1))
                last.then_inc(s_vp[g], 1)

            def content(g):
                for h in range(H):
                    q0 = 64 * (h % 2)
                    last = pe.matmul(heads(4 + 2 * g, G)[:, h % 2 * HB + h // 2, :],
                                     qw[q0:q0 + 64, h // 2, g * G:(g + 1) * G],
                                     kT[q0:q0 + 64, h // 2, g * G:(g + 1) * G],
                                     start=(h // 2 == 0), stop=True, skip_group_check=True)
                last.then_inc(s_sp[g], 1)

            def gate_rows(s):
                for g in range(2):
                    pe.wait_ge(s_xr[g], s + 1)
                    for k in range(2):
                        last = pe.transpose(PS[0:KD, 3, k * G2 + g * G:k * G2 + (g + 1) * G],
                                            xn2[:, g, k * KD:(k + 1) * KD], ident[0:G, 0:G])
                last.then_inc(s_xrp, 1)

            def gate(s):
                pe.wait_ge(s_xrT, s + 1)
                for g in range(2):
                    for k in range(2):
                        last = pe.matmul(PS[0:G, 3, g * E:(g + 1) * E], xnT[:, k, g * G:(g + 1) * G], wg[:, k, :],
                                         start=(g == 0 and k == 0), stop=(k == 1), skip_group_check=True)
                last.then_inc(s_lp, 1)

            def step(s):
                here = not is_step(s, STEPS)
                before_ = not is_step(s, 0)
                before2 = before_ and not is_step(s, 1)
                if here:
                    pe.wait_ge(s_xT, s + 1)
                    if before2:
                        pe.wait_ge(s_h1[1], s - 1)
                    elif before_:
                        pe.wait_ge(s_v[0], s)
                    project(0, 0, 1, s_qp)
                    project(0, H * K, 2, s_kp)
                if before2:
                    gate(s - 2)
                if here:
                    if before2:
                        pe.wait_ge(s_h1[0], s - 1)
                    project(1, 0, 0, s_qp)
                    if before2:
                        pe.wait_ge(s_l, s - 1)
                    elif before_:
                        pe.wait_ge(s_v[1], s)
                    project(1, H * K, 3, s_kp)
                if before_:
                    pe.wait_ge(s_p[0], s)
                    probs_transposed(0)
                if here:
                    pe.wait_ge(s_q, s * 2 + 2)
                    if before_:
                        pe.wait_ge(s_sc[1], s)
                    else:
                        pe.wait_ge(s_rk, 1)
                    relative(0)
                if before_:
                    pe.wait_ge(s_p[1], s)
                    if here:
                        pe.wait_ge(s_k, s * 2 + 2)
                    else:
                        pe.wait_ge(s_xT, s + 1)
                        pe.wait_ge(s_l, s - 1)
                    probs_transposed(1)
                if here:
                    relative(1)
                if before_:
                    for g in range(2):
                        pe.wait_ge(s_pt[g], s)
                        pe.wait_ge(s_v[g], s)
                        probs_values(g)
                    pe.wait_ge(s_o[0], s)
                    if here:
                        pe.wait_ge(s_re[0], s + 1)
                    else:
                        pe.wait_ge(s_sc[1], s)
                    outputs_transposed(0)
                if here:
                    pe.wait_ge(s_re[1], s + 1)
                    values(0)
                if before_:
                    pe.wait_ge(s_o[1], s)
                    outputs_transposed(1)
                if here:
                    if not before_:
                        pe.wait_ge(s_k, 2)
                    values(1)
                if before_:
                    for g in range(2):
                        pe.wait_ge(s_ot[g], s)
                        if here:
                            pe.wait_ge(s_v[0], s + 1)
                        else:
                            pe.wait_ge(s_h1[g], s - 1)
                        output_product(g)
                if here:
                    rows_transposed(s + 1)
                    pe.wait_ge(s_k, s * 2 + 2)
                    if before_:
                        pe.wait_ge(s_ot[1], s)
                    content(0)
                    if before_:
                        pe.wait_ge(s_ot[0], s)
                    else:
                        pe.wait_ge(s_re[0], 1)
                    content(1)
                if before_:
                    if not here:
                        pe.wait_ge(s_o[1], s)
                    gate_rows(s - 1)

            rows_transposed(0)
            pe.wait_ge(s_wh, 1)
            pe.wait_ge(s_wl, 1)
            step(0)
            step(1)
            with pe.Fori(2, STEPS) as s:
                step(s)
            step(STEPS)
            gate(STEPS - 1)

            pe.wait_ge(s_prio, 1)
            for g in range(NG):
                last = pe.transpose(PS[0:G, g // 4, (g % 4) * G:(g % 4 + 1) * G],
                                    bc(prio[:, g:g + 1], [G, G]), ident[0:G, 0:G])
                if g % 4 == 3 or g == NG - 1:
                    last.then_inc(s_pbp, 1)

            for nth, j in enumerate(2 * q + a for q in RANKED for a in range(2)):
                at = PS[0:G, 6 + nth // 2 % 2, j % 2 * E:(j % 2 + 1) * E]
                if j < NG - RT:
                    pe.wait_ge(s_bef, j + 1)
                if nth == 0:
                    pe.wait_ge(s_own, 1)
                if nth % 2 == 0 and nth >= 4:
                    pe.wait_ge(s_slot, nth // 2 - 1)
                if j == NG - RT:
                    pe.wait_ge(s_sgn, 1)
                for i in range(NG):
                    if i == j or j < NG - RT:
                        lhsT = own[:, j, :] if i == j else before[j % 2][:, i, :]
                        last = pe.matmul(at, lhsT, ohb[:, i, :],
                                         start=(j % 2 == 0 and i == 0), stop=True, skip_group_check=True)
                    else:
                        last = pe.matmul(at, sgn[:, j - (NG - RT), i, :], ohh[:, i, :],
                                         start=(j % 2 == 0 and i == 0), stop=True, skip_group_check=True)
                if j >= NG - RT:
                    pe.matmul(at, onesb[:, :], ohsb[:, :], start=False, stop=True, skip_group_check=True)
                    last = pe.matmul(at, onesb[:, :], ohn[:, j, :], start=False, stop=True, skip_group_check=True)
                last.then_inc(s_cnt, 1)

            def expert_rows(e, p, i2, e_before=None):
                pe.wait_ge(s_ex[p], i2 * 32 + 32)
                for k in range(2):
                    if k == 1 and e_before is not None:
                        pe.wait_ge(s_hg, e_before * HC + 4)
                    for i in range(NT):
                        n = tile_rows(i)
                        last = pe.transpose(PS[:, 2 * k + i // 4, 128 * (i % 4):128 * (i % 4) + n],
                                            xe[0:n, p, i, k * 64:k * 64 + 128], ident[0:n, 0:n])
                last.then_inc(s_xep, 1)

            def hidden(e, first):
                pe.wait_ge(s_xeh, e + 1)
                pe.wait_ge(s_xel, e + 1)
                pe.wait_ge(s_w1h, e + 1)
                pe.wait_ge(s_w1l, e + 1)
                if first:
                    pe.wait_ge(s_zw, 1)
                for c in range(HC):
                    if c == 1 and not first:
                        pe.wait_ge(s_ye, e * NT)
                    if c >= 3:
                        pe.wait_ge(s_hg, e * HC + c - 2)
                    w = slice(c * 128, (c + 1) * 128)
                    for n in range(2):
                        for nth, (hl, b_) in enumerate(BLOCKS):
                            last = pe.matmul(PS[:, hidden_bank(c) + n, 0:HALF], (w1h, w1l)[hl][:, b_, w],
                                             xeT[:, b_, n * HALF:(n + 1) * HALF],
                                             start=(nth == 0), stop=(nth == len(BLOCKS) - 1))
                    last.then_inc(s_hp, 1)

            def results(e):
                pe.wait_ge(s_w2h, e + 1)
                pe.wait_ge(s_w2l, e + 1)
                pe.wait_ge(s_hg, e * HC + HC - 1)
                pe.wait_ge(s_hl, e * HC + HC - 1)
                for i in range(NT):
                    bank = 4 + i % 4
                    n = tile_rows(i)
                    if i >= 4:
                        pe.wait_ge(s_ye, e * NT + i - 3)
                    for c in range(HC):
                        if i == 0 and c == HC - 1:
                            pe.wait_ge(s_hg, e * HC + HC)
                            pe.wait_ge(s_hl, e * HC + HC)
                        at = slice(128 * i, 128 * i + n)
                        pe.matmul(PS[0:n, bank, 0:D], hTh[:, c, at], w2h[:, c, :], start=(c == 0), stop=False)
                        pe.matmul(PS[0:n, bank, 0:D], hTh[:, c, at], w2l[:, c, :], start=False, stop=False)
                        last = pe.matmul(PS[0:n, bank, 0:D], hTl[:, c, at], w2h[:, c, :], start=False,
                                         stop=(c == HC - 1))
                    last.then_inc(s_yp, 1)

            expert_rows(0, 0, 0)
            hidden(0, True)
            expert_rows(1, 1, 0, 0)
            results(0)
            with pe.Fori(0, E // 2 - 1) as i:
                hidden(i * 2 + 1, False)
                expert_rows(i * 2 + 2, 0, i + 1, i * 2 + 1)
                results(i * 2 + 1)
                hidden(i * 2 + 2, False)
                expert_rows(i * 2 + 3, 1, i + 1, i * 2 + 2)
                results(i * 2 + 2)
            hidden(E - 1, False)
            results(E - 1)

        @blk.scalar
        def _(act):
            for u in range(UNITS):
                act.wait_ge(s_tT, u + 1)
                if u >= 2:
                    act.wait_ge(s_tz, u - 1)
                nc.scalar.copy(xTt[:, u % 2, :, :].rearrange("p (a c) n -> p a (c n)", a=2),
                               PS[:, 2 * (u % 2):2 * (u % 2) + 2, 0:384]).then_inc(s_tTa, 1)

            def rows_transposed(s):
                act.wait_ge(s_xTp, s + 1)
                nc.scalar.copy(xT[:, 0:2, :].rearrange("p k n -> p (k n)"), PS[:, 2, 0:2 * G2]).then_inc(s_xTh, 1)

            def queries(s, m2):
                act.wait_ge(s_qp, s * 2 + m2 + 1)
                for q, b_ in ((qr, rrb), (qw, rwb)):
                    for m in (2 * m2, 2 * m2 + 1):
                        last = nc.scalar.activation(q[:, m, :], PS[:, 1 - m2, (m % 2) * G2:(m % 2 + 1) * G2],
                                                    ACT.Identity, bias=b_[:, m:m + 1], scale=K ** -0.5)
                last.then_inc(s_q, 1)

            def relative(s, g):
                act.wait_ge(s_rp[g], s + 1)
                if not is_step(s, 0):
                    act.wait_ge(s_ro[g], 96 * s)
                nc.scalar.copy(rel[:, g, :].rearrange("p (a n) -> p a n", a=2),
                               PS[0:G, (6, 0)[g]:(8, 2)[g], 0:HB * R]).then_inc(s_re[g], 1)

            def outputs(s, g):
                act.wait_ge(s_otp[g], s + 1)
                nc.scalar.copy(oT[:, g, :].rearrange("p (a n) -> p a n", a=2),
                               PS[:, (6, 4)[g]:(8, 6)[g], 0:3 * G]).then_inc(s_ot[g], 1)

            def values(s, g):
                act.wait_ge(s_vp[g], s + 1)
                nc.scalar.copy(v_sb[:, g, :].rearrange("p (a n) -> p a n", a=2),
                               PS[0:G, 2 * g:2 * g + 2, 0:HB * V]).then_inc(s_v[g], 1)

            def probs(s, g):
                act.wait_ge(s_sh[g], s + 1)
                nc.scalar.activation(
                    pb[:, g, :].rearrange("p (h i t) -> p h i t", h=H, i=IPG),
                    bc(sc[:, g, :].rearrange("p (h a t) -> p h a t", h=H, a=1), [G, H, IPG, T]),
                    ACT.Exp).then_inc(s_p[g], 1)

            def gate_rows(s):
                act.wait_ge(s_xrp, s + 1)
                nc.scalar.copy(xnT[:, :, :].rearrange("p k n -> p (k n)"), PS[0:KD, 3, 0:2 * G2]).then_inc(s_xrT, 1)

            def logits(s):
                act.wait_ge(s_lp, s + 1)
                nc.scalar.copy(logit[:, bass.ds(2 * s, 2), :],
                               PS[0:G, 3, 0:2 * E].rearrange("p (g e) -> p g e", g=2)).then_inc(s_l, 1)

            act.wait_ge(s_qkv, 16 * N_QKV)
            nc.scalar.copy(wh[:, :, :], wraw[:, :, :]).then_inc(s_wh, 1)
            act.wait_ge(s_aw, 16 * N_AW)
            rows_transposed(0)

            def step(s):
                here = not is_step(s, STEPS)
                before_ = not is_step(s, 0)
                if before_:
                    probs(s - 1, 0)
                if here:
                    queries(s, 0)
                if before_ and not is_step(s, 1):
                    logits(s - 2)
                if here:
                    queries(s, 1)
                if before_:
                    probs(s - 1, 1)
                if here:
                    relative(s, 0)
                    relative(s, 1)
                for g in range(2):
                    if before_:
                        outputs(s - 1, g)
                    if here:
                        values(s, g)
                if here:
                    rows_transposed(s + 1)
                if before_:
                    gate_rows(s - 1)

            step(0)
            step(1)
            with act.Fori(2, STEPS) as s:
                step(s)
            step(STEPS)
            logits(STEPS - 1)
            act.wait_ge(s_d, 1)
            nc.scalar.activation(ex[:, :], ex[:, :], ACT.Exp).then_inc(s_e, 1)

            for b_ in range(3, -(-NG // 4)):
                act.wait_ge(s_pbp, b_ + 1)
                n = min(4, NG - 4 * b_) * G
                last = nc.scalar.copy(prow[:, b_ * 4 * G:b_ * 4 * G + n], PS[0:G, b_, 0:n])
            last.then_inc(s_pba, 1)
            act.wait_ge(s_pba, 1)
            act.wait_ge(s_nudge, 1)
            pcols = prow[:, (NG - RT) * G:].rearrange("p (j n) -> p j n", j=RT)
            for i in range(NG):
                for j0, j1, bias in ((0, i, prio_dn), (i + 1, NG, prio_up)):
                    a, b_ = max(0, j0 - (NG - RT)), j1 - (NG - RT)
                    if b_ > a:
                        last = nc.scalar.activation(sgn[:, a:b_, i, :], pcols[:, a:b_, :], ACT.Sign,
                                                    bias=bias[:, i:i + 1], scale=-1.0)
            last.then_inc(s_sgn, 1)

            def w1_high(e):
                act.wait_ge(s_w1r, e * 64 + 64)
                act.wait_ge(s_hp, e * HC) if not is_step(e, 0) else None
                nc.scalar.copy(w1h[:, :, :], w1r[:, :, :]).then_inc(s_w1h, 1)

            def rows_high(e):
                act.wait_ge(s_xep, e + 1)
                for k in range(2):
                    last = nc.scalar.copy(xeT[:, k, :], both_banks(2 * k))
                last.then_inc(s_xeh, 1)

            def expert(e, p, i2, first):
                act.wait_ge(s_w2r, e * 16 + 16)
                if not first:
                    act.wait_ge(s_yp, e * NT)
                nc.scalar.copy(w2h[:, :, :], w2r[:, :, :]).then_inc(s_w2h, 1)
                act.wait_ge(s_eb[p], i2 * 32 + 32)
                for c in range(HC):
                    act.wait_ge(s_hp, e * HC + c + 1)
                    src = PS[:, hidden_bank(c):hidden_bank(c) + 2, 0:HALF]
                    if not first or c >= 2:
                        act.wait_ge(s_hl, e * HC + c - 1)
                    last = nc.scalar.activation(hf[:, c % 2, :].rearrange("p (a n) -> p a n", a=2), src, ACT.Gelu,
                                                bias=b1s[:, p, c:c + 1])
                    if c not in HIGH_BY_DVE:
                        last = nc.scalar.activation(hTh[:, c, :].rearrange("p (a n) -> p a n", a=2), src, ACT.Gelu,
                                                    bias=b1s[:, p, c:c + 1])
                    last.then_inc(s_hg, 1)

            act.wait_ge(s_cnt, NG)
            w1_high(0)
            rows_high(0)
            expert(0, 0, 0, True)
            rows_high(1)
            w1_high(1)
            with act.Fori(0, E // 2 - 1) as i:
                for p in (1, 0):
                    e = i * 2 + 2 - p
                    expert(e, p, i + 1 - p, False)
                    rows_high(e + 1)
                    w1_high(e + 1)
            expert(E - 1, 1, E // 2 - 1, False)

        @blk.vector
        def _(dve):
            v = nc.vector

            def ch(ins):
                dve.drain()

            v.memset(ones[:, :], 1.0)
            v.memset(zeros[:, :], 0.0).then_inc(s_set, 1)
            v.memset(meanw[:, :], 1.0 / PD).then_inc(s_set, 1)
            v.memset(h_all[:, NG:NG + 2, :], 0.0)
            v.memset(onesb[:, :], 1.0)
            v.memset(nhalf[:, :], -0.5).then_inc(s_setv, 1)

            dve.wait_ge(s_early, 16 * N_EARLY)
            for c in range(PC):
                last = v.tensor_scalar(W_cen[:, c, :], W_raw[:, c, :], g1[:, c:c + 1], None, ALU.mult)
            last.then_inc(s_gw, 1)
            dve.wait_ge(s_gw, 1)

            def ln1_stats(j, w):
                if w % (NH // 2) == 0:
                    dve.wait_ge(s_x[j][w // (NH // 2)], 32)
                for q in range(2):
                    v.bn_stats(bn1[:, j, w, q, :], xv[:, j, w, q * (PD // 2):(q + 1) * (PD // 2)])

            def ln1_end(j):
                dve.drain()
                for w in range(NH):
                    last = v.bn_aggr(mv1[:, j, w, :], bn1[:, j, w, :, :])
                ch(last)
                v.tensor_scalar(ve1[:, j, :], mv1[:, j, :, 1], EPS, None, ALU.add).then_inc(s_v1, 1)

            for w in range(NH // 2):
                ln1_stats(0, w)
            dve.wait_ge(s_mean, 1)
            v.tensor_copy(cB[:, :], PS[:, 7, 0:D])
            for c in range(PC):
                last = v.tensor_tensor(W_cen[:, c, :], W_cen[:, c, :], PS[:, 6, 0:D], ALU.subtract)
            last.then_inc(s_wc, 1)
            for w in range(NH // 2, NH):
                ln1_stats(0, w)
            ln1_end(0)

            def ln2_stats(j):
                dve.wait_ge(s_tze, (j + 1) * NH)
                for w in range(NH):
                    last = v.bn_stats(bnt[:, j, w, :], zt[:, j, w, :])
                ch(last)
                for w in range(NH):
                    last = v.bn_aggr(mvt[:, j, w, :], bnt[:, j, w, :])
                ch(last)
                v.tensor_scalar(vet[:, j, :], mvt[:, j, :, 1], EPS, None, ALU.add).then_inc(s_v2, 1)

            def ln2_rows(j):
                dve.wait_ge(s_r2, j + 1)
                for w in range(NH):
                    last = v.tensor_scalar(zt[:, j, w, :], zt[:, j, w, :], mvt[:, j, w, 0:1], rst[:, j, w:w + 1],
                                           ALU.subtract, ALU.mult)
                last.then_inc(s_tn, 1)

            for j in range(NH // 2):
                dve.wait_ge(s_r1, j + 1)
                for w in range(NH):
                    u = j * NH + w
                    dve.wait_ge(s_tz, u + 1)
                    v.scalar_tensor_tensor(zt[:, j, w, :], PS[:, 4 + u % 4, 0:D], rs1[:, j, w:w + 1], cB[:, :],
                                           ALU.mult, ALU.add).then_inc(s_tze, 1)
                    if j + 1 < NH // 2:
                        ln1_stats(j + 1, w)
                    if w == 1 and j:
                        ln2_rows(j - 1)
                if j + 1 < NH // 2:
                    ln1_end(j + 1)
                ln2_stats(j)
            ln2_rows(NH // 2 - 1)
            dve.wait_ge(s_const, 16 * N_CONST)
            v.memset(wl[0:64, 1, :].bitcast(F32), 0.0)
            dve.wait_ge(s_wh, 1)
            v.tensor_tensor(wl[:, 0, :], wraw[:, 0, :], wh[:, 0, :].bitcast(F32), ALU.subtract)
            v.tensor_tensor(wl[64:128, 1, :], wraw[64:128, 2, :], wh[64:128, 2, :].bitcast(F32),
                            ALU.subtract).then_inc(s_wl, 1)
            dve.wait_ge(s_rkp, 1)
            v.tensor_copy(rk[:, :, :].rearrange("p m r -> p (m r)"), PS[:, 6, 0:HB * R]).then_inc(s_rk, 1)

            def ln1(s):
                for g in range(2):
                    ch(v.bn_stats(st[:, :], h_all[:, 2 * s + g, :]))
                    ch(v.bn_aggr(mv[:, g, :], st[:, :]))
                v.tensor_scalar(ve[:, :], mv[:, :, 1], EPS, None, ALU.add).then_inc(s_va, 1)
                dve.wait_ge(s_ra, s + 1)
                for g in range(2):
                    last = v.tensor_scalar(xn[:, g, :], h_all[:, 2 * s + g, :], mv[:, g, 0:1], rs[:, g:g + 1],
                                           ALU.subtract, ALU.mult)
                last.then_inc(s_xn, 1)

            def rows_low(s):
                dve.wait_ge(s_xTh, s + 1)
                ch(v.tensor_tensor(xT[:, 2, :], PS[:, 2, G2:2 * G2], xT[:, 1, :].bitcast(F32), ALU.subtract))
                v.tensor_tensor(xT[0:64, 1, :], PS[0:64, 2, 0:G2], xT[0:64, 0, :].bitcast(F32),
                                ALU.subtract).then_inc(s_xT, 1)

            def keys(s):
                for m2 in range(2):
                    dve.wait_ge(s_kp, s * 2 + m2 + 1)
                    v.tensor_copy(kT[:, 2 * m2:2 * m2 + 2, :].rearrange("p m n -> p (m n)"),
                                  PS[:, 2 + m2, 0:2 * G2]).then_inc(s_k, 1)

            def softmax(s):
                for g in range(2):
                    dve.wait_ge(s_sp[g], s + 1)
                    dve.wait_ge(s_ri[g], s * 32 + 32)
                    a3 = sc[:, g, :].rearrange("p (h t) -> p h t", h=H)
                    r3 = relw[:, g, :].rearrange("p (h t) -> p h t", h=H)
                    for i in range(IPG):
                        ins = v.scalar_tensor_tensor(a3, heads(4 + 2 * g, G)[:, :, i * T:(i + 1) * T],
                                                     ind[:, i:i + 1], a3 if i else r3, ALU.mult, ALU.add)
                        if i < IPG - 1:
                            ch(ins)
                    ins.then_inc(s_sc[g], 1)
                    dve.wait_ge(s_sc[g], s + 1)
                    ch(v.tensor_reduce(mx[:, g, :], a3, AX.X, ALU.max))
                    v.tensor_tensor(a3, a3, bc(mx[:, g, :].rearrange("p (h a) -> p h a", a=1), [G, H, T]),
                                    ALU.subtract).then_inc(s_sh[g], 1)

            def masked(s):
                for g in range(2):
                    dve.wait_ge(s_ptp[g], s + 1)
                    v.tensor_tensor(pT[:, g, :].rearrange("p (h t) -> p h t", h=H), heads(4 - 2 * g, G),
                                    bc(block[:, :].rearrange("p (a t) -> p a t", a=1), [G, H, G]),
                                    ALU.mult).then_inc(s_pt[g], 1)
                    dve.wait_ge(s_p[g], s + 1)
                    ch(v.tensor_reduce(rsum[:, g, :], pb[:, g, :].rearrange("p (h i t) -> p h i t", h=H, i=IPG)[:, :, 0, :],
                                       AX.X, ALU.add))
                    ch(v.reciprocal(rinv[:, g, :], rsum[:, g, :]))
                for g in range(2):
                    dve.wait_ge(s_op[g], s + 1)
                    v.tensor_tensor(o_sb[:, g, :].rearrange("p (h t) -> p h t", h=H), heads(4 - 2 * g, V),
                                    bc(rinv[:, g, :].rearrange("p (h a) -> p h a", a=1), [G, H, V]),
                                    ALU.mult).then_inc(s_o[g], 1)

            def residual(s):
                dve.wait_ge(s_hb, s + 1)
                for g in range(2):
                    dve.wait_ge(s_wop[g], s + 1)
                    v.tensor_tensor(h_all[:, 2 * s + g, :], h_all[:, 2 * s + g, :], PS[0:G, g, 0:D],
                                    ALU.add).then_inc(s_h1[g], 1)
                    dve.drain()
                    ch(v.bn_stats(st2[:, :], h_all[:, 2 * s + g, :]))
                    ch(v.bn_aggr(mv2[:, g, :], st2[:, :]))
                    v.tensor_scalar(ve2[:, g:g + 1], mv2[:, g, 1:2], EPS, None, ALU.add).then_inc(s_vb[g], 1)
                for g in range(2):
                    dve.wait_ge(s_rb[g], s + 1)
                    if g == 0:
                        if not is_step(s, 0):
                            for c in s_xrc:
                                dve.wait_ge(c, s)
                    v.tensor_scalar(xn2[:, g, :], h_all[:, 2 * s + g, :], mv2[:, g, 0:1], rs2[:, g:g + 1],
                                    ALU.subtract, ALU.mult).then_inc(s_xr[g], 1)

            def step(s):
                here = not is_step(s, STEPS)
                before_ = not is_step(s, 0)
                if before_:
                    softmax(s - 1)
                if here:
                    keys(s)
                if before_:
                    masked(s - 1)
                if here:
                    ln1(s + 1)
                if before_:
                    residual(s - 1)
                if here:
                    rows_low(s + 1)

            dve.wait_ge(s_h, 32)
            ln1(0)
            rows_low(0)
            dve.wait_ge(s_h, 64)
            step(0)
            step(1)
            with dve.Fori(2, STEPS) as s:
                step(s)
            step(STEPS)

            dve.wait_ge(s_l, STEPS)
            dve.wait_ge(s_aw, 16 * N_AW)
            io = bc(iota8[:, 0:1, :], [G, NG, E])
            io8 = bc(iota8[:, 1:2, :], [G, NG, E])
            col = lambda a: bc(a.rearrange("p (g a) -> p g a", a=1), [G, NG, E])
            src = logit[:, :, :]
            for k, (m, ii) in enumerate(((m1, i1), (m2, i2))):
                ch(v.tensor_reduce(m[:, :], src, AX.X, ALU.max))
                ch(v.tensor_tensor(tmp8[:, :, :], src, col(m[:, :]), ALU.is_equal))
                ch(v.scalar_tensor_tensor(tmp8[:, :, :], tmp8[:, :, :], -8.0, io8, ALU.mult, ALU.add))
                ch(v.tensor_reduce(ii[:, :], tmp8[:, :, :], AX.X, ALU.min))
                ch(v.tensor_tensor(oh[:, k], io, col(ii[:, :]), ALU.is_equal))
                if k == 0:
                    ch(v.scalar_tensor_tensor(l2[:, :, :], oh[:, 0], -1.0e30, src, ALU.mult, ALU.add))
                    src = l2[:, :, :]
            v.tensor_tensor(ex[:, :], m2[:, :], m1[:, :], ALU.subtract).then_inc(s_d, 1)
            for k in range(2):
                ch(v.tensor_tensor(oh[:, k], oh[:, k], col(real[:, :]), ALU.mult))
            ch(v.tensor_tensor(ohb[:, :, :], oh[:, 0], oh[:, 1], ALU.add))
            dve.wait_ge(s_e, 1)
            ch(v.tensor_scalar(w01[:, 0, :], ex[:, :], 1.0, None, ALU.add))
            ch(v.reciprocal(w01[:, 0, :], w01[:, 0, :]))
            ch(v.tensor_tensor(w01[:, 1, :], w01[:, 0, :], ex[:, :], ALU.mult))
            v.tensor_scalar(prio[:, :], w01[:, 0, :], -0.75, -0.25, ALU.add, ALU.max).then_inc(s_prio, 1)
            dve.wait_ge(s_prio, 1)
            v.tensor_scalar(prio_up[:, :], prio[:, :], HALF_ULP, None, ALU.add)
            v.tensor_scalar(prio_dn[:, :], prio[:, :], -HALF_ULP, None, ALU.add).then_inc(s_nudge, 1)
            v.tensor_copy(xr_all[:, :, D], w01[:, 0, :])
            v.tensor_copy(xr_all[:, :, D + 1], w01[:, 1, :])
            v.tensor_copy(xr_all[:, :, D + 2], i1[:, :])
            v.tensor_copy(xr_all[:, :, D + 3], tok[:, :])
            for k, ii in enumerate((i1, i2)):
                v.tensor_scalar(base[:, k, :], ii[:, :], float(CAP), BIG, ALU.mult, ALU.add)
            v.tensor_scalar(lower_by[:, :], upper[:, :], HALF_ULP, None, ALU.mult)
            v.tensor_scalar(ohh[:, :, :], ohb[:, :, :], 0.5, None, ALU.mult)
            v.tensor_scalar(ohn[:, :, :], ohb[:, :, :], -0.5, None, ALU.mult)
            ch(v.tensor_reduce(ohs[:, :], ohb[:, :, :].rearrange("p g e -> p e g"), AX.X, ALU.add))
            v.tensor_scalar(ohsb[:, :], ohs[:, :], 0.5, None, ALU.mult)
            for b_ in range(3):
                dve.wait_ge(s_pbp, b_ + 1)
                last = v.tensor_copy(prow[:, b_ * 4 * G:(b_ + 1) * 4 * G], PS[0:G, b_, 0:4 * G])
            last.then_inc(s_pb, 1)
            dve.wait_ge(s_pb, 1)

            def compare(j):
                pj = prow[:, j * G:(j + 1) * G]
                if j >= 2:
                    dve.wait_ge(s_cnt, 2 * RANKED.index(j // 2 - 1) + j % 2 + 1)
                for a, b_, op in ((0, j, ALU.is_le), (j + 1, NG, ALU.is_lt)):
                    if b_ > a:
                        last = v.tensor_tensor(before[j % 2][:, a:b_, :],
                                               bc(pj.rearrange("p (a n) -> p a n", a=1), [G, b_ - a, G]),
                                               bc(prio[:, a:b_].rearrange("p (i a) -> p i a", a=1),
                                                  [G, b_ - a, G]), op)
                last.then_inc(s_bef, 1)

            def compare_own():
                dve.wait_ge(s_pba, 1)
                p3 = prow[:, :].rearrange("p (j n) -> p j n", j=NG)
                l3 = bc(lower_by[:, :].rearrange("p (a n) -> p a n", a=1), [G, NG, G])
                ch(v.tensor_tensor(nudged[:, :, :], p3, l3, ALU.subtract))
                v.tensor_tensor(own[:, :, :], nudged[:, :, :], bc(prio[:, :].rearrange("p (j a) -> p j a", a=1), [G, NG, G]),
                                ALU.is_lt).then_inc(s_own, 1)

            def slots(nth):
                dve.wait_ge(s_cnt, 2 * nth + 2)
                q = RANKED[nth]
                w2 = slice(2 * q, 2 * q + 2)
                ranks = PS[0:G, 6 + nth % 2, 0:2 * E].rearrange("p (a g e) -> p a g e", a=1, g=2)
                ch(v.tensor_tensor(tmp4[:, :, :, :], oh[:, :, w2, :], bc(ranks, [G, 2, 2, E]), ALU.mult))
                ch(v.tensor_reduce(posk[:, :, w2], tmp4[:, :, :, :], AX.X, ALU.add))
                v.scalar_tensor_tensor(keep[:, :, w2], posk[:, :, w2], float(CAP),
                                          bc(real[:, w2].rearrange("p (a g) -> p a g", a=1), [G, 2, 2]),
                                          ALU.is_lt, ALU.mult)
                ch(v.tensor_tensor(slot[:, :, w2], base[:, :, w2], posk[:, :, w2], ALU.add))
                v.scalar_tensor_tensor(sloti[:, :, w2], keep[:, :, w2], -BIG, slot[:, :, w2], ALU.mult,
                                       ALU.add).then_inc(s_slot, 1)

            compare(0)
            compare_own()
            for j in range(1, NG - RT):
                compare(j)
                if j in SLOTS_AFTER:
                    slots(SLOTS_AFTER[j])
            for nth in range(len(SLOTS_AFTER), NG // 2):
                slots(nth)

            def w1_low(e):
                dve.wait_ge(s_w1h, e + 1)
                v.tensor_tensor(w1l[:, 0, :], w1r[:, 0, :], w1h[:, 0, :].bitcast(F32), ALU.subtract)
                v.tensor_tensor(w1l[64:128, 1, :], w1r[64:128, 2, :], w1h[64:128, 2, :].bitcast(F32),
                                ALU.subtract).then_inc(s_w1l, 1)

            def rows_low(e, p):
                dve.wait_ge(s_xeh, e + 1)
                ch(v.tensor_tensor(xeT[:, 2, :], both_banks(2), xeT[:, 1, :].bitcast(F32), ALU.subtract))
                v.tensor_tensor(xeT[0:64, 1, :], both_banks(0)[0:64], xeT[0:64, 0, :].bitcast(F32),
                                ALU.subtract).then_inc(s_xel, 1)

            def routing(e, p, i):
                t = lambda n: xe[:, p, :, D + n]
                ch(v.tensor_scalar(first[:, p, :], t(2), eidx[:, bass.ds(e, 1)], None, ALU.is_equal))
                ch(v.tensor_tensor(wtmp[:, p, :], first[:, p, :], t(0), ALU.mult))
                ch(v.tensor_scalar(first[:, p, :], first[:, p, :], -1.0, 1.0, ALU.mult, ALU.add))
                v.scalar_tensor_tensor(dst[:, p, :], first[:, p, :], float(ROWS), t(3), ALU.mult, ALU.add)
                ch(v.tensor_tensor(wsel[:, p, :], first[:, p, :], t(1), ALU.mult))
                v.tensor_tensor(wsel[:, p, :], wsel[:, p, :], wtmp[:, p, :], ALU.add).then_inc(s_wsel, 1)
                if not is_step(i, 0):
                    dve.wait_ge(s_ys[p], i * (16 * NT))
                v.tensor_copy(dsti[:, p, :], dst[:, p, :]).then_inc(s_di, 1)

            def hidden_low(e, first):
                dve.wait_ge(s_w2h, e + 1)
                v.tensor_tensor(w2l[:, :, :], w2r[:, :, :], w2h[:, :, :].bitcast(F32), ALU.subtract
                                ).then_inc(s_w2l, 1)
                for c in range(HC):
                    dve.wait_ge(s_hg, e * HC + c + 1)
                    if c in HIGH_BY_DVE:
                        ch(v.tensor_copy(hTh[:, c, :], hf[:, c % 2, :]))
                    v.tensor_tensor(hTl[:, c, :], hf[:, c % 2, :], hTh[:, c, :].bitcast(F32), ALU.subtract
                                    ).then_inc(s_hl, 1)

            def results(e, p):
                dve.wait_ge(s_wb, e + 1)
                for n in range(NT):
                    dve.wait_ge(s_yp, e * NT + n + 1)
                    r = tile_rows(n)
                    v.scalar_tensor_tensor(ye[0:r, p, n, :], PS[0:r, 4 + n % 4, 0:D], wsel[0:r, p, n:n + 1],
                                           wb2[0:r, p, n, :], ALU.mult, ALU.add).then_inc(s_ye, 1)

            v.memset(w1l[0:64, 1, :].bitcast(F32), 0.0).then_inc(s_zw, 1)
            w1_low(0)
            rows_low(0, 0)
            routing(0, 0, 0)
            hidden_low(0, True)
            rows_low(1, 1)
            routing(1, 1, 0)
            w1_low(1)
            results(0, 0)
            with dve.Fori(0, E // 2 - 1) as i:
                for p in (1, 0):
                    e = i * 2 + 2 - p
                    hidden_low(e, False)
                    rows_low(e + 1, 1 - p)
                    routing(e + 1, 1 - p, i + 1)
                    w1_low(e + 1)
                    results(e, p)
            hidden_low(E - 1, False)
            results(E - 1, 1)

            def total(s, p, i):
                dve.wait_ge(s_yl[p], i * 64 + 64)
                ch(v.tensor_tensor(ycat[:, p, 0], ycat[:, p, 0], ycat[:, p, 1], ALU.add))
                if not isinstance(i, int) or i:
                    dve.wait_ge(s_out[p], i * 64)
                v.tensor_tensor(res[:, p], ycat[:, p, 0], h_all[:, bass.ds(2 * s, 2), :], ALU.add).then_inc(s_sum, 1)

            for p in range(2):
                total(p, p, 0)
            with dve.Fori(1, (STEPS - 1) // 2) as i:
                for p in range(2):
                    total(i * 2 + p, p, i)
            total(STEPS - 1, 0, (STEPS - 1) // 2)

        @blk.gpsimd
        def _(pool):
            p_ = nc.gpsimd

            def rsqrt(o, i):
                return p_.tensor_tensor(o, i, nhalf[0:i.shape[0], 0:i.shape[1]], ALU.pow)

            pool.wait_ge(s_setv, 1)
            pool.wait_ge(s_v1, 1)
            rsqrt(rs1[:, 0, :], ve1[:, 0, :]).then_inc(s_r1, 1)
            pool.wait_ge(s_const, 16 * N_CONST)
            p_.tensor_tensor(clsP[:, :], clsB[:, 0, :], clsB[:, 1, :], ALU.add).then_inc(s_cls, 1)
            rows = lambda b_: bc(b_[:, :].rearrange("p (a d) -> p a d", a=1), [128, NH, D])
            for j in range(NH // 2):
                pv = posB[:, j, :].rearrange("p (w d) -> p w d", w=NH)
                p_.tensor_tensor(pv, pv, rows(b2B), ALU.add).then_inc(s_pos, 1)
            for j in range(NH // 2):
                if j + 1 < NH // 2:
                    pool.wait_ge(s_v1, j + 2)
                    rsqrt(rs1[:, j + 1, :], ve1[:, j + 1, :]).then_inc(s_r1, 1)
                pool.wait_ge(s_v2, j + 1)
                rsqrt(rst[:, j, :], vet[:, j, :]).then_inc(s_r2, 1)
                pool.wait_ge(s_tn, j + 1)
                pool.wait_ge(s_pos, j + 1)
                p_.tensor_tensor(zt[:, j], zt[:, j], rows(g2B), ALU.mult)
                pool.drain()
                p_.tensor_tensor(zt[:, j], zt[:, j], posB[:, j, :].rearrange("p (w d) -> p w d", w=NH),
                                 ALU.add).then_inc(s_ht, 1)
            pool.wait_ge(s_aw, 16 * N_AW)

            def ln1(s):
                pool.wait_ge(s_va, s + 1)
                rsqrt(rs[:, :], ve[:, :]).then_inc(s_ra, 1)

            def bias(s):
                pool.wait_ge(s_xn, s + 1)
                hs = h_all[:, bass.ds(2 * s, 2), :]
                p_.tensor_tensor(hs, hs, bc(boB[:, :].rearrange("p (a d) -> p a d", a=1), [G, 2, D]),
                                 ALU.add).then_inc(s_hb, 1)

            def ln2(s):
                for g in range(2):
                    pool.wait_ge(s_vb[g], s + 1)
                    rsqrt(rs2[:, g:g + 1], ve2[:, g:g + 1]).then_inc(s_rb[g], 1)
                for g in range(2):
                    pool.wait_ge(s_xr[g], s + 1)
                    p_.tensor_copy(xr_all[:, 2 * s + g, 0:D], xn2[:, g, :]).then_inc(s_xrc[g], 1)

            ln1(0)
            bias(0)
            ln1(1)
            bias(1)
            with pool.Fori(1, STEPS) as s:
                ln1(s + 1)
                bias(s + 1)
                ln2(s - 1)
            ln2(STEPS - 1)

            for c in s_xrc:
                pool.wait_ge(c, STEPS)
            pool.wait_ge(s_own, 1)
            p_.memset(xe[:, :, :, :], 0.0).then_inc(s_xe0, 1)
            pool.wait_ge(s_fill, 16 * N_FILL)
            for nth, g in enumerate(2 * q + a for q in RANKED for a in range(2)):
                if nth % 2 == 0:
                    pool.wait_ge(s_slot, nth // 2 + 1)
                for k in range(2):
                    p_.indirect_dma_start(xbuf, bass.IndirectOffsetOnAxis(ap=sloti[:, k, g:g + 1], axis=0),
                                          xr_all[:, g, :], None, bounds_check=E * CAP - 1,
                                          oob_is_err=False).then_inc(s_sct, 16)

            def expert(e, p):
                pool.wait_ge(s_eb[p], 32 * (e // 2 + 1))
                pool.wait_ge(s_wsel, e + 1)
                if e >= 2:
                    pool.wait_ge(s_ye, NT * (e - 1))
                for n in range(NT):
                    last = p_.tensor_scalar(wb2[:, p, n, :], b2s[:, p, :], wsel[:, p, n:n + 1], None, ALU.mult)
                last.then_inc(s_wb, 1)
                pool.wait_ge(s_di, e + 1)
                for n in range(NT):
                    r = tile_rows(n)
                    pool.wait_ge(s_ye, e * NT + n + 1)
                    p_.indirect_dma_start(ybuf, bass.IndirectOffsetOnAxis(ap=dsti[0:r, p, n:n + 1], axis=0),
                                          ye[0:r, p, n, :], None, bounds_check=2 * ROWS - 1,
                                          oob_is_err=False).then_inc(s_ys[p], 16)

            for e in range(E):
                expert(e, e % 2)


_INS = ["x", "L0_tok_ln1_g", "L0_tok_ln1_b", "L0_tok_W_lin", "L0_tok_b_lin", "L0_tok_ln2_g", "L0_tok_ln2_b",
        "L0_tok_pos_embedding", "L0_tok_cls_token", "L0_attn_Wq", "L0_attn_Wk", "L0_attn_Wv", "L0_attn_Wrk",
        "L0_attn_r_w_bias", "L0_attn_r_r_bias", "L0_attn_Wo", "L0_attn_bo", "L0_ffn_Wg", "L0_ffn_W1", "L0_ffn_b1",
        "L0_ffn_W2", "L0_ffn_b2"]


def constants():
    f = np.float32
    r = np.arange(G)
    block = (r[:, None] // T == r[None, :] // T).astype(f)
    ind = (r[:, None] // T == np.arange(IPG)[None, :]).astype(f)
    positions = np.arange(-T + 1, T).astype(f)
    nb = F // 2
    widths = np.exp(np.log(T + 1) / nb).astype(f) ** np.arange(1, nb + 1).astype(f) - f(1)
    emb = (widths[None, :] > np.abs(positions)[:, None]).astype(f)
    pos = np.concatenate([emb, np.sign(positions)[:, None] * emb], axis=-1)
    iota = np.stack([np.arange(E), np.arange(E) + E]).astype(f)
    tok = (np.arange(NG)[None, :] * G + r[:, None]).astype(f)
    blank = np.zeros((128, XW), f)
    blank[:, XW - 1] = BIG
    return {
        "c_ident": np.eye(128, dtype=f), "c_block": block, "c_ind": ind, "c_pos": np.ascontiguousarray(pos.T),
        "c_iota": np.ascontiguousarray(np.broadcast_to(iota, (128, 2, E))),
        "c_upper": (r[None, :] > r[:, None]).astype(f), "c_real": (tok < B * T).astype(f), "c_tok": tok,
        "c_blank": blank,
    }


def kernel(**inputs):
    import concourse.bacc as bacc
    from concourse.bass_utils import run_bass_kernel_spmd

    nc = bacc.Bacc("TRN2", target_bir_lowering=False, num_devices=1)
    arrays, args = {}, []
    feed = [(n, np.ascontiguousarray(inputs[n])) for n in _INS] + list(constants().items())
    for name, a in feed:
        if name in ("L0_attn_r_w_bias", "L0_attn_r_r_bias"):
            a = np.ascontiguousarray(a.reshape(HB, 128).T)
        elif name == "L0_attn_Wo":
            a = np.ascontiguousarray(a.reshape(H, V, D)[[head_at(j) for j in range(H)]].reshape(H * V, D))
        elif name in ("L0_tok_ln1_g", "L0_tok_ln1_b"):
            a = np.ascontiguousarray(a.reshape(PC, 128).T)
        elif name == "x":
            a = a.reshape(B, C, NH, PATCH, NH, PATCH).transpose(2, 0, 4, 3, 5, 1)
            a = np.ascontiguousarray(a.reshape(NH, B, NH * PD))
        elif name == "L0_ffn_b1":
            a = np.ascontiguousarray(a.reshape(E, HC, 128).transpose(0, 2, 1))
        arrays[name] = a
        args.append(nc.dram_tensor(name, a.shape, mybir.dt.from_np(a.dtype), kind="ExternalInput").ap())
    args.append(nc.dram_tensor("out", (B * T, D), F32, kind="ExternalOutput").ap())
    build(nc, *args)
    r = run_bass_kernel_spmd(nc, [arrays], core_ids=[0])
    return r.results[0]["out"].reshape(B, T, D)
```

```python
from contextlib import ExitStack

import numpy as np

import concourse.bass as bass
from concourse import mybir

F32 = mybir.dt.float32
BF16 = mybir.dt.bfloat16
F32R = mybir.dt.float32r
I32 = mybir.dt.int32
ALU = mybir.AluOpType
ACT = mybir.ActivationFunctionType
AX = mybir.AxisListType

B, C, IMG, PATCH = 64, 3, 96, 16
NH = IMG // PATCH
D = 192
T = NH * NH + 1
H, K, V, F = 8, 64, 96, 32
R = 2 * T - 1
E, HID = 8, 4 * D
CAP = int(1.25 * B * T * 2 / E)
EPS = 1e-5

IPG = 3
G = IPG * T
NG = -(-B // IPG)
STEPS = NG // 2
ROWS = NG * G
LAST = B * T - (NG - 1) * G
G2 = 2 * G
KD = D // 2
HB = H // 2
WIDE = 640
SKEW = WIDE - 1
REL_IMG = T * SKEW
SPLIT = 96
PD = C * PATCH * PATCH
PC = PD // 128
XF = NH * PD
TAIL = 4
XW = D + TAIL
NT = -(-CAP // 128)
HALF = CAP // 2
HC = HID // 128
NQKV = 2 * H * K + H * V
HIGH_BY_DVE = (1, 3)
N_EARLY, N_CONST, N_QKV, N_AW = 5, 18, 12, 7
UNITS = NH * NH // 2
NF = NH // 2
N_FILL = 2
BY_ACT = ((10, 14), (14, NG))
ND = BY_ACT[0][0]
RANKED = [0, 1, 5, 6, 2, 3, 7, 4, 8, 9, 10]
SLOTS_AFTER = {2: (0,), 4: (1,), 5: (2, 3), 7: (4,), 8: (5,), 9: (6,)}
OWN_BEFORE = {0: (0, 4), 4: (10, 14), 5: (4, 10), 8: (14, NG)}
HALF_ULP = 2.0 ** -25
BIG = 1.0e6
assert NG % 2 == 0 and 36 * WIDE + H * R <= REL_IMG


BLOCKS = ((0, 0), (0, 1), (0, 2), (1, 0), (1, 1))


def head_at(j):
    return j % HB * 2 + j // HB


def is_step(s, n):
    return isinstance(s, int) and s == n


def tile_rows(i):
    return min(128, CAP - 128 * i)


def build(nc, x, ln1_g, ln1_b, W_lin, b_lin, ln2_g, ln2_b, pos_embedding, cls_token,
          Wq, Wk, Wv, Wrk, r_w_bias, r_r_bias, Wo, bo, Wg, W1, b1, W2, b2,
          c_ident, c_block, c_ind, c_pos, c_iota, c_upper, c_real, c_tok, c_blank, out):
    h_dram = nc.dram_tensor("h_tokens", [ROWS, D], F32).ap()
    rel_dram = nc.dram_tensor("rel_scores", [NG * IPG * REL_IMG + WIDE], F32).ap()
    xbuf = nc.dram_tensor("routed_rows", [E * CAP, XW], F32).ap()

    with ExitStack() as ctx:
        def sb(name, shape, dt=F32):
            return ctx.enter_context(nc.sbuf_tensor(name, shape, dt))

        phase = ctx.enter_context(ExitStack())

        def early(name, shape, dt=F32):
            return phase.enter_context(nc.sbuf_tensor(name, shape, dt))

        def sem(name):
            return ctx.enter_context(nc.semaphore(name))

        PS = ctx.enter_context(nc.psum_tensor("PS", [128, 8, 512], F32))

        ident = sb("ident", [128, 128])
        eidx = sb("eidx", [128, E])
        one_row = sb("one_row", [1, 128])
        h_all = sb("h_all", [G, NG + 2, D])
        b1s = sb("b1s", [128, 2, HC])
        b2r = sb("b2r", [1, 2, D])
        first = sb("first", [128, 2, NT])
        wsel = sb("wsel", [128, 2, NT])
        wtmp = sb("wtmp", [128, 2, NT])
        dsti = sb("dsti", [128, 2, NT], I32)

        wh = early("wh", [128, 3, NQKV], F32R)
        wl = early("wl", [128, 2, NQKV], F32R)
        wide = early("wide", [128, (NH // 2) * XF])

        block = early("block", [G, G])
        ind = early("ind", [G, IPG])
        pos_f = early("pos_f", [F, R])
        iota8 = early("iota8", [G, 2, E])
        upper = early("upper", [G, G])
        real = early("real", [G, NG])
        tok = early("tok", [G, NG])
        blank = early("blank", [128, XW])
        ones = early("ones", [128, 128])
        zeros = early("zeros", [128, D])
        meanw = early("meanw", [128, 128])
        g1 = early("g1", [128, PC])
        bb1 = early("bb1", [128, PC])
        blin = early("blin", [1, D])
        cB = early("cB", [128, D])
        g2B = early("g2B", [128, D])
        b2B = early("b2B", [128, D])
        xT = early("xT", [128, 3, G2], F32R)
        wrk = early("wrk", [F, H * K])
        rk = early("rk", [128, HB, R])
        rwb = early("rwb", [128, HB])
        rrb = early("rrb", [128, HB])
        wo = early("wo", [128, HC, D])
        boB = early("boB", [G, D])
        wg = early("wg", [KD, 2, E])

        def carve(memory):
            at = [0]

            def piece(parts, n, dt=F32):
                words = n if dt is F32 else n // 2
                a, at[0] = at[0], at[0] + words
                assert at[0] <= memory.shape[1]
                v = memory[0:parts, a:a + words]
                return v if dt is F32 else v.bitcast(dt)
            return piece

        xv = wide[:, :].rearrange("p (j w f) -> p j w f", j=NH // 2, w=NH)
        piece = carve(wide)
        wraw = piece(128, 3 * NQKV).rearrange("p (b n) -> p b n", b=3)
        piece = carve(wide)
        qw = piece(128, HB * G2).rearrange("p (m n) -> p m n", m=HB)
        qr = piece(128, HB * G2).rearrange("p (m n) -> p m n", m=HB)
        kT = piece(128, HB * G2).rearrange("p (m n) -> p m n", m=HB)
        v_sb = piece(G, 2 * H * V).rearrange("p (g n) -> p g n", g=2)
        rel = piece(G, 2 * H * R).rearrange("p (g n) -> p g n", g=2)
        relw = piece(G, 2 * H * T).rearrange("p (g n) -> p g n", g=2)
        sc = piece(G, 2 * H * T).rearrange("p (g n) -> p g n", g=2)
        pb = piece(G, 2 * H * G).rearrange("p (g n) -> p g n", g=2)
        pT = piece(G, 2 * H * G).rearrange("p (g n) -> p g n", g=2)
        o_sb = piece(G, 2 * H * V).rearrange("p (g n) -> p g n", g=2)
        piece = carve(wide)
        prow = piece(G, ROWS)
        lot_size = [end - start for start, end in BY_ACT]
        sgn = [None, piece(G, lot_size[1] * ROWS, BF16).rearrange("p (j i n) -> p j i n", j=lot_size[1], i=NG)]

        bn1 = early("bn1", [128, NH // 2, NH, 2, 6])
        mv1 = early("mv1", [128, NH // 2, NH, 2])
        ve1 = early("ve1", [128, NH // 2, NH])
        rs1 = early("rs1", [128, NH // 2, NH])
        bnt = early("bnt", [128, NH // 2, NH, 6])
        mvt = early("mvt", [128, NH // 2, NH, 2])
        vet = early("vet", [128, NH // 2, NH])
        rst = early("rst", [128, NH // 2, NH])
        nhalf = early("nhalf", [128, NH])
        xr_all = early("xr_all", [G, NG, XW])
        xn = early("xn", [G, 2, D])
        xn2 = early("xn2", [G, 2, D])
        xnT = early("xnT", [KD, 2, G2])
        st = early("st", [G, 6])
        mv = early("mv", [G, 2, 2])
        ve = early("ve", [G, 2])
        rs = early("rs", [G, 2])
        st2 = early("st2", [G, 6])
        mv2 = early("mv2", [G, 2, 2])
        ve2 = early("ve2", [G, 2])
        rs2 = early("rs2", [G, 2])
        mx = early("mx", [G, 2, H])
        rsum = early("rsum", [G, 2, H])
        rinv = early("rinv", [G, 2, H])
        logit = early("logit", [G, NG, E])
        m1 = early("m1", [G, NG])
        m2 = early("m2", [G, NG])
        i1 = early("i1", [G, NG])
        i2 = early("i2", [G, NG])
        oh = early("oh", [G, 2, NG, E])
        ohb = early("ohb", [G, NG, E], BF16)
        tmp8 = early("tmp8", [G, NG, E])
        l2 = early("l2", [G, NG, E])
        ex = early("ex", [G, NG])
        w01 = early("w01", [G, 2, NG])
        prio = early("prio", [G, NG])
        prio_up = early("prio_up", [G, NG])
        prio_dn = early("prio_dn", [G, NG])
        lower_by = early("lower_by", [G, G])
        ohh = early("ohh", [G, NG, E], BF16)
        ohn = early("ohn", [G, NG, E], BF16)
        ohs = early("ohs", [G, E])
        ohsb = early("ohsb", [G, E], BF16)
        onesb = early("onesb", [G, G], BF16)
        base = early("base", [G, 2, NG])
        tmp4 = early("tmp4", [G, 2, 2, E])
        posk = early("posk", [G, 2, NG])
        keep = early("keep", [G, 2, NG])
        slot = early("slot", [G, 2, NG])
        sloti = early("sloti", [G, 2, NG], I32)

        narrow_stage = ExitStack()
        phase.enter_context(narrow_stage)
        narrow = narrow_stage.enter_context(nc.sbuf_tensor("narrow", [128, 60 * D], F32))
        piece = carve(narrow)
        W_raw = piece(128, PC * D).rearrange("p (c d) -> p c d", c=PC)
        W_cen = piece(128, PC * D).rearrange("p (c d) -> p c d", c=PC)
        posB = piece(128, NH * NH // 2 * D).rearrange("p (j n) -> p j n", j=NH // 2)
        xTt = piece(128, 2 * 6 * 128).rearrange("p (a c n) -> p a c n", a=2, c=6)
        zt = piece(128, UNITS * D).rearrange("p (j w d) -> p j w d", j=NH // 2, w=NH)
        clsB = piece(64, 2 * D).rearrange("p (a d) -> p a d", a=2)
        clsP = piece(64, D)
        piece = carve(narrow)
        nudged = piece(G, ROWS).rearrange("p (j n) -> p j n", j=NG)
        own = piece(G, ROWS, BF16).rearrange("p (j n) -> p j n", j=NG)
        before = [piece(G, ROWS, BF16).rearrange("p (i n) -> p i n", i=NG) for _ in range(2)]
        sgn[0] = piece(G, lot_size[0] * ROWS, BF16).rearrange("p (j i n) -> p j i n", j=lot_size[0], i=NG)

        narrow_stage.close()
        woh = early("woh", [128, HC, D], F32R)
        wol = early("wol", [128, HC, D], F32R)
        oTh = early("oTh", [128, 2, HC * G], F32R)
        oTl = early("oTl", [128, 2, HC * G], F32R)

        phase.close()
        w1r = sb("w1r", [128, 3, HID])
        w2r = sb("w2r", [128, HC, D])
        xe = sb("xe", [128, 2, NT, XW])
        w1h = sb("w1h", [128, 3, HID], F32R)
        w1l = sb("w1l", [128, 2, HID], F32R)
        w2hl = sb("w2hl", [128, HC, 2, D], F32R)
        b2hl = sb("b2hl", [1, 2, D], F32R)
        onesr = sb("onesr", [1, 128], F32R)
        xeT = sb("xeT", [128, 3, CAP], F32R)
        hTh = sb("hTh", [128, HC, CAP], F32R)
        hTl = sb("hTl", [128, HC, CAP], F32R)
        hf = sb("hf", [128, 2, CAP])
        ye = sb("ye", [128, 2, NT, D])
        acc = sb("acc", [128, 2, NT, D])

        s_const = sem("const_loaded")
        s_early = sem("tok_weights_loaded")
        s_x = [[sem(f"x_loaded{j}_{f}") for f in range(2)] for j in range(NH // 2)]
        s_aw = sem("attn_weights_loaded")
        s_set = sem("memsets_done")
        s_setv = sem("dve_consts_done")
        s_gw = sem("gw_done")
        s_mean = sem("colmean_psum")
        s_rkp = sem("rk_psum")
        s_wc = sem("w_centred")
        s_rk = sem("rk_ready")
        s_xrc = [sem(f"routed_rows_copied{g}") for g in range(2)]
        s_cls = sem("cls_ready")
        s_tT = sem("tok_transposed")
        s_tTa = sem("tok_evac_act")
        s_tz = sem("tok_product")
        s_tze = sem("tok_product_used")
        s_v1 = sem("tok_var1")
        s_r1 = sem("tok_rstd1")
        s_v2 = sem("tok_var2")
        s_r2 = sem("tok_rstd2")
        s_tn = sem("tok_normed")
        s_pos = sem("positions_ready")
        s_hb = sem("h_with_bias")
        s_wsel = sem("routing_weights_ready")
        s_ht = sem("tok_rows_ready")
        s_ht_last = sem("last_tok_rows_ready")
        s_brow = sem("bias_row_psum")
        s_cb = sem("bias_row_copied")
        s_ho = [sem(f"tok_rows_stored{j}") for j in range(NH // 2)]
        s_fill = sem("dram_prefilled")
        s_h = sem("h_loaded")
        s_va = sem("ln1_var")
        s_ra = sem("ln1_rstd")
        s_xn = sem("ln1_rows")
        s_xTp = sem("xT_psum")
        s_xTh = sem("xT_high")
        s_xT = sem("xT_ready")
        s_qkv = sem("qkv_weights_loaded")
        s_wh = sem("qkv_weights_high")
        s_wl = sem("qkv_weights_low")
        s_qp = sem("q_psum")
        s_kp = sem("k_psum")
        s_qr = sem("q_for_relative_ready")
        s_q = sem("q_ready")
        s_k = sem("k_ready")
        s_rp = [sem(f"rel_psum{g}") for g in range(2)]
        s_re = [sem(f"rel_evacuated{g}") for g in range(2)]
        s_ro = [sem(f"rel_stored{g}") for g in range(2)]
        s_ri = [sem(f"rel_skewed{g}") for g in range(2)]
        s_vp = [sem(f"v_psum{g}") for g in range(2)]
        s_v = [sem(f"v_ready{g}") for g in range(2)]
        s_sp = [sem(f"scores_psum{g}") for g in range(2)]
        s_sc = [sem(f"scores_compact{g}") for g in range(2)]
        s_sh = [sem(f"scores_shifted{g}") for g in range(2)]
        s_p = [sem(f"probs_ready{g}") for g in range(2)]
        s_ptp = [sem(f"pT_psum{g}") for g in range(2)]
        s_pt = [sem(f"pT_ready{g}") for g in range(2)]
        s_op = [sem(f"o_psum{g}") for g in range(2)]
        s_o = [sem(f"o_ready{g}") for g in range(2)]
        s_otp = [sem(f"oT_psum{g}") for g in range(2)]
        s_oth = [sem(f"oT_high{g}") for g in range(2)]
        s_woh = sem("wo_high")
        s_wol = sem("wo_low")
        s_ot = [sem(f"oT_ready{g}") for g in range(2)]
        s_wop = [sem(f"proj_psum{g}") for g in range(2)]
        s_h1 = [sem(f"h1_ready{g}") for g in range(2)]
        s_vb = [sem(f"ln2_var{g}") for g in range(2)]
        s_rb = [sem(f"ln2_rstd{g}") for g in range(2)]
        s_xr = [sem(f"ln2_rows{g}") for g in range(2)]
        s_xrp = sem("xnT_psum")
        s_xrT = sem("xnT_ready")
        s_lp = sem("logits_psum")
        s_l = sem("logits_ready")
        s_d = sem("gap_ready")
        s_e = sem("gap_exp")
        s_prio = sem("prio_ready")
        s_pbp = sem("prio_rows_psum")
        s_pb = sem("prio_rows_ready")
        s_bef = sem("before_ready")
        s_cnt = sem("before_counted")
        s_nudge = sem("nudged_prios_ready")
        s_sgn = sem("signs_ready")
        s_own = sem("own_tiles_ready")
        s_pba = sem("prio_rows_ready_act")
        s_xe0 = sem("expert_rows_cleared")
        s_slot = sem("slots_ready")
        s_sct = sem("rows_scattered")
        s_ex = [sem(f"expert_rows_loaded{p}") for p in range(2)]
        s_eb = [sem(f"expert_biases_loaded{p}") for p in range(2)]
        s_w1r = sem("w1_loaded")
        s_w2r = sem("w2_loaded")
        s_w1h = sem("w1_high")
        s_w1l = sem("w1_low")
        s_w2h = sem("w2_high")
        s_w2l = sem("w2_low")
        s_xep = sem("xeT_psum")
        s_xeh = sem("xeT_high")
        s_xel = sem("xeT_low")
        s_hp = sem("hidden_psum")
        s_hg = sem("hidden_ready")
        s_hl = sem("hidden_low_ready")
        s_yp = sem("y_psum")
        s_ye = sem("y_scaled")
        s_di = sem("dest_ready")
        s_zw = sem("w1_low_zeros")
        s_acc0 = sem("sums_cleared")
        s_acc = sem("sums_gathered")
        s_ys = sem("y_scattered")
        s_out = sem("out_started")

        def bc(ap, shape):
            return ap.to_broadcast(shape)

        def heads(bank, n):
            return PS[0:G, bank:bank + 2, :].rearrange("p a (h t) -> p (a h) t", h=HB)[:, :, 0:n]

        def hidden_bank(c):
            return 2 + 2 * (c % 3)

        def both_banks(bank):
            return PS[:, bank:bank + 2, :].rearrange("p a n -> p (a n)")[:, 0:CAP]

        blk = ctx.enter_context(nc.Block())

        @blk.sync
        def _(sp):
            def load_x(j):
                for f in range(2):
                    for u in range(2):
                        sp.dma_start(wide[64 * u:64 * u + 64, j * XF + f * (XF // 2):j * XF + (f + 1) * (XF // 2)],
                                     x[2 * j + u][:, f * (XF // 2):(f + 1) * (XF // 2)]).then_inc(s_x[j][f], 16)

            sp.dma_start(W_raw[:, :, :], W_lin.rearrange("(c p) d -> p c d", p=128)).then_inc(s_early, 16)
            sp.dma_start(g1[:, :], ln1_g).then_inc(s_early, 16)
            sp.dma_start(bb1[:, :], ln1_b).then_inc(s_early, 16)
            row = lambda ap: ap.rearrange("(a d) -> a d", a=1)
            sp.dma_start(blin[:, :], row(b_lin)).then_inc(s_early, 16)
            sp.dma_start(ident[:, :], c_ident).then_inc(s_early, 16)
            load_x(0)
            load_x(1)
            sp.dma_start(block[:, :], c_block).then_inc(s_const, 16)
            sp.dma_start(ind[:, :], c_ind).then_inc(s_const, 16)
            sp.dma_start(pos_f[:, :], c_pos).then_inc(s_const, 16)
            sp.dma_start(iota8[:, :, :], c_iota[0:G]).then_inc(s_const, 16)
            sp.dma_start(eidx[:, :], c_iota[:, 0, :]).then_inc(s_const, 16)
            sp.dma_start(upper[:, :], c_upper).then_inc(s_const, 16)
            sp.dma_start(real[:, :], c_real).then_inc(s_const, 16)
            sp.dma_start(blank[:, :], c_blank).then_inc(s_const, 16)
            sp.dma_start(g2B[:, :], bc(row(ln2_g), [128, D])).then_inc(s_const, 16)
            sp.dma_start(b2B[:, :], bc(row(ln2_b), [128, D])).then_inc(s_const, 16)
            for n in range(NH):
                src = pos_embedding[0, 1 + n * NH:1 + (n + 1) * NH, :].rearrange("(a t) d -> a (t d)", a=1)
                sp.dma_start(posB[64 * (n % 2):64 * (n % 2) + 64, n // 2, :],
                             bc(src, [64, NH * D])).then_inc(s_const, 16)
            sp.dma_start(clsB[:, 0, :], bc(cls_token[0], [64, D])).then_inc(s_const, 16)
            sp.dma_start(clsB[:, 1, :], bc(pos_embedding[0, 0:1, :], [64, D])).then_inc(s_const, 16)
            load_x(2)
            sp.dma_start(wrk[:, :], Wrk).then_inc(s_aw, 16)
            sp.dma_start(rwb[:, :], r_w_bias).then_inc(s_aw, 16)
            sp.dma_start(rrb[:, :], r_r_bias).then_inc(s_aw, 16)
            sp.dma_start(wo[:, :, :], Wo.rearrange("(c p) d -> p c d", p=128)).then_inc(s_aw, 16)
            sp.dma_start(boB[:, :], bc(row(bo), [G, D])).then_inc(s_aw, 16)
            sp.dma_start(wg[:, :, :], Wg.rearrange("(k p) n -> p k n", k=2)).then_inc(s_aw, 16)
            sp.dma_start(tok[:, :], c_tok).then_inc(s_aw, 16)

            sp.wait_ge(s_set, 1)
            sp.wait_ge(s_const, 16 * N_CONST)
            n0 = E * CAP // 128 * 128
            sp.dma_start(xbuf[0:n0].rearrange("(p n) w -> p n w", p=128),
                         bc(blank[:, :].rearrange("p (a w) -> p a w", a=1), [128, n0 // 128, XW])).then_inc(s_fill, 16)
            sp.dma_start(xbuf[n0:E * CAP], blank[0:E * CAP - n0, :]).then_inc(s_fill, 16)

            hv = h_dram[0:B * T, :].rearrange("(b t) d -> b t d", t=T)
            for j in range(NH // 2):
                for f in range(2):
                    if (j, f) == (NH // 2 - 1, 1):
                        sp.wait_ge(s_ht_last, 1)
                    else:
                        sp.wait_ge(s_ht, 2 * j + f + 1)
                    for u in range(2):
                        t0 = 1 + (2 * j + u) * NH + f * NF
                        sp.dma_start(hv[:, t0:t0 + NF, :].rearrange("b t d -> b (t d)"),
                                     zt[64 * u:64 * u + 64, j, f * NF:(f + 1) * NF].rearrange("p t d -> p (t d)")
                                     ).then_inc(s_ho[j], 16)
                if j == 0:
                    sp.wait_ge(s_cls, 1)
                    sp.dma_start(hv[:, 0, :], clsP[:, :]).then_inc(s_ho[0], 16)
                    sp.dma_start(h_dram[B * T:ROWS, :], zeros[0:ROWS - B * T, 0:D]).then_inc(s_ho[0], 16)
                    sp.wait_ge(s_tT, 3 * NH // 2)
                    sp.wait_ge(s_v1, 2)
                    at = 0
                    for W in (Wq, Wk, Wv):
                        n = W.shape[1]
                        for p0, b_, r0, rows_ in ((0, 0, 0, 128), (0, 1, 0, 64), (64, 1, 128, 64), (0, 2, 64, 128)):
                            sp.dma_start(wraw[p0:p0 + rows_, b_, at:at + n], W[r0:r0 + rows_]).then_inc(s_qkv, 16)
                        at += n
            for j in range(NH // 2):
                sp.wait_ge(s_ho[j], 96 if j == 0 else 64)

            hg = h_dram.rearrange("(g p) d -> p g d", p=G)
            for a, b_ in ((0, 2), (2, NG)):
                sp.dma_start(h_all[0:SPLIT, a:b_], hg[0:SPLIT, a:b_]).then_inc(s_h, 16)
                sp.dma_start(h_all[SPLIT:G, a:b_], hg[SPLIT:G, a:b_]).then_inc(s_h, 16)
                sp.wait_ge(s_h, 32 if a == 0 else 64)

            def rows_of(start, n, pitch):
                return rel_dram[bass.ds(start, n * pitch)].rearrange("(p w) -> p w", w=pitch)[:, 0:H * R]

            def rel_roundtrip(s):
                for g in range(2):
                    base = (2 * s + g) * (IPG * REL_IMG)
                    sp.wait_ge(s_re[g], s + 1)
                    for i in range(IPG):
                        for t0, t1 in ((0, 32), (32, T)):
                            sp.dma_start(rows_of(base + i * REL_IMG + t0 * WIDE, t1 - t0, WIDE),
                                         rel[i * T + t0:i * T + t1, g, :]).then_inc(s_ro[g], 16)
                for g in range(2):
                    base = (2 * s + g) * (IPG * REL_IMG) + T - 1
                    sp.wait_ge(s_ro[g], 16 * 6 * (s + 1))
                    if not isinstance(s, int) or s:
                        sp.wait_ge(s_sc[g], s)
                    for p0, p1 in ((0, SPLIT), (SPLIT, G)):
                        sp.dma_start(relw[p0:p1, g, :].rearrange("p (h t) -> p h t", h=H),
                                     rows_of(base + p0 * SKEW, p1 - p0, SKEW).rearrange(
                                         "p (h r) -> p h r", h=H)[:, :, 0:T]).then_inc(s_ri[g], 16)

            rel_roundtrip(0)
            with sp.Fori(1, STEPS) as s:
                rel_roundtrip(s)

            def load_w1(e):
                w = W1[bass.ds(e, 1)]
                half = w.rearrange("a (c p) n -> p (a c) n", p=64)
                sp.dma_start(w1r[:, 0, :], w.rearrange("a d n -> d (a n)")[0:128]).then_inc(s_w1r, 16)
                sp.dma_start(w1r[0:64, 1, :], half[:, 0, :]).then_inc(s_w1r, 16)
                sp.dma_start(w1r[64:128, 1, :], half[:, 2, :]).then_inc(s_w1r, 16)
                sp.dma_start(w1r[:, 2, :], w.rearrange("a d n -> d (a n)")[64:192]).then_inc(s_w1r, 16)

            def load_w2(e):
                sp.dma_start(w2r[:, :, :], W2[bass.ds(e, 1)].rearrange("a (c p) d -> p (a c) d", p=128)
                             ).then_inc(s_w2r, 16)

            def load_biases(e, p):
                sp.dma_start(b1s[:, p], b1[bass.ds(e, 1)].rearrange("a p c -> p (a c)")).then_inc(s_eb[p], 16)
                sp.dma_start(b2r[:, p], b2[bass.ds(e, 1)]).then_inc(s_eb[p], 16)

            def load_rows(e, p):
                full = CAP // 128
                sp.dma_start(xe[:, p, 0:full],
                             xbuf[bass.ds(e * CAP, full * 128)].rearrange("(n q) w -> q n w", q=128)
                             ).then_inc(s_ex[p], 16)
                sp.dma_start(xe[0:CAP - full * 128, p, full],
                             xbuf[bass.ds(e * CAP + full * 128, CAP - full * 128)]).then_inc(s_ex[p], 16)

            for g in range(2):
                sp.wait_ge(s_h1[g], STEPS)
            og = out[0:(NG - 1) * G].rearrange("(g p) d -> p g d", p=G)
            for p0, p1 in ((0, SPLIT), (SPLIT, G)):
                sp.dma_start(og[p0:p1], h_all[p0:p1, 0:NG - 1]).then_inc(s_out, 16)
            for p0, p1 in ((0, LAST // 16 * 16), (LAST // 16 * 16, LAST)):
                sp.dma_start(out[(NG - 1) * G + p0:(NG - 1) * G + p1], h_all[p0:p1, NG - 1]).then_inc(s_out, 16)
            load_w1(0)
            load_w2(0)
            for p in range(2):
                load_biases(p, p)
            sp.wait_ge(s_sct, 16 * 2 * NG)
            sp.wait_ge(s_xe0, 1)
            for p in range(2):
                load_rows(p, p)

            def load_next(e, p, more):
                sp.wait_ge(s_w1h, e)
                sp.wait_ge(s_w1l, e)
                load_w1(e)
                sp.wait_ge(s_w2h, e)
                sp.wait_ge(s_w2l, e)
                load_w2(e)
                if more:
                    sp.wait_ge(s_di, e)
                    sp.wait_ge(s_xep, e)
                    load_rows(e + 1, 1 - p)
                    sp.wait_ge(s_hg, e * HC)
                    sp.wait_ge(s_w2l, e)
                    load_biases(e + 1, 1 - p)

            load_next(1, 1, True)
            with sp.Fori(1, E // 2 - 1) as i:
                load_next(i * 2, 0, True)
                load_next(i * 2 + 1, 1, True)
            load_next(E - 2, 0, True)
            load_next(E - 1, 1, False)

            sp.wait_ge(s_fill, 16 * N_FILL)
            sp.wait_ge(s_ys, 16 * NT * E)

        @blk.tensor
        def _(pe):
            pe.wait_ge(s_early, 16 * N_EARLY)
            pe.wait_ge(s_set, 2)
            pe.wait_ge(s_gw, 1)
            for c in range(PC):
                last = pe.matmul(PS[:, 6, 0:D], meanw[:, :], W_cen[:, c, :], start=(c == 0), stop=(c == PC - 1))
            last.then_inc(s_mean, 1)

            units = [(j, w) for j in range(NH // 2) for w in range(NH)]

            def tok_transpose(u):
                j, w = units[u]
                if w % (NH // 2) == 0:
                    pe.wait_ge(s_x[j][w // (NH // 2)], 32)
                if u >= 2:
                    pe.wait_ge(s_tTa, u - 1)
                for c in range(PC):
                    last = pe.transpose(PS[:, 2 * (u % 2) + c // 3, 128 * (c % 3):128 * (c % 3) + 128],
                                        xv[:, j, w, 128 * c:128 * c + 128], ident[:, :])
                last.then_inc(s_tT, 1)

            def tok_product(u):
                pe.wait_ge(s_tTa, u + 1)
                if u == 3:
                    pe.wait_ge(s_cb, 1)
                if u >= 4:
                    pe.wait_ge(s_tze, u - 3)
                for c in range(PC):
                    last = pe.matmul(PS[:, 4 + u % 4, 0:D], xTt[:, u % 2, c, :], W_cen[:, c, :],
                                     start=(c == 0), stop=(c == PC - 1))
                last.then_inc(s_tz, 1)

            tok_transpose(0)
            for c in range(PC):
                pe.matmul(PS[:, 7, 0:D], bc(bb1[:, c:c + 1], [128, 128]), W_raw[:, c, :], start=(c == 0), stop=False)
            pe.matmul(PS[:, 7, 0:D], ones[0:1, :], blin[:, :], start=False, stop=True).then_inc(s_brow, 1)
            pe.wait_ge(s_wc, 1)
            for u in range(len(units)):
                if u + 1 < len(units):
                    tok_transpose(u + 1)
                tok_product(u)

            pe.wait_ge(s_tze, UNITS)
            pe.wait_ge(s_const, 16 * N_CONST)
            pe.wait_ge(s_aw, 16 * N_AW)
            for m in range(HB):
                last = pe.matmul(PS[:, 6, m * R:(m + 1) * R], wrk[:, m * 128:(m + 1) * 128], pos_f[:, :],
                                 start=(m == 0), stop=(m == HB - 1), skip_group_check=True)
            last.then_inc(s_rkp, 1)

            def rows_transposed(s):
                pe.wait_ge(s_xn, s + 1)
                if not is_step(s, 0):
                    pe.wait_ge(s_v[1], s)
                for g in range(2):
                    for k in range(2):
                        last = pe.transpose(PS[:, 2, k * G2 + g * G:k * G2 + (g + 1) * G],
                                            xn[:, g, k * 64:k * 64 + 128], ident[0:G, 0:G])
                last.then_inc(s_xTp, 1)

            def project(m2, w0, bank, done):
                for m in (2 * m2, 2 * m2 + 1):
                    for nth, (w, b_) in enumerate(BLOCKS):
                        lhsT = (wh, wl)[w][:, b_, w0 + m * 128:w0 + (m + 1) * 128]
                        last = pe.matmul(PS[:, bank, (m % 2) * G2:(m % 2 + 1) * G2], lhsT, xT[:, b_, :],
                                         start=(nth == 0 and m % 2 == 0), stop=(nth == len(BLOCKS) - 1),
                                         skip_group_check=True)
                last.then_inc(done, 1)

            def relative(g):
                for h in range(H):
                    q0 = 64 * (h % 2)
                    last = pe.matmul(PS[0:G, (6, 0)[g] + h % 2, (h // 2) * R:(h // 2 + 1) * R],
                                     qr[q0:q0 + 64, h // 2, g * G:(g + 1) * G], rk[q0:q0 + 64, h // 2, :],
                                     start=(h // 2 == 0), stop=True, skip_group_check=True)
                last.then_inc(s_rp[g], 1)

            def probs_transposed(g):
                for j in range(H):
                    last = pe.transpose(heads(4 - 2 * g, G)[:, j, :], pb[:, g, j * G:(j + 1) * G], ident[0:G, 0:G])
                last.then_inc(s_ptp[g], 1)

            def probs_values(g):
                for j in range(H):
                    h = head_at(j)
                    last = pe.matmul(heads(4 - 2 * g, V)[:, j, :],
                                     pT[:, g, j * G:(j + 1) * G], v_sb[:, g, h * V:(h + 1) * V],
                                     start=(j % HB == 0), stop=True, skip_group_check=True)
                last.then_inc(s_op[g], 1)

            def outputs_transposed(g):
                for c in range(HC):
                    last = pe.transpose(PS[:, (6, 4)[g] + c // 3, (c % 3) * G:(c % 3 + 1) * G],
                                        o_sb[:, g, c * 128:(c + 1) * 128], ident[0:G, 0:G])
                last.then_inc(s_otp[g], 1)

            def output_product(g):
                for c in range(HC):
                    at = slice(c * G, (c + 1) * G)
                    pe.matmul(PS[0:G, g, 0:D], oTh[:, g, at], woh[:, c, :], start=(c == 0), stop=False)
                    pe.matmul(PS[0:G, g, 0:D], oTh[:, g, at], wol[:, c, :], start=False, stop=False)
                    last = pe.matmul(PS[0:G, g, 0:D], oTl[:, g, at], woh[:, c, :], start=False, stop=(c == HC - 1))
                last.then_inc(s_wop[g], 1)

            def values(g):
                for n in range(2):
                    at = 2 * H * K + n * HB * V
                    for nth, (w, b_) in enumerate(BLOCKS):
                        last = pe.matmul(PS[0:G, 2 * g + n, 0:HB * V], xT[:, b_, g * G:(g + 1) * G],
                                         (wh, wl)[w][:, b_, at:at + HB * V],
                                         start=(nth == 0), stop=(nth == len(BLOCKS) - 1))
                last.then_inc(s_vp[g], 1)

            def content(g):
                for h in range(H):
                    q0 = 64 * (h % 2)
                    last = pe.matmul(heads(4 + 2 * g, G)[:, h % 2 * HB + h // 2, :],
                                     qw[q0:q0 + 64, h // 2, g * G:(g + 1) * G],
                                     kT[q0:q0 + 64, h // 2, g * G:(g + 1) * G],
                                     start=(h // 2 == 0), stop=True, skip_group_check=True)
                last.then_inc(s_sp[g], 1)

            def gate_rows(s):
                for g in range(2):
                    pe.wait_ge(s_xr[g], s + 1)
                    for k in range(2):
                        last = pe.transpose(PS[0:KD, 3, k * G2 + g * G:k * G2 + (g + 1) * G],
                                            xn2[:, g, k * KD:(k + 1) * KD], ident[0:G, 0:G])
                last.then_inc(s_xrp, 1)

            def gate(s):
                pe.wait_ge(s_xrT, s + 1)
                for g in range(2):
                    for k in range(2):
                        last = pe.matmul(PS[0:G, 3, g * E:(g + 1) * E], xnT[:, k, g * G:(g + 1) * G], wg[:, k, :],
                                         start=(g == 0 and k == 0), stop=(k == 1), skip_group_check=True)
                last.then_inc(s_lp, 1)

            def step(s):
                here = not is_step(s, STEPS)
                before_ = not is_step(s, 0)
                before2 = before_ and not is_step(s, 1)
                if here:
                    pe.wait_ge(s_xT, s + 1)
                    if before2:
                        pe.wait_ge(s_h1[1], s - 1)
                    elif before_:
                        pe.wait_ge(s_v[0], s)
                    project(0, 0, 1, s_qp)
                    project(0, H * K, 2, s_kp)
                if before2:
                    gate(s - 2)
                if here:
                    if before2:
                        pe.wait_ge(s_h1[0], s - 1)
                    project(1, 0, 0, s_qp)
                    if before2:
                        pe.wait_ge(s_l, s - 1)
                    elif before_:
                        pe.wait_ge(s_v[1], s)
                    project(1, H * K, 3, s_kp)
                if before_:
                    pe.wait_ge(s_p[0], s)
                    probs_transposed(0)
                if here:
                    pe.wait_ge(s_qr, s + 1)
                    if before_:
                        pe.wait_ge(s_sc[1], s)
                    else:
                        pe.wait_ge(s_rk, 1)
                    relative(0)
                if before_:
                    pe.wait_ge(s_p[1], s)
                    if here:
                        pe.wait_ge(s_k, s * 2 + 2)
                    else:
                        pe.wait_ge(s_xT, s + 1)
                        pe.wait_ge(s_l, s - 1)
                    probs_transposed(1)
                if here:
                    pe.wait_ge(s_q, s + 1)
                    relative(1)
                if before_:
                    for g in range(2):
                        pe.wait_ge(s_pt[g], s)
                        pe.wait_ge(s_v[g], s)
                        probs_values(g)
                    pe.wait_ge(s_o[0], s)
                    if here:
                        pe.wait_ge(s_re[0], s + 1)
                    else:
                        pe.wait_ge(s_sc[1], s)
                    outputs_transposed(0)
                if here:
                    pe.wait_ge(s_re[1], s + 1)
                    values(0)
                if before_:
                    pe.wait_ge(s_o[1], s)
                    outputs_transposed(1)
                if here:
                    if not before_:
                        pe.wait_ge(s_k, 2)
                    values(1)
                if before_:
                    for g in range(2):
                        pe.wait_ge(s_ot[g], s)
                        if here:
                            pe.wait_ge(s_v[0], s + 1)
                        else:
                            pe.wait_ge(s_h1[g], s - 1)
                        output_product(g)
                if here:
                    rows_transposed(s + 1)
                    pe.wait_ge(s_k, s * 2 + 2)
                    if before_:
                        pe.wait_ge(s_ot[1], s)
                    content(0)
                    if before_:
                        pe.wait_ge(s_ot[0], s)
                    else:
                        pe.wait_ge(s_re[0], 1)
                    content(1)
                if before_:
                    if not here:
                        pe.wait_ge(s_o[1], s)
                    gate_rows(s - 1)

            rows_transposed(0)
            pe.wait_ge(s_wh, 1)
            pe.wait_ge(s_wl, 1)
            step(0)
            pe.wait_ge(s_woh, 1)
            pe.wait_ge(s_wol, 1)
            step(1)
            with pe.Fori(2, STEPS) as s:
                step(s)
            step(STEPS)
            gate(STEPS - 1)

            pe.wait_ge(s_prio, 1)
            for g in range(NG):
                last = pe.transpose(PS[0:G, g // 4, (g % 4) * G:(g % 4 + 1) * G],
                                    bc(prio[:, g:g + 1], [G, G]), ident[0:G, 0:G])
                if g % 4 == 3 or g == NG - 1:
                    last.then_inc(s_pbp, 1)

            for nth, j in enumerate(2 * q + a for q in RANKED for a in range(2)):
                at = PS[0:G, 6 + nth // 2 % 2, j % 2 * E:(j % 2 + 1) * E]
                lot = [n for n, (a, b_) in enumerate(BY_ACT) if a <= j < b_]
                if j < ND:
                    pe.wait_ge(s_bef, j + 1)
                else:
                    pe.wait_ge(s_sgn, lot[0] + 1)
                pe.wait_ge(s_own, [a <= j < b_ for a, b_ in OWN_BEFORE.values()].index(True) + 1)
                if nth % 2 == 0 and nth >= 4:
                    pe.wait_ge(s_slot, nth // 2 - 1)
                for i in range(NG):
                    if i == j or j < ND:
                        lhsT = own[:, j, :] if i == j else before[j % 2][:, i, :]
                        last = pe.matmul(at, lhsT, ohb[:, i, :],
                                         start=(j % 2 == 0 and i == 0), stop=True, skip_group_check=True)
                    else:
                        last = pe.matmul(at, sgn[lot[0]][:, j - BY_ACT[lot[0]][0], i, :], ohh[:, i, :],
                                         start=(j % 2 == 0 and i == 0), stop=True, skip_group_check=True)
                if j >= ND:
                    pe.matmul(at, onesb[:, :], ohsb[:, :], start=False, stop=True, skip_group_check=True)
                    last = pe.matmul(at, onesb[:, :], ohn[:, j, :], start=False, stop=True, skip_group_check=True)
                last.then_inc(s_cnt, 1)

            def expert_rows(e, p, i2, e_before=None):
                pe.wait_ge(s_ex[p], i2 * 32 + 32)
                for k in range(2):
                    if k == 1 and e_before is not None:
                        pe.wait_ge(s_hg, e_before * HC + 4)
                    for i in range(NT):
                        n = tile_rows(i)
                        last = pe.transpose(PS[:, 2 * k + i // 4, 128 * (i % 4):128 * (i % 4) + n],
                                            xe[0:n, p, i, k * 64:k * 64 + 128], ident[0:n, 0:n])
                last.then_inc(s_xep, 1)

            def hidden(e, first):
                pe.wait_ge(s_xeh, e + 1)
                pe.wait_ge(s_xel, e + 1)
                pe.wait_ge(s_w1h, e + 1)
                pe.wait_ge(s_w1l, e + 1)
                if first:
                    pe.wait_ge(s_zw, 1)
                for c in range(HC):
                    if c == 1 and not first:
                        pe.wait_ge(s_ye, e * NT)
                    if c >= 3:
                        pe.wait_ge(s_hg, e * HC + c - 2)
                    w = slice(c * 128, (c + 1) * 128)
                    for n in range(2):
                        for nth, (hl, b_) in enumerate(BLOCKS):
                            last = pe.matmul(PS[:, hidden_bank(c) + n, 0:HALF], (w1h, w1l)[hl][:, b_, w],
                                             xeT[:, b_, n * HALF:(n + 1) * HALF],
                                             start=(nth == 0), stop=(nth == len(BLOCKS) - 1))
                    last.then_inc(s_hp, 1)

            def results(e):
                pe.wait_ge(s_w2h, e + 1)
                pe.wait_ge(s_w2l, e + 1)
                pe.wait_ge(s_hg, e * HC + HC - 1)
                pe.wait_ge(s_hl, e * HC + HC - 1)
                for i in range(NT):
                    bank = 4 + i % 4
                    n = tile_rows(i)
                    if i >= 4:
                        pe.wait_ge(s_ye, e * NT + i - 3)
                    both = lambda w: w.rearrange("p a d -> p (a d)")
                    pe.matmul(PS[0:n, bank, 0:2 * D], onesr[:, 0:n], both(b2hl[:, :, :]), start=True, stop=False)
                    at = slice(128 * i, 128 * i + n)
                    for c in range(HC):
                        if i == 0 and c == HC - 1:
                            pe.wait_ge(s_hg, e * HC + HC)
                            pe.wait_ge(s_hl, e * HC + HC)
                        pe.matmul(PS[0:n, bank, 0:D], hTl[:, c, at], w2hl[:, c, 0, :], start=False, stop=False,
                                  skip_group_check=True)
                        last = pe.matmul(PS[0:n, bank, 0:2 * D], hTh[:, c, at], both(w2hl[:, c, :, :]),
                                         start=False, stop=(c == HC - 1))
                    last.then_inc(s_yp, 1)

            expert_rows(0, 0, 0)
            hidden(0, True)
            expert_rows(1, 1, 0, 0)
            results(0)
            with pe.Fori(0, E // 2 - 1) as i:
                hidden(i * 2 + 1, False)
                expert_rows(i * 2 + 2, 0, i + 1, i * 2 + 1)
                results(i * 2 + 1)
                hidden(i * 2 + 2, False)
                expert_rows(i * 2 + 3, 1, i + 1, i * 2 + 2)
                results(i * 2 + 2)
            hidden(E - 1, False)
            results(E - 1)

        @blk.scalar
        def _(act):
            for u in range(UNITS):
                act.wait_ge(s_tT, u + 1)
                if u >= 2:
                    act.wait_ge(s_tz, u - 1)
                nc.scalar.copy(xTt[:, u % 2, :, :].rearrange("p (a c) n -> p a (c n)", a=2),
                               PS[:, 2 * (u % 2):2 * (u % 2) + 2, 0:384]).then_inc(s_tTa, 1)

            def rows_transposed(s):
                act.wait_ge(s_xTp, s + 1)
                nc.scalar.copy(xT[:, 0:2, :].rearrange("p k n -> p (k n)"), PS[:, 2, 0:2 * G2]).then_inc(s_xTh, 1)

            def queries(s, q, bias, done):
                for m in range(HB):
                    if m % 2 == 0:
                        act.wait_ge(s_qp, s * 2 + m // 2 + 1)
                    last = nc.scalar.activation(q[:, m, :], PS[:, 1 - m // 2, (m % 2) * G2:(m % 2 + 1) * G2],
                                                ACT.Identity, bias=bias[:, m:m + 1], scale=K ** -0.5)
                last.then_inc(done, 1)

            def relative(s, g):
                act.wait_ge(s_rp[g], s + 1)
                if not is_step(s, 0):
                    act.wait_ge(s_ro[g], 96 * s)
                nc.scalar.copy(rel[:, g, :].rearrange("p (a n) -> p a n", a=2),
                               PS[0:G, (6, 0)[g]:(8, 2)[g], 0:HB * R]).then_inc(s_re[g], 1)

            def outputs(s, g):
                act.wait_ge(s_otp[g], s + 1)
                nc.scalar.copy(oTh[:, g, :].rearrange("p (a n) -> p a n", a=2),
                               PS[:, (6, 4)[g]:(8, 6)[g], 0:3 * G]).then_inc(s_oth[g], 1)

            def values(s, g):
                act.wait_ge(s_vp[g], s + 1)
                nc.scalar.copy(v_sb[:, g, :].rearrange("p (a n) -> p a n", a=2),
                               PS[0:G, 2 * g:2 * g + 2, 0:HB * V]).then_inc(s_v[g], 1)

            def probs(s, g):
                act.wait_ge(s_sh[g], s + 1)
                nc.scalar.activation(
                    pb[:, g, :].rearrange("p (h i t) -> p h i t", h=H, i=IPG),
                    bc(sc[:, g, :].rearrange("p (h a t) -> p h a t", h=H, a=1), [G, H, IPG, T]),
                    ACT.Exp).then_inc(s_p[g], 1)

            def gate_rows(s):
                act.wait_ge(s_xrp, s + 1)
                nc.scalar.copy(xnT[:, :, :].rearrange("p k n -> p (k n)"), PS[0:KD, 3, 0:2 * G2]).then_inc(s_xrT, 1)

            def logits(s):
                act.wait_ge(s_lp, s + 1)
                nc.scalar.copy(logit[:, bass.ds(2 * s, 2), :],
                               PS[0:G, 3, 0:2 * E].rearrange("p (g e) -> p g e", g=2)).then_inc(s_l, 1)

            act.wait_ge(s_qkv, 16 * N_QKV)
            nc.scalar.copy(wh[:, :, :], wraw[:, :, :]).then_inc(s_wh, 1)
            act.wait_ge(s_aw, 16 * N_AW)
            nc.scalar.copy(woh[:, :, :], wo[:, :, :]).then_inc(s_woh, 1)
            rows_transposed(0)

            def step(s):
                here = not is_step(s, STEPS)
                before_ = not is_step(s, 0)
                if before_:
                    probs(s - 1, 0)
                if before_ and not is_step(s, 1):
                    logits(s - 2)
                if here:
                    queries(s, qr, rrb, s_qr)
                    queries(s, qw, rwb, s_q)
                if before_:
                    probs(s - 1, 1)
                if here:
                    relative(s, 0)
                    relative(s, 1)
                for g in range(2):
                    if before_:
                        outputs(s - 1, g)
                    if here:
                        values(s, g)
                if here:
                    rows_transposed(s + 1)
                if before_:
                    gate_rows(s - 1)

            step(0)
            step(1)
            with act.Fori(2, STEPS) as s:
                step(s)
            step(STEPS)
            logits(STEPS - 1)
            act.wait_ge(s_d, 1)
            nc.scalar.activation(ex[:, :], ex[:, :], ACT.Exp).then_inc(s_e, 1)

            for b_ in range(2, -(-NG // 4)):
                act.wait_ge(s_pbp, b_ + 1)
                n = min(4, NG - 4 * b_) * G
                last = nc.scalar.copy(prow[:, b_ * 4 * G:b_ * 4 * G + n], PS[0:G, b_, 0:n])
            last.then_inc(s_pba, 1)
            act.wait_ge(s_pba, 1)
            act.wait_ge(s_nudge, 1)
            for lot, (first_, end) in enumerate(BY_ACT):
                pcols = prow[:, first_ * G:end * G].rearrange("p (j n) -> p j n", j=end - first_)
                for i in range(NG):
                    for j0, j1, bias in ((0, i, prio_dn), (i + 1, NG, prio_up)):
                        a, b_ = max(0, j0 - first_), min(j1, end) - first_
                        if b_ > a:
                            last = nc.scalar.activation(sgn[lot][:, a:b_, i, :], pcols[:, a:b_, :], ACT.Sign,
                                                        bias=bias[:, i:i + 1], scale=-1.0)
                last.then_inc(s_sgn, 1)

            def w1_high(e):
                act.wait_ge(s_w1r, e * 64 + 64)
                if not is_step(e, 0):
                    act.wait_ge(s_hp, e * HC)
                nc.scalar.copy(w1h[:, :, :], w1r[:, :, :]).then_inc(s_w1h, 1)

            def rows_high(e):
                act.wait_ge(s_xep, e + 1)
                for k in range(2):
                    last = nc.scalar.copy(xeT[:, k, :], both_banks(2 * k))
                last.then_inc(s_xeh, 1)

            def expert(e, p, i2, first):
                act.wait_ge(s_w2r, e * 16 + 16)
                if not first:
                    act.wait_ge(s_yp, e * NT)
                act.wait_ge(s_eb[p], i2 * 32 + 32)
                nc.scalar.copy(b2hl[:, 0, :], b2r[:, p, :])
                nc.scalar.copy(w2hl[:, :, 0, :], w2r[:, :, :]).then_inc(s_w2h, 1)
                for c in range(HC):
                    act.wait_ge(s_hp, e * HC + c + 1)
                    src = PS[:, hidden_bank(c):hidden_bank(c) + 2, 0:HALF]
                    if not first or c >= 2:
                        act.wait_ge(s_hl, e * HC + c - 1)
                    last = nc.scalar.activation(hf[:, c % 2, :].rearrange("p (a n) -> p a n", a=2), src, ACT.Gelu,
                                                bias=b1s[:, p, c:c + 1])
                    if c not in HIGH_BY_DVE:
                        last = nc.scalar.activation(hTh[:, c, :].rearrange("p (a n) -> p a n", a=2), src, ACT.Gelu,
                                                    bias=b1s[:, p, c:c + 1])
                    last.then_inc(s_hg, 1)

            act.wait_ge(s_cnt, NG)
            w1_high(0)
            rows_high(0)
            expert(0, 0, 0, True)
            rows_high(1)
            w1_high(1)
            with act.Fori(0, E // 2 - 1) as i:
                for p in (1, 0):
                    e = i * 2 + 2 - p
                    expert(e, p, i + 1 - p, False)
                    rows_high(e + 1)
                    w1_high(e + 1)
            expert(E - 1, 1, E // 2 - 1, False)

        @blk.vector
        def _(dve):
            v = nc.vector

            def ch(ins):
                dve.drain()

            v.memset(ones[:, :], 1.0)
            v.memset(zeros[:, :], 0.0).then_inc(s_set, 1)
            v.memset(meanw[:, :], 1.0 / PD).then_inc(s_set, 1)
            v.memset(h_all[:, NG:NG + 2, :], 0.0)
            v.memset(onesb[:, :], 1.0)
            v.memset(one_row[:, :], 1.0)
            v.memset(nhalf[:, :], -0.5).then_inc(s_setv, 1)

            v.memset(wl[0:64, 1, :].bitcast(F32), 0.0)
            dve.wait_ge(s_early, 16 * N_EARLY)
            for c in range(PC):
                last = v.tensor_scalar(W_cen[:, c, :], W_raw[:, c, :], g1[:, c:c + 1], None, ALU.mult)
            last.then_inc(s_gw, 1)
            dve.wait_ge(s_gw, 1)

            def ln1_stats(j, w):
                if w % (NH // 2) == 0:
                    dve.wait_ge(s_x[j][w // (NH // 2)], 32)
                for q in range(2):
                    v.bn_stats(bn1[:, j, w, q, :], xv[:, j, w, q * (PD // 2):(q + 1) * (PD // 2)])

            def ln1_end(j):
                dve.drain()
                for w in range(NH):
                    last = v.bn_aggr(mv1[:, j, w, :], bn1[:, j, w, :, :])
                ch(last)
                v.tensor_scalar(ve1[:, j, :], mv1[:, j, :, 1], EPS, None, ALU.add).then_inc(s_v1, 1)

            dve.wait_ge(s_mean, 1)
            for c in range(PC):
                last = v.tensor_tensor(W_cen[:, c, :], W_cen[:, c, :], PS[:, 6, 0:D], ALU.subtract)
            last.then_inc(s_wc, 1)
            for w in range(NH):
                ln1_stats(0, w)
            ln1_end(0)
            dve.wait_ge(s_brow, 1)
            v.tensor_copy(cB[:, :], PS[:, 7, 0:D]).then_inc(s_cb, 1)
            dve.wait_ge(s_cb, 1)

            def ln2_stats(j, f):
                ws = range(f * NF, (f + 1) * NF)
                dve.wait_ge(s_tze, j * NH + (f + 1) * NF)
                for w in ws:
                    last = v.bn_stats(bnt[:, j, w, :], zt[:, j, w, :])
                ch(last)
                for w in ws:
                    last = v.bn_aggr(mvt[:, j, w, :], bnt[:, j, w, :])
                ch(last)
                v.tensor_scalar(vet[:, j, f * NF:(f + 1) * NF], mvt[:, j, f * NF:(f + 1) * NF, 1], EPS, None, ALU.add
                                ).then_inc(s_v2, 1)

            def ln2_rows(j, f):
                dve.wait_ge(s_r2, 2 * j + f + 1)
                for w in range(f * NF, (f + 1) * NF):
                    last = v.tensor_scalar(zt[:, j, w, :], zt[:, j, w, :], mvt[:, j, w, 0:1], rst[:, j, w:w + 1],
                                           ALU.subtract, ALU.mult)
                last.then_inc(s_tn, 1)

            for j in range(NH // 2):
                dve.wait_ge(s_r1, j + 1)
                for w in range(NH):
                    u = j * NH + w
                    dve.wait_ge(s_tz, u + 1)
                    v.scalar_tensor_tensor(zt[:, j, w, :], PS[:, 4 + u % 4, 0:D], rs1[:, j, w:w + 1], cB[:, :],
                                           ALU.mult, ALU.add).then_inc(s_tze, 1)
                    if j + 1 < NH // 2:
                        ln1_stats(j + 1, w)
                        if w == NH - 1:
                            ln1_end(j + 1)
                    if w % NF == NF - 1:
                        ln2_stats(j, w // NF)
                    if w % NF == 1 and u >= NF:
                        ln2_rows((u - NF) // NH, (u - NF) // NF % 2)
            ln2_rows(NH // 2 - 1, 1)
            dve.wait_ge(s_pos, NH // 2)
            dve.wait_ge(s_tn, NH)
            z3 = zt[:, NH // 2 - 1, NF:]
            three = lambda b_: bc(b_[:, :].rearrange("p (a d) -> p a d", a=1), [128, NF, D])
            ch(v.tensor_tensor(z3, z3, three(g2B), ALU.mult))
            v.tensor_tensor(z3, z3, posB[:, NH // 2 - 1, NF * D:].rearrange("p (w d) -> p w d", w=NF),
                            ALU.add).then_inc(s_ht_last, 1)
            dve.wait_ge(s_const, 16 * N_CONST)
            dve.wait_ge(s_wh, 1)
            v.tensor_tensor(wl[:, 0, :], wraw[:, 0, :], wh[:, 0, :].bitcast(F32), ALU.subtract)
            v.tensor_tensor(wl[64:128, 1, :], wraw[64:128, 2, :], wh[64:128, 2, :].bitcast(F32),
                            ALU.subtract).then_inc(s_wl, 1)
            dve.wait_ge(s_rkp, 1)
            v.tensor_copy(rk[:, :, :].rearrange("p m r -> p (m r)"), PS[:, 6, 0:HB * R]).then_inc(s_rk, 1)

            def ln1_var(s):
                for g in range(2):
                    ch(v.bn_stats(st[:, :], h_all[:, 2 * s + g, :]))
                    ch(v.bn_aggr(mv[:, g, :], st[:, :]))
                v.tensor_scalar(ve[:, :], mv[:, :, 1], EPS, None, ALU.add).then_inc(s_va, 1)

            def ln1_rows(s):
                dve.wait_ge(s_ra, s + 1)
                for g in range(2):
                    last = v.tensor_scalar(xn[:, g, :], h_all[:, 2 * s + g, :], mv[:, g, 0:1], rs[:, g:g + 1],
                                           ALU.subtract, ALU.mult)
                last.then_inc(s_xn, 1)

            def rows_low(s):
                dve.wait_ge(s_xTh, s + 1)
                ch(v.tensor_tensor(xT[:, 2, :], PS[:, 2, G2:2 * G2], xT[:, 1, :].bitcast(F32), ALU.subtract))
                v.tensor_tensor(xT[0:64, 1, :], PS[0:64, 2, 0:G2], xT[0:64, 0, :].bitcast(F32),
                                ALU.subtract).then_inc(s_xT, 1)

            def keys(s):
                for m2 in range(2):
                    dve.wait_ge(s_kp, s * 2 + m2 + 1)
                    v.tensor_copy(kT[:, 2 * m2:2 * m2 + 2, :].rearrange("p m n -> p (m n)"),
                                  PS[:, 2 + m2, 0:2 * G2]).then_inc(s_k, 1)

            def softmax(s):
                for g in range(2):
                    dve.wait_ge(s_sp[g], s + 1)
                    dve.wait_ge(s_ri[g], s * 32 + 32)
                    a3 = sc[:, g, :].rearrange("p (h t) -> p h t", h=H)
                    r3 = relw[:, g, :].rearrange("p (h t) -> p h t", h=H)
                    for i in range(IPG):
                        ins = v.scalar_tensor_tensor(a3, heads(4 + 2 * g, G)[:, :, i * T:(i + 1) * T],
                                                     ind[:, i:i + 1], a3 if i else r3, ALU.mult, ALU.add)
                        if i < IPG - 1:
                            ch(ins)
                    ins.then_inc(s_sc[g], 1)
                    dve.wait_ge(s_sc[g], s + 1)
                    ch(v.tensor_reduce(mx[:, g, :], a3, AX.X, ALU.max))
                    v.tensor_tensor(a3, a3, bc(mx[:, g, :].rearrange("p (h a) -> p h a", a=1), [G, H, T]),
                                    ALU.subtract).then_inc(s_sh[g], 1)

            def masked(s):
                for g in range(2):
                    dve.wait_ge(s_ptp[g], s + 1)
                    v.tensor_tensor(pT[:, g, :].rearrange("p (h t) -> p h t", h=H), heads(4 - 2 * g, G),
                                    bc(block[:, :].rearrange("p (a t) -> p a t", a=1), [G, H, G]),
                                    ALU.mult).then_inc(s_pt[g], 1)
                    dve.wait_ge(s_p[g], s + 1)
                    ch(v.tensor_reduce(rsum[:, g, :], pb[:, g, :].rearrange("p (h i t) -> p h i t", h=H, i=IPG)[:, :, 0, :],
                                       AX.X, ALU.add))
                    ch(v.reciprocal(rinv[:, g, :], rsum[:, g, :]))
                for g in range(2):
                    dve.wait_ge(s_op[g], s + 1)
                    v.tensor_tensor(o_sb[:, g, :].rearrange("p (h t) -> p h t", h=H), heads(4 - 2 * g, V),
                                    bc(rinv[:, g, :].rearrange("p (h a) -> p h a", a=1), [G, H, V]),
                                    ALU.mult).then_inc(s_o[g], 1)

            def outputs_low(s, g):
                dve.wait_ge(s_oth[g], s + 1)
                part = lambda t: t[:, g, :].rearrange("p (a n) -> p a n", a=2)
                v.tensor_tensor(part(oTl), PS[:, (6, 4)[g]:(8, 6)[g], 0:3 * G], part(oTh).bitcast(F32),
                                ALU.subtract).then_inc(s_ot[g], 1)

            def residual(s):
                dve.wait_ge(s_hb, s + 1)
                for g in range(2):
                    dve.wait_ge(s_wop[g], s + 1)
                    v.tensor_tensor(h_all[:, 2 * s + g, :], h_all[:, 2 * s + g, :], PS[0:G, g, 0:D],
                                    ALU.add).then_inc(s_h1[g], 1)
                    dve.drain()
                    ch(v.bn_stats(st2[:, :], h_all[:, 2 * s + g, :]))
                    ch(v.bn_aggr(mv2[:, g, :], st2[:, :]))
                    v.tensor_scalar(ve2[:, g:g + 1], mv2[:, g, 1:2], EPS, None, ALU.add).then_inc(s_vb[g], 1)
                for g in range(2):
                    dve.wait_ge(s_rb[g], s + 1)
                    if g == 0:
                        if not is_step(s, 0):
                            for c in s_xrc:
                                dve.wait_ge(c, s)
                    v.tensor_scalar(xn2[:, g, :], h_all[:, 2 * s + g, :], mv2[:, g, 0:1], rs2[:, g:g + 1],
                                    ALU.subtract, ALU.mult).then_inc(s_xr[g], 1)

            def step(s):
                here = not is_step(s, STEPS)
                before_ = not is_step(s, 0)
                if before_:
                    softmax(s - 1)
                if here:
                    keys(s)
                if before_:
                    masked(s - 1)
                    outputs_low(s - 1, 0)
                if here:
                    ln1_var(s + 1)
                if before_:
                    outputs_low(s - 1, 1)
                if here:
                    ln1_rows(s + 1)
                if before_:
                    residual(s - 1)
                if here:
                    rows_low(s + 1)

            dve.wait_ge(s_h, 32)
            ln1_var(0)
            ln1_rows(0)
            rows_low(0)
            dve.wait_ge(s_woh, 1)
            v.tensor_tensor(wol[:, :, :], wo[:, :, :], woh[:, :, :].bitcast(F32), ALU.subtract).then_inc(s_wol, 1)
            dve.wait_ge(s_h, 64)
            step(0)
            step(1)
            with dve.Fori(2, STEPS) as s:
                step(s)
            step(STEPS)

            dve.wait_ge(s_l, STEPS)
            dve.wait_ge(s_aw, 16 * N_AW)
            io = bc(iota8[:, 0:1, :], [G, NG, E])
            io8 = bc(iota8[:, 1:2, :], [G, NG, E])
            col = lambda a: bc(a.rearrange("p (g a) -> p g a", a=1), [G, NG, E])
            lg = logit[:, :, :]

            def lowest(src, m):
                ch(v.tensor_tensor(tmp8[:, :, :], src, col(m[:, :]), ALU.is_equal))
                ch(v.scalar_tensor_tensor(tmp8[:, :, :], tmp8[:, :, :], -8.0, io8, ALU.mult, ALU.add))

            def one_hot(k, ii):
                ch(v.tensor_reduce(ii[:, :], tmp8[:, :, :], AX.X, ALU.min))
                ch(v.tensor_tensor(oh[:, k], io, col(ii[:, :]), ALU.is_equal))

            ch(v.tensor_reduce(m1[:, :], lg, AX.X, ALU.max))
            lowest(lg, m1)
            one_hot(0, i1)
            ch(v.scalar_tensor_tensor(l2[:, :, :], oh[:, 0], -1.0e30, lg, ALU.mult, ALU.add))
            ch(v.tensor_reduce(m2[:, :], l2[:, :, :], AX.X, ALU.max))
            v.tensor_tensor(ex[:, :], m2[:, :], m1[:, :], ALU.subtract).then_inc(s_d, 1)
            lowest(l2[:, :, :], m2)
            dve.wait_ge(s_e, 1)
            ch(v.tensor_scalar(w01[:, 0, :], ex[:, :], 1.0, None, ALU.add))
            ch(v.reciprocal(w01[:, 0, :], w01[:, 0, :]))
            v.tensor_scalar(prio[:, :], w01[:, 0, :], -0.75, -0.25, ALU.add, ALU.max).then_inc(s_prio, 1)
            v.tensor_tensor(w01[:, 1, :], w01[:, 0, :], ex[:, :], ALU.mult)
            one_hot(1, i2)
            for k in range(2):
                last = v.tensor_tensor(oh[:, k], oh[:, k], col(real[:, :]), ALU.mult)
            ch(last)
            ch(v.tensor_tensor(ohb[:, :, :], oh[:, 0], oh[:, 1], ALU.add))
            dve.wait_ge(s_prio, 1)
            v.tensor_scalar(prio_up[:, :], prio[:, :], HALF_ULP, None, ALU.add)
            v.tensor_scalar(prio_dn[:, :], prio[:, :], -HALF_ULP, None, ALU.add).then_inc(s_nudge, 1)
            v.tensor_scalar(lower_by[:, :], upper[:, :], HALF_ULP, None, ALU.mult)

            def prio_rows(b_):
                dve.wait_ge(s_pbp, b_ + 1)
                v.tensor_copy(prow[:, b_ * 4 * G:(b_ + 1) * 4 * G], PS[0:G, b_, 0:4 * G]).then_inc(s_pb, 1)
                dve.wait_ge(s_pb, b_ + 1)

            def rows_carry():
                v.tensor_copy(xr_all[:, :, D], w01[:, 0, :])
                v.tensor_copy(xr_all[:, :, D + 1], w01[:, 1, :])
                v.tensor_copy(xr_all[:, :, D + 2], i1[:, :])
                v.tensor_copy(xr_all[:, :, D + 3], tok[:, :])
                for k, ii in enumerate((i1, i2)):
                    v.tensor_scalar(base[:, k, :], ii[:, :], float(CAP), BIG, ALU.mult, ALU.add)
                v.tensor_scalar(ohh[:, :, :], ohb[:, :, :], 0.5, None, ALU.mult)
                v.tensor_scalar(ohn[:, :, :], ohb[:, :, :], -0.5, None, ALU.mult)
                ch(v.tensor_reduce(ohs[:, :], ohb[:, :, :].rearrange("p g e -> p e g"), AX.X, ALU.add))
                v.tensor_scalar(ohsb[:, :], ohs[:, :], 0.5, None, ALU.mult)

            def compare(j):
                pj = prow[:, j * G:(j + 1) * G]
                if j >= 2:
                    dve.wait_ge(s_cnt, 2 * RANKED.index(j // 2 - 1) + j % 2 + 1)
                for a, b_, op in ((0, j, ALU.is_le), (j + 1, NG, ALU.is_lt)):
                    if b_ > a:
                        last = v.tensor_tensor(before[j % 2][:, a:b_, :],
                                               bc(pj.rearrange("p (a n) -> p a n", a=1), [G, b_ - a, G]),
                                               bc(prio[:, a:b_].rearrange("p (i a) -> p i a", a=1),
                                                  [G, b_ - a, G]), op)
                last.then_inc(s_bef, 1)

            def compare_own(a, b_):
                tiles = [G, b_ - a, G]
                if b_ > 8:
                    dve.wait_ge(s_pba, 1)
                p3 = prow[:, a * G:b_ * G].rearrange("p (j n) -> p j n", j=b_ - a)
                l3 = bc(lower_by[:, :].rearrange("p (a n) -> p a n", a=1), tiles)
                ch(v.tensor_tensor(nudged[:, a:b_, :], p3, l3, ALU.subtract))
                v.tensor_tensor(own[:, a:b_, :], nudged[:, a:b_, :],
                                bc(prio[:, a:b_].rearrange("p (j a) -> p j a", a=1), tiles),
                                ALU.is_lt).then_inc(s_own, 1)

            def slots(nth):
                dve.wait_ge(s_cnt, 2 * nth + 2)
                q = RANKED[nth]
                w2 = slice(2 * q, 2 * q + 2)
                ranks = PS[0:G, 6 + nth % 2, 0:2 * E].rearrange("p (a g e) -> p a g e", a=1, g=2)
                ch(v.tensor_tensor(tmp4[:, :, :, :], oh[:, :, w2, :], bc(ranks, [G, 2, 2, E]), ALU.mult))
                ch(v.tensor_reduce(posk[:, :, w2], tmp4[:, :, :, :], AX.X, ALU.add))
                v.scalar_tensor_tensor(keep[:, :, w2], posk[:, :, w2], float(CAP),
                                          bc(real[:, w2].rearrange("p (a g) -> p a g", a=1), [G, 2, 2]),
                                          ALU.is_lt, ALU.mult)
                ch(v.tensor_tensor(slot[:, :, w2], base[:, :, w2], posk[:, :, w2], ALU.add))
                v.scalar_tensor_tensor(sloti[:, :, w2], keep[:, :, w2], -BIG, slot[:, :, w2], ALU.mult,
                                       ALU.add).then_inc(s_slot, 1)

            prio_rows(0)
            for j in range(ND):
                if j in OWN_BEFORE:
                    compare_own(*OWN_BEFORE[j])
                compare(j)
                if j == 0:
                    rows_carry()
                if j == 2:
                    prio_rows(1)
                for nth in SLOTS_AFTER.get(j, ()):
                    slots(nth)
            for nth in range(sum(map(len, SLOTS_AFTER.values())), NG // 2):
                slots(nth)

            def w1_low(e):
                dve.wait_ge(s_w1h, e + 1)
                v.tensor_tensor(w1l[:, 0, :], w1r[:, 0, :], w1h[:, 0, :].bitcast(F32), ALU.subtract)
                v.tensor_tensor(w1l[64:128, 1, :], w1r[64:128, 2, :], w1h[64:128, 2, :].bitcast(F32),
                                ALU.subtract).then_inc(s_w1l, 1)

            def rows_low(e, p):
                dve.wait_ge(s_xeh, e + 1)
                ch(v.tensor_tensor(xeT[:, 2, :], both_banks(2), xeT[:, 1, :].bitcast(F32), ALU.subtract))
                v.tensor_tensor(xeT[0:64, 1, :], both_banks(0)[0:64], xeT[0:64, 0, :].bitcast(F32),
                                ALU.subtract).then_inc(s_xel, 1)

            def routing(e, p, i):
                t = lambda n: xe[:, p, :, D + n]
                ch(v.tensor_scalar(first[:, p, :], t(2), eidx[:, bass.ds(e, 1)], None, ALU.is_equal))
                ch(v.tensor_tensor(wtmp[:, p, :], first[:, p, :], t(0), ALU.mult))
                ch(v.tensor_scalar(first[:, p, :], first[:, p, :], -1.0, 1.0, ALU.mult, ALU.add))
                ch(v.tensor_tensor(wsel[:, p, :], first[:, p, :], t(1), ALU.mult))
                v.tensor_tensor(wsel[:, p, :], wsel[:, p, :], wtmp[:, p, :], ALU.add).then_inc(s_wsel, 1)
                if not is_step(i, 0):
                    dve.wait_ge(s_ys, (i * 2 + p - 1) * (16 * NT))
                v.tensor_copy(dsti[:, p, :], t(3)).then_inc(s_di, 1)

            def hidden_low(e, p):
                dve.wait_ge(s_w2h, e + 1)
                v.tensor_tensor(b2hl[:, 1, :], b2r[:, p, :], b2hl[:, 0, :].bitcast(F32), ALU.subtract)
                v.tensor_tensor(w2hl[:, :, 1, :], w2r[:, :, :], w2hl[:, :, 0, :].bitcast(F32), ALU.subtract
                                ).then_inc(s_w2l, 1)
                for c in range(HC):
                    dve.wait_ge(s_hg, e * HC + c + 1)
                    if c in HIGH_BY_DVE:
                        ch(v.tensor_copy(hTh[:, c, :], hf[:, c % 2, :]))
                    v.tensor_tensor(hTl[:, c, :], hf[:, c % 2, :], hTh[:, c, :].bitcast(F32), ALU.subtract
                                    ).then_inc(s_hl, 1)

            def results(e, p, i, more):
                dve.wait_ge(s_acc, e * (16 * NT) + 16 * NT)
                for n in range(NT):
                    if more and n == 2:
                        w1_low(e + 1)
                    dve.wait_ge(s_yp, e * NT + n + 1)
                    r = tile_rows(n)
                    last = v.scalar_tensor_tensor(acc[0:r, p, n, :], PS[0:r, 4 + n % 4, D:2 * D],
                                                  wsel[0:r, p, n:n + 1], acc[0:r, p, n, :], ALU.mult, ALU.add)
                    if n in (0, 2):
                        continue
                    ch(last)
                    for m in (n - 1, n) if n in (1, 3) else (n,):
                        r = tile_rows(m)
                        v.scalar_tensor_tensor(ye[0:r, p, m, :], PS[0:r, 4 + m % 4, 0:D], wsel[0:r, p, m:m + 1],
                                               acc[0:r, p, m, :], ALU.mult, ALU.add).then_inc(s_ye, 1)

            v.memset(w1l[0:64, 1, :].bitcast(F32), 0.0).then_inc(s_zw, 1)
            v.tensor_copy(onesr[:, :], one_row[:, :])
            w1_low(0)
            rows_low(0, 0)
            routing(0, 0, 0)
            hidden_low(0, 0)
            rows_low(1, 1)
            results(0, 0, 0, True)
            routing(1, 1, 0)
            with dve.Fori(0, E // 2 - 1) as i:
                for p in (1, 0):
                    e = i * 2 + 2 - p
                    hidden_low(e, p)
                    rows_low(e + 1, 1 - p)
                    results(e, p, i + 1 - p, True)
                    routing(e + 1, 1 - p, i + 1)
            hidden_low(E - 1, 1)
            results(E - 1, 1, E // 2 - 1, False)

        @blk.gpsimd
        def _(pool):
            p_ = nc.gpsimd

            def rsqrt(o, i):
                return p_.tensor_tensor(o, i, nhalf[0:i.shape[0], 0:i.shape[1]], ALU.pow)

            pool.wait_ge(s_setv, 1)

            def rstd1(j):
                pool.wait_ge(s_v1, j + 1)
                rsqrt(rs1[:, j, :], ve1[:, j, :]).then_inc(s_r1, 1)

            def rstd2(j, f):
                pool.wait_ge(s_v2, 2 * j + f + 1)
                rsqrt(rst[:, j, f * NF:(f + 1) * NF], vet[:, j, f * NF:(f + 1) * NF]).then_inc(s_r2, 1)

            def rows(b_, n):
                return bc(b_[:, :].rearrange("p (a d) -> p a d", a=1), [128, n, D])

            def positions(j):
                pv = posB[:, j, :].rearrange("p (w d) -> p w d", w=NH)
                p_.tensor_tensor(pv, pv, rows(b2B, NH), ALU.add).then_inc(s_pos, 1)

            def finish(j, f):
                pool.wait_ge(s_tn, 2 * j + f + 1)
                pool.wait_ge(s_pos, j + 1)
                zh = zt[:, j, f * NF:(f + 1) * NF]
                p_.tensor_tensor(zh, zh, rows(g2B, NF), ALU.mult)
                pool.drain()
                p_.tensor_tensor(zh, zh, posB[:, j, f * NF * D:(f + 1) * NF * D].rearrange("p (w d) -> p w d", w=NF),
                                 ALU.add).then_inc(s_ht, 1)

            rstd1(0)
            rstd2(0, 0)
            rstd1(1)
            rstd2(0, 1)
            pool.wait_ge(s_const, 16 * N_CONST)
            p_.tensor_tensor(clsP[:, :], clsB[:, 0, :], clsB[:, 1, :], ALU.add).then_inc(s_cls, 1)
            positions(0)
            finish(0, 0)
            finish(0, 1)
            rstd2(1, 0)
            positions(1)
            finish(1, 0)
            rstd1(2)
            rstd2(1, 1)
            finish(1, 1)
            positions(2)
            rstd2(2, 0)
            finish(2, 0)
            rstd2(2, 1)
            pool.wait_ge(s_aw, 16 * N_AW)

            def ln1(s):
                pool.wait_ge(s_va, s + 1)
                rsqrt(rs[:, :], ve[:, :]).then_inc(s_ra, 1)

            def bias(s):
                pool.wait_ge(s_xn, s + 1)
                hs = h_all[:, bass.ds(2 * s, 2), :]
                p_.tensor_tensor(hs, hs, bc(boB[:, :].rearrange("p (a d) -> p a d", a=1), [G, 2, D]),
                                 ALU.add).then_inc(s_hb, 1)

            def ln2(s):
                for g in range(2):
                    pool.wait_ge(s_vb[g], s + 1)
                    rsqrt(rs2[:, g:g + 1], ve2[:, g:g + 1]).then_inc(s_rb[g], 1)
                for g in range(2):
                    pool.wait_ge(s_xr[g], s + 1)
                    p_.tensor_copy(xr_all[:, 2 * s + g, 0:D], xn2[:, g, :]).then_inc(s_xrc[g], 1)

            ln1(0)
            bias(0)
            ln1(1)
            bias(1)
            with pool.Fori(1, STEPS) as s:
                ln1(s + 1)
                bias(s + 1)
                ln2(s - 1)
            ln2(STEPS - 1)

            for c in s_xrc:
                pool.wait_ge(c, STEPS)
            p_.memset(xe[:, :, :, :], 0.0).then_inc(s_xe0, 1)
            pool.wait_ge(s_fill, 16 * N_FILL)
            for nth, g in enumerate(2 * q + a for q in RANKED for a in range(2)):
                if nth % 2 == 0:
                    pool.wait_ge(s_slot, nth // 2 + 1)
                for k in range(2):
                    p_.indirect_dma_start(xbuf, bass.IndirectOffsetOnAxis(ap=sloti[:, k, g:g + 1], axis=0),
                                          xr_all[:, g, :], None, bounds_check=E * CAP - 1,
                                          oob_is_err=False).then_inc(s_sct, 16)

            pool.wait_ge(s_sct, 16 * 2 * NG)
            p_.memset(acc[:, :, :, :], 0.0).then_inc(s_acc0, 1)
            pool.wait_ge(s_acc0, 1)

            def expert(e, p):
                pool.wait_ge(s_di, e + 1)
                if e == 0:
                    pool.wait_ge(s_out, 64)
                else:
                    pool.wait_ge(s_ys, 16 * NT * e)
                for n in range(NT):
                    r = tile_rows(n)
                    p_.indirect_dma_start(acc[0:r, p, n, :], None, out,
                                          bass.IndirectOffsetOnAxis(ap=dsti[0:r, p, n:n + 1], axis=0),
                                          bounds_check=B * T - 1, oob_is_err=False).then_inc(s_acc, 16)
                for n in range(NT):
                    r = tile_rows(n)
                    pool.wait_ge(s_ye, e * NT + n + 1)
                    p_.indirect_dma_start(out, bass.IndirectOffsetOnAxis(ap=dsti[0:r, p, n:n + 1], axis=0),
                                          ye[0:r, p, n, :], None, bounds_check=B * T - 1,
                                          oob_is_err=False).then_inc(s_ys, 16)

            for e in range(E):
                expert(e, e % 2)


_INS = ["x", "L0_tok_ln1_g", "L0_tok_ln1_b", "L0_tok_W_lin", "L0_tok_b_lin", "L0_tok_ln2_g", "L0_tok_ln2_b",
        "L0_tok_pos_embedding", "L0_tok_cls_token", "L0_attn_Wq", "L0_attn_Wk", "L0_attn_Wv", "L0_attn_Wrk",
        "L0_attn_r_w_bias", "L0_attn_r_r_bias", "L0_attn_Wo", "L0_attn_bo", "L0_ffn_Wg", "L0_ffn_W1", "L0_ffn_b1",
        "L0_ffn_W2", "L0_ffn_b2"]


def constants():
    f = np.float32
    r = np.arange(G)
    block = (r[:, None] // T == r[None, :] // T).astype(f)
    ind = (r[:, None] // T == np.arange(IPG)[None, :]).astype(f)
    positions = np.arange(-T + 1, T).astype(f)
    nb = F // 2
    widths = np.exp(np.log(T + 1) / nb).astype(f) ** np.arange(1, nb + 1).astype(f) - f(1)
    emb = (widths[None, :] > np.abs(positions)[:, None]).astype(f)
    pos = np.concatenate([emb, np.sign(positions)[:, None] * emb], axis=-1)
    iota = np.stack([np.arange(E), np.arange(E) + E]).astype(f)
    tok = (np.arange(NG)[None, :] * G + r[:, None]).astype(f)
    blank = np.zeros((128, XW), f)
    blank[:, XW - 1] = BIG
    return {
        "c_ident": np.eye(128, dtype=f), "c_block": block, "c_ind": ind, "c_pos": np.ascontiguousarray(pos.T),
        "c_iota": np.ascontiguousarray(np.broadcast_to(iota, (128, 2, E))),
        "c_upper": (r[None, :] > r[:, None]).astype(f), "c_real": (tok < B * T).astype(f), "c_tok": tok,
        "c_blank": blank,
    }


def kernel(**inputs):
    import concourse.bacc as bacc
    from concourse.bass_utils import run_bass_kernel_spmd

    nc = bacc.Bacc("TRN2", target_bir_lowering=False, num_devices=1)
    arrays, args = {}, []
    feed = [(n, np.ascontiguousarray(inputs[n])) for n in _INS] + list(constants().items())
    for name, a in feed:
        if name in ("L0_attn_r_w_bias", "L0_attn_r_r_bias"):
            a = np.ascontiguousarray(a.reshape(HB, 128).T)
        elif name == "L0_attn_Wo":
            a = np.ascontiguousarray(a.reshape(H, V, D)[[head_at(j) for j in range(H)]].reshape(H * V, D))
        elif name in ("L0_tok_ln1_g", "L0_tok_ln1_b"):
            a = np.ascontiguousarray(a.reshape(PC, 128).T)
        elif name == "x":
            a = a.reshape(B, C, NH, PATCH, NH, PATCH).transpose(2, 0, 4, 3, 5, 1)
            a = np.ascontiguousarray(a.reshape(NH, B, NH * PD))
        elif name == "L0_ffn_b1":
            a = np.ascontiguousarray(a.reshape(E, HC, 128).transpose(0, 2, 1))
        arrays[name] = a
        args.append(nc.dram_tensor(name, a.shape, mybir.dt.from_np(a.dtype), kind="ExternalInput").ap())
    args.append(nc.dram_tensor("out", (B * T, D), F32, kind="ExternalOutput").ap())
    build(nc, *args)
    r = run_bass_kernel_spmd(nc, [arrays], core_ids=[0])
    return r.results[0]["out"].reshape(B, T, D)
```
